# Optimizing a Trainium2 kernel written in Bass

```python
import numpy as np
import jax
import jax.numpy as jnp

def _softmax(x, axis=-1):
    return jax.nn.softmax(x, axis=axis)

def _gelu(x):
    return jax.nn.gelu(x, approximate=True)

def _silu(x):
    return jax.nn.silu(x)

def _sigmoid(x):
    return jax.nn.sigmoid(x)

def _layernorm(x, axis=-1, eps=1e-05):
    m = jnp.mean(x, axis=axis, keepdims=True)
    v = jnp.var(x, axis=axis, keepdims=True)
    return (x - m) / jnp.sqrt(v + eps)

def _scatter_add(tgt, idx, src, axis=0):
    return tgt.at[idx].add(src)

def _segment_sum(src, seg, n):
    return jax.ops.segment_sum(src, seg, n)
kernel_name = 'mk_hybrid_d1_jaxref_r4_97693e'

def setup_inputs(seed: int=0):
    np.random.seed(seed)
    _w = jnp.asarray

    def _L0_attn_a_setup():
        import jax, jax.numpy as jnp
        import numpy as np
        NUM_HEADS = 16
        D_MODEL = 256
        HEAD_DIM = D_MODEL // NUM_HEADS
        EPS = 1e-06

        def _feature_map(x):
            return jax.nn.elu(x) + 1.0
        key = jax.random.key(seed)
        ks = jax.random.split(key, 9)
        B, S, D = (4, 2048, D_MODEL)
        scale = 1.0 / np.sqrt(D)
        inputs_q = jax.random.normal(ks[0], (B, S, D), dtype=jnp.float32)
        Wq = jax.random.normal(ks[1], (D, D), dtype=jnp.float32) * scale
        Wk = jax.random.normal(ks[2], (D, D), dtype=jnp.float32) * scale
        Wv = jax.random.normal(ks[3], (D, D), dtype=jnp.float32) * scale
        Wo = jax.random.normal(ks[4], (D, D), dtype=jnp.float32) * scale
        bq = jnp.zeros((D,), jnp.float32)
        bk = jnp.zeros((D,), jnp.float32)
        bv = jnp.zeros((D,), jnp.float32)
        bo = jnp.zeros((D,), jnp.float32)
        return {'inputs_q': inputs_q, 'Wq': Wq, 'bq': bq, 'Wk': Wk, 'bk': bk, 'Wv': Wv, 'bv': bv, 'Wo': Wo, 'bo': bo}
    _L0_attn_a_in = _L0_attn_a_setup()

    def _L0_attn_b_setup():
        import jax, jax.numpy as jnp
        import numpy as np
        D_MODEL, D_STATE, D_CONV, EXPAND = (256, 16, 4, 2)
        D_INNER = EXPAND * D_MODEL
        BATCH, SEQ = (2, 512)

        def _forward(x, in_proj_w, conv_w, conv_b, dt_w, dt_b, A_log, D, B_w, C_w, out_w):
            xz = x @ in_proj_w.T
            xc, z = jnp.split(xz, 2, axis=-1)
            h = jnp.transpose(xc, (0, 2, 1))
            h = jnp.pad(h, ((0, 0), (0, 0), (D_CONV - 1, 0)))
            h = jax.lax.conv_general_dilated(h, conv_w, (1,), 'VALID', dimension_numbers=('NCH', 'OIH', 'NCH'))
            h = h + conv_b[None, :, None]
            u = jnp.transpose(h, (0, 2, 1))
            dt = jnp.clip(jax.nn.sigmoid(u @ dt_w.T + dt_b), 0.0001, 1.0)
            A = -jnp.exp(A_log)
            Bm = u @ B_w.T
            Cm = u @ C_w.T
            u_t = jnp.transpose(u, (1, 0, 2))
            dt_t = jnp.transpose(dt, (1, 0, 2))
            B_t = jnp.transpose(Bm, (1, 0, 2))
            C_t = jnp.transpose(Cm, (1, 0, 2))

            def step(state, inp):
                ut, dtt, bt, ct = inp
                dA = jnp.exp(jnp.clip(dtt[:, :, None] * A, -5.0, 5.0))
                dB = dtt[:, :, None] * bt[:, None, :] * ut[:, :, None]
                state = dA * state + dB + 1e-06
                y = jnp.sum(state * ct[:, None, :], axis=-1) + D * ut
                return (state, y)
            state0 = jnp.zeros((x.shape[0], D_INNER, D_STATE), x.dtype)
            _, ys = jax.lax.scan(step, state0, (u_t, dt_t, B_t, C_t))
            y = jnp.transpose(ys, (1, 0, 2))
            y = y * jax.nn.silu(z)
            return y @ out_w.T
        key = jax.random.key(seed)
        ks = jax.random.split(key, 10)
        inv = lambda n: 1.0 / np.sqrt(n)
        return {'x': jax.random.normal(ks[0], (BATCH, SEQ, D_MODEL), jnp.float32), 'in_proj_w': jax.random.uniform(ks[1], (2 * D_INNER, D_MODEL), jnp.float32, -inv(D_MODEL), inv(D_MODEL)), 'conv_w': jax.random.uniform(ks[2], (D_INNER, D_INNER, D_CONV), jnp.float32, -inv(D_INNER * D_CONV), inv(D_INNER * D_CONV)), 'conv_b': jax.random.uniform(ks[3], (D_INNER,), jnp.float32, -inv(D_INNER * D_CONV), inv(D_INNER * D_CONV)), 'dt_w': jax.random.uniform(ks[4], (D_INNER, D_INNER), jnp.float32, -inv(D_INNER), inv(D_INNER)), 'dt_b': jax.random.uniform(ks[5], (D_INNER,), jnp.float32, -inv(D_INNER), inv(D_INNER)), 'A_log': jax.random.normal(ks[6], (D_INNER, D_STATE), jnp.float32) * 0.01, 'D': jnp.ones((D_INNER,), jnp.float32), 'B_w': jax.random.uniform(ks[7], (D_STATE, D_INNER), jnp.float32, -inv(D_INNER), inv(D_INNER)), 'C_w': jax.random.uniform(ks[8], (D_STATE, D_INNER), jnp.float32, -inv(D_INNER), inv(D_INNER)), 'out_w': jax.random.uniform(ks[9], (D_MODEL, D_INNER), jnp.float32, -inv(D_INNER), inv(D_INNER))}
    _L0_attn_b_in = _L0_attn_b_setup()

    def _L0_ffn_setup():
        import jax, jax.numpy as jnp
        import numpy as np
        B, S, D, H, E = (4, 512, 256, 512, 8)
        key = jax.random.key(seed)
        ks = jax.random.split(key, 8)
        scale = 0.02
        return {'x': jax.random.normal(ks[0], (B, S, D), dtype=jnp.float32), 'Wr': jax.random.normal(ks[1], (D, E), dtype=jnp.float32) * scale, 'br': jnp.zeros((E,), dtype=jnp.float32), 'W1': jax.random.normal(ks[2], (E, D, H), dtype=jnp.float32) * scale, 'b1': jnp.zeros((E, H), dtype=jnp.float32), 'W2': jax.random.normal(ks[3], (E, H, D), dtype=jnp.float32) * scale, 'b2': jnp.zeros((E, D), dtype=jnp.float32)}
    _L0_ffn_in = _L0_ffn_setup()
    _d = {'L0_attn_a_inputs_q': _L0_attn_a_in['inputs_q'], 'L0_attn_a_Wq': _L0_attn_a_in['Wq'], 'L0_attn_a_bq': _L0_attn_a_in['bq'], 'L0_attn_a_Wk': _L0_attn_a_in['Wk'], 'L0_attn_a_bk': _L0_attn_a_in['bk'], 'L0_attn_a_Wv': _L0_attn_a_in['Wv'], 'L0_attn_a_bv': _L0_attn_a_in['bv'], 'L0_attn_a_Wo': _L0_attn_a_in['Wo'], 'L0_attn_a_bo': _L0_attn_a_in['bo'], 'L0_attn_b_in_proj_w': _L0_attn_b_in['in_proj_w'], 'L0_attn_b_conv_w': _L0_attn_b_in['conv_w'], 'L0_attn_b_conv_b': _L0_attn_b_in['conv_b'], 'L0_attn_b_dt_w': _L0_attn_b_in['dt_w'], 'L0_attn_b_dt_b': _L0_attn_b_in['dt_b'], 'L0_attn_b_A_log': _L0_attn_b_in['A_log'], 'L0_attn_b_D': _L0_attn_b_in['D'], 'L0_attn_b_B_w': _L0_attn_b_in['B_w'], 'L0_attn_b_C_w': _L0_attn_b_in['C_w'], 'L0_attn_b_out_w': _L0_attn_b_in['out_w'], 'L0_ffn_Wr': _L0_ffn_in['Wr'], 'L0_ffn_br': _L0_ffn_in['br'], 'L0_ffn_W1': _L0_ffn_in['W1'], 'L0_ffn_b1': _L0_ffn_in['b1'], 'L0_ffn_W2': _L0_ffn_in['W2'], 'L0_ffn_b2': _L0_ffn_in['b2']}
    _x0 = _d['L0_attn_a_inputs_q']
    _d['L0_attn_a_inputs_q'] = jax.random.normal(jax.random.fold_in(jax.random.key(seed), 1), (8, 512, 256), dtype=_x0.dtype)
    del _x0
    return _d

def reference(L0_attn_a_inputs_q, L0_attn_a_Wq, L0_attn_a_bq, L0_attn_a_Wk, L0_attn_a_bk, L0_attn_a_Wv, L0_attn_a_bv, L0_attn_a_Wo, L0_attn_a_bo, L0_attn_b_in_proj_w, L0_attn_b_conv_w, L0_attn_b_conv_b, L0_attn_b_dt_w, L0_attn_b_dt_b, L0_attn_b_A_log, L0_attn_b_D, L0_attn_b_B_w, L0_attn_b_C_w, L0_attn_b_out_w, L0_ffn_Wr, L0_ffn_br, L0_ffn_W1, L0_ffn_b1, L0_ffn_W2, L0_ffn_b2):

    def _L0_attn_a_ref(inputs_q, Wq, bq, Wk, bk, Wv, bv, Wo, bo):
        import jax, jax.numpy as jnp
        import numpy as np
        NUM_HEADS = 16
        D_MODEL = 256
        HEAD_DIM = D_MODEL // NUM_HEADS
        EPS = 1e-06

        def _feature_map(x):
            return jax.nn.elu(x) + 1.0
        B, S, D = inputs_q.shape
        H, Dh = (NUM_HEADS, HEAD_DIM)
        q = (inputs_q @ Wq + bq).reshape(B, S, H, Dh)
        k = (inputs_q @ Wk + bk).reshape(B, S, H, Dh)
        v = (inputs_q @ Wv + bv).reshape(B, S, H, Dh)
        q = _feature_map(q)
        k = _feature_map(k)
        kv = jnp.einsum('bkhd,bkhm->bhdm', k, v)
        out = jnp.einsum('bqhd,bhdm->bqhm', q, kv)
        normalizer = jnp.einsum('bqhd,bkhd->bqh', q, k)
        normalizer = jnp.maximum(normalizer, EPS)
        out = out / normalizer[..., None]
        out = out.reshape(B, S, D)
        return out @ Wo + bo

    def _L0_attn_b_ref(x, in_proj_w, conv_w, conv_b, dt_w, dt_b, A_log, D, B_w, C_w, out_w):
        import jax, jax.numpy as jnp
        import numpy as np
        D_MODEL, D_STATE, D_CONV, EXPAND = (256, 16, 4, 2)
        D_INNER = EXPAND * D_MODEL
        BATCH, SEQ = (2, 512)

        def _forward(x, in_proj_w, conv_w, conv_b, dt_w, dt_b, A_log, D, B_w, C_w, out_w):
            xz = x @ in_proj_w.T
            xc, z = jnp.split(xz, 2, axis=-1)
            h = jnp.transpose(xc, (0, 2, 1))
            h = jnp.pad(h, ((0, 0), (0, 0), (D_CONV - 1, 0)))
            h = jax.lax.conv_general_dilated(h, conv_w, (1,), 'VALID', dimension_numbers=('NCH', 'OIH', 'NCH'))
            h = h + conv_b[None, :, None]
            u = jnp.transpose(h, (0, 2, 1))
            dt = jnp.clip(jax.nn.sigmoid(u @ dt_w.T + dt_b), 0.0001, 1.0)
            A = -jnp.exp(A_log)
            Bm = u @ B_w.T
            Cm = u @ C_w.T
            u_t = jnp.transpose(u, (1, 0, 2))
            dt_t = jnp.transpose(dt, (1, 0, 2))
            B_t = jnp.transpose(Bm, (1, 0, 2))
            C_t = jnp.transpose(Cm, (1, 0, 2))

            def step(state, inp):
                ut, dtt, bt, ct = inp
                dA = jnp.exp(jnp.clip(dtt[:, :, None] * A, -5.0, 5.0))
                dB = dtt[:, :, None] * bt[:, None, :] * ut[:, :, None]
                state = dA * state + dB + 1e-06
                y = jnp.sum(state * ct[:, None, :], axis=-1) + D * ut
                return (state, y)
            state0 = jnp.zeros((x.shape[0], D_INNER, D_STATE), x.dtype)
            _, ys = jax.lax.scan(step, state0, (u_t, dt_t, B_t, C_t))
            y = jnp.transpose(ys, (1, 0, 2))
            y = y * jax.nn.silu(z)
            return y @ out_w.T
        return _forward(x, in_proj_w, conv_w, conv_b, dt_w, dt_b, A_log, D, B_w, C_w, out_w)

    def _L0_ffn_ref(x, Wr, br, W1, b1, W2, b2):
        import jax, jax.numpy as jnp
        import numpy as np
        B, S, D, H, E = (4, 512, 256, 512, 8)
        d = x.shape[-1]
        tokens = x.reshape(-1, d)
        logits = tokens @ Wr + br
        probs = jax.nn.softmax(logits, axis=-1)
        expert = jnp.argmax(probs, axis=-1)
        max_prob = jnp.take_along_axis(probs, expert[:, None], axis=-1)
        h = jax.nn.relu(jnp.einsum('td,edh->teh', tokens, W1) + b1[None])
        y = jnp.einsum('teh,ehd->ted', h, W2) + b2[None]
        out = jnp.take_along_axis(y, expert[:, None, None], axis=1)[:, 0, :]
        return (out * max_prob).reshape(x.shape)
    x = L0_attn_a_inputs_q
    x = x + _L0_attn_a_ref(_layernorm(x, axis=-1), L0_attn_a_Wq, L0_attn_a_bq, L0_attn_a_Wk, L0_attn_a_bk, L0_attn_a_Wv, L0_attn_a_bv, L0_attn_a_Wo, L0_attn_a_bo)
    x = x + _L0_ffn_ref(_layernorm(x, axis=-1), L0_ffn_Wr, L0_ffn_br, L0_ffn_W1, L0_ffn_b1, L0_ffn_W2, L0_ffn_b2)
    x = x + _L0_attn_b_ref(_layernorm(x, axis=-1), L0_attn_b_in_proj_w, L0_attn_b_conv_w, L0_attn_b_conv_b, L0_attn_b_dt_w, L0_attn_b_dt_b, L0_attn_b_A_log, L0_attn_b_D, L0_attn_b_B_w, L0_attn_b_C_w, L0_attn_b_out_w)
    x = x + _L0_ffn_ref(_layernorm(x, axis=-1), L0_ffn_Wr, L0_ffn_br, L0_ffn_W1, L0_ffn_b1, L0_ffn_W2, L0_ffn_b2)
    return x

_drawn_inputs = setup_inputs


def setup_inputs(seed=0):
    import zlib

    import numpy as np

    out = dict(_drawn_inputs(seed))
    spreads = {'L0_attn_a_bq': (0.0, 0.8),
     'L0_attn_a_bk': (0.0, 0.8),
     'L0_attn_a_bv': (0.0, 0.1),
     'L0_attn_a_bo': (0.0, 0.1),
     'L0_attn_b_D': (1.0, 0.6),
     'L0_ffn_br': (0.0, 0.1),
     'L0_ffn_b1': (0.0, 0.641),
     'L0_ffn_b2': (0.0, 0.1)}
    factors = {'L0_attn_a_Wq': 6.376,
     'L0_attn_a_Wk': 3.379,
     'L0_attn_b_conv_b': 8.0,
     'L0_attn_b_dt_w': 8.0,
     'L0_attn_b_dt_b': 8.0,
     'L0_attn_b_A_log': 8.0,
     'L0_attn_b_B_w': 8.0,
     'L0_attn_b_C_w': 7.845}
    for name, (base, spread) in spreads.items():
        noise = np.random.default_rng([zlib.crc32(name.encode()), seed]).standard_normal(out[name].shape)
        drawn = base * np.exp(spread * noise) if base else spread * noise
        out[name] = jnp.asarray(drawn.astype(out[name].dtype))
    for name, factor in factors.items():
        out[name] = (out[name] * factor).astype(out[name].dtype)
    return out
```

```python
from contextlib import ExitStack

import concourse.bass as bass
from concourse import mybir

P = 128
BATCH, SEQ, D = 8, 512, 256
TOK = BATCH * SEQ
NCH = TOK // P
CPB = SEQ // P
KD = D // P
HEAD = 16
E, HID = 8, 512
KH = HID // P
DI, NS, TAPS = 512, 16, 4
KI = DI // P
TILES = NCH + E - 1
PAD = TAPS - 1
LN_EPS, NORM_EPS = 1e-5, 1e-6

F32 = mybir.dt.float32
F32R = mybir.dt.float32r
I32 = mybir.dt.int32
U32 = mybir.dt.uint32
ALU = mybir.AluOpType
ACT = mybir.ActivationFunctionType
AX = mybir.AxisListType
ds = bass.DynSlice

C_ID, C_TRI, C_ONE, C_BLK = 0, P, 2 * P, 3 * P
C_RST = 4 * P
C_THR = C_RST + E * NCH
C_DESC = C_THR + NCH
C_IOTA = C_DESC + E
C_STK = C_IOTA + 40
C_ALL = C_STK + 32


def build(nc, T):
    with ExitStack() as ctx:
        sems = {}

        def S(name):
            if name not in sems:
                sems[name] = ctx.enter_context(nc.semaphore(name))
            return sems[name]

        def sb(name, shape, dt=F32):
            return ctx.enter_context(nc.sbuf_tensor(name, shape, dt))

        x = sb("x", [P, NCH, D])
        cst = sb("cst", [P, C_ALL])
        stats = sb("stats", [P, NCH, 6])
        mean, rstd = sb("mean", [P, NCH]), sb("rstd", [P, NCH])
        nw = [sb(f"nw{i}", [P, NCH]) for i in range(4)]
        ident = cst[:, C_ID:C_ID + P]
        tri, ones = cst[:, C_TRI:C_TRI + P], cst[:, C_ONE:C_ONE + P]
        blk = cst[:, C_BLK:C_BLK + P]
        tapw = sb("tapw", [P, TAPS, KD, DI])
        zw = sb("zw", [P, KD, DI])
        dtw = sb("dtw", [P, KI, DI])
        bcw = sb("bcw", [P, KI, 2 * NS])
        outw = sb("outw", [P, KI, D])
        a_neg = sb("a_neg", [P, KI, NS])
        mvec = sb("mvec", [P, 3, KI])
        stack = sb("stack", [2 * 2 * NS, 2 * NS], F32R)
        wr = sb("wr", [P, KD, E])
        br = sb("br", [P, E])
        b1t = sb("b1t", [P, E, KH])
        pmax = sb("pmax", [P, NCH])
        pos = sb("pos", [P, NCH], U32)
        tile_e = sb("tile_e", [P, 40], I32)
        AR = 34100
        arena = sb("arena", [P, AR])

        class Space:

            def __init__(self, at):
                self.at = at

            def take(self, n):
                v = arena[:, self.at:self.at + n]
                self.at += n
                assert self.at <= AR, self.at
                return v

        fs = Space(0)
        w1 = fs.take(E * KD * HID).rearrange("p (e k h) -> p e k h", e=E, k=KD)
        w2 = fs.take(E * KH * D).rearrange("p (e k d) -> p e k d", e=E, k=KH)
        b2 = fs.take(E * D).rearrange("p (e d) -> p e d", e=E)
        FEED = fs.at

        s = Space(FEED)
        wqkv = s.take(KD * 3 * D).rearrange("p (k n) -> p k n", k=KD)
        wo = s.take(KD * D).rearrange("p (k n) -> p k n", k=KD)
        bkv = s.take(2 * D)
        bo = s.take(D)
        bq = s.take(KD)
        a_xn = s.take(CPB * D).rearrange("p (c d) -> p c d", c=CPB)
        a_xt = s.take(KD * SEQ).rearrange("p (k t) -> p k t", k=KD)
        a_eq = s.take(KD * SEQ).rearrange("p (k t) -> p k t", k=KD)
        a_rq = s.take(KD * SEQ).rearrange("p (k t) -> p k t", k=KD)
        a_qf = s.take(KD * SEQ).rearrange("p (k t) -> p k t", k=KD)
        a_k = s.take(CPB * D).rearrange("p (c d) -> p c d", c=CPB)
        a_ek = s.take(CPB * D).rearrange("p (c d) -> p c d", c=CPB)
        a_v = s.take(CPB * KD * (P + 1)).rearrange("p (c k n) -> p c k n", c=CPB, k=KD)
        a_kv = s.take(KD * P).rearrange("p (k n) -> p k n", k=KD)
        a_z = s.take(KD * P).rearrange("p (k n) -> p k n", k=KD)
        a_nr = s.take(KD * SEQ).rearrange("p (k t) -> p k t", k=KD)
        a_o = s.take(KD * SEQ).rearrange("p (k t) -> p k t", k=KD)
        a_y = s.take(CPB * D).rearrange("p (c d) -> p c d", c=CPB)

        s = Space(FEED)
        f_xn = s.take(NCH * D).rearrange("p (c d) -> p c d", c=NCH)
        f_gather = f_xn
        tail = s.at
        f_xt = [s.take(KD * SEQ).rearrange("p (k t) -> p k t", k=KD) for _ in range(2)]
        r_lg, r_eq, r_ex, r_oh, r_pm, r_tot, r_cum, r_cmp = [s.take(NCH * E) for _ in range(8)]
        r_mx, r_se, r_m2, r_pf = [s.take(NCH) for _ in range(4)]
        r_tl, r_te, r_ba = [s.take(E) for _ in range(3)]
        assert s.at <= AR - KI * (DI + D)
        s = Space(tail)
        r_cmp2, r_te40 = s.take(40 * E), s.take(40)
        s = Space(tail)
        t_x = [s.take(D) for _ in range(2)]
        t_xt = [s.take(KD * P).rearrange("p (k t) -> p k t", k=KD) for _ in range(2)]
        t_h = [s.take(HID) for _ in range(2)]
        t_ht = [s.take(HID).rearrange("p (k t) -> p k t", k=KH) for _ in range(2)]
        t_y = [s.take(D) for _ in range(2)]
        s = Space(AR - KI * (DI + D))
        cw = s.take(KI * DI).rearrange("p (k n) -> p k n", k=KI)
        ipw = s.take(KI * D).rearrange("p (k n) -> p k n", k=KI)

        s = Space(0)
        m_u, m_dt, m_sz = [[s.take(KI * SEQ).rearrange("p (k t) -> p k t", k=KI) for _ in range(2)]
                           for _ in range(3)]
        m_w = s.take(KI * SEQ).rearrange("p (k t) -> p k t", k=KI)
        m_xn = s.take(CPB * D).rearrange("p (c d) -> p c d", c=CPB)
        m_xt = s.take(KD * (SEQ + PAD)).rearrange("p (k t) -> p k t", k=KD)
        m_a = [s.take(KI * SEQ).rearrange("p (k t) -> p k t", k=KI) for _ in range(2)]
        m_b = [s.take(KI * SEQ).rearrange("p (k t) -> p k t", k=KI) for _ in range(4)]
        m_q = s.take(KI * SEQ).rearrange("p (k t) -> p k t", k=KI)
        m_y = s.take(KI * SEQ).rearrange("p (k t) -> p k t", k=KI)
        m_bc = [sb(f"m_bc{i}", [4 * NS, SEQ], F32R) for i in range(2)]

        ps = [ctx.enter_context(nc.psum_tensor(f"ps{i}", [P, 512], F32)) for i in range(8)]

        xs = nc.dram_tensor("sorted_rows", (TILES * P, D), F32, kind="Internal").ap()
        ys = [nc.dram_tensor(f"sorted_results{r}", (TILES * P, D), F32, kind="Internal").ap() for r in range(2)]

        block = ctx.enter_context(nc.Block())

        def row(c):
            return ds(c, 1) if not isinstance(c, int) else slice(c, c + 1)

        def load_ffn(eng, r):
            for e in range(E):
                eng.dma_start(w1[:, e], T["W1"][e].rearrange("(k p) h -> p k h", p=P)).then_inc(S(f"ld_ffn{r}"), 16)
                eng.dma_start(w2[:, e], T["W2"][e].rearrange("(k p) d -> p k d", p=P)).then_inc(S(f"ld_ffn{r}"), 16)
            eng.dma_start(b2, T["b2"].partition_broadcast(P)).then_inc(S(f"ld_ffn{r}"), 16)

        LD_FFN = 16 * (2 * E + 1)

        @block.sync
        def _(sp):
            xin = T["x"].rearrange("b (c p) d -> p b c d", p=P)
            sp.dma_start(cst[:, :], T["cst"]).then_inc(S("ld_cst"), 16)
            for b in range(BATCH):
                sp.dma_start(x[:, b * CPB:(b + 1) * CPB, :], xin[:, b]).then_inc(S("ld_x"), 16)
            load_ffn(sp, 0)
            sp.wait_ge(S("a_xupd"), BATCH)
            sp.dma_start(ipw, T["ip_x"].rearrange("(k p) d -> p k d", p=P)).then_inc(S("ld_ipw"), 16)
            for k in range(TAPS):
                if k:
                    sp.wait_ge(S("tap_mm"), KD * k)
                sp.dma_start(cw, T["conv"][k].rearrange("(k p) d -> p k d", p=P)).then_inc(S(f"ld_cw{k}"), 16)

            def tiles_loop(r):
                def at(j):
                    return xs[j * P:(j + 1) * P] if isinstance(j, int) else xs[ds(j * P, P)]

                def to(j):
                    return ys[r][j * P:(j + 1) * P] if isinstance(j, int) else ys[r][ds(j * P, P)]

                def load(j, par):
                    sp.dma_start(t_x[par], at(j)).then_inc(S(f"f{r}_x{par}"), 16)

                def store(j, par, n):
                    sp.wait_ge(S(f"f{r}_y{par}"), n)
                    sp.dma_start(to(j), t_y[par]).then_inc(S(f"f{r}_st{par}"), 16)

                H = TILES // 2
                sp.wait_ge(S(f"f{r}_scat"), 16 * NCH)
                load(0, 0)
                load(1, 1)

                def turn(i, more):
                    sp.wait_ge(S(f"f{r}_tr0"), i + 1)
                    load(2 * i + 2, 0)
                    if more:
                        sp.wait_ge(S(f"f{r}_tr1"), i + 1)
                        load(2 * i + 3, 1)
                    store(2 * i, 0, i + 1)
                    store(2 * i + 1, 1, i + 1)

                turn(0, True)
                with sp.Fori(1, H - 1) as i:
                    turn(i, True)
                turn(H - 1, False)
                store(TILES - 1, 0, H + 1)

            tiles_loop(0)
            sp.wait_ge(S("m_xupd"), 2 * BATCH)
            load_ffn(sp, 1)
            tiles_loop(1)
            out = T["out"].rearrange("b (c p) d -> p b c d", p=P)
            for b in range(BATCH):
                sp.wait_ge(S("f1_xupd"), b + 1)
                sp.dma_start(out[:, b], x[:, b * CPB:(b + 1) * CPB, :]).then_inc(S("out_done"), 16)
            sp.wait_ge(S("out_done"), 16 * BATCH)

        @block.gpsimd
        def _(g):
            g.memset(a_y, 0.0).then_inc(S("zero"), 1)
            g.wait_ge(S("zero"), 1)
            z = a_y.rearrange("p c d -> p (c d)")[:, 0:D]
            g.dma_start(xs.rearrange("(n p) d -> p n d", p=P), z.unsqueeze(1).to_broadcast([P, TILES, D]))\
                .then_inc(S("xs_zeroed"), 16)
            g.memset(a_v[:, :, :, P:P + 1], 1.0).then_inc(S("a_vone"), 1)

            def scatter(r):
                g.wait_ge(S(f"f{r}_pos"), 1)
                if r == 0:
                    g.wait_ge(S("xs_zeroed"), 16)
                for c in range(NCH):
                    g.indirect_dma_start(out=xs, out_offset=bass.IndirectOffsetOnAxis(ap=pos[:, c:c + 1], axis=0),
                                         in_=f_xn[:, c, :], in_offset=None).then_inc(S(f"f{r}_scat"), 16)

            def gather(r):
                g.wait_ge(S(f"f{r}_st0"), 16 * (TILES - TILES // 2))
                g.wait_ge(S(f"f{r}_st1"), 16 * (TILES // 2))
                for c in range(NCH):
                    g.indirect_dma_start(out=f_gather[:, c, :], out_offset=None, in_=ys[r],
                                         in_offset=bass.IndirectOffsetOnAxis(ap=pos[:, c:c + 1], axis=0))\
                        .then_inc(S(f"f{r}_g{c // CPB}"), 16)

            scatter(0)
            gather(0)
            g.wait_ge(S("f0_xupd"), BATCH)
            for a in m_a:
                g.memset(a[:, :, 0:1], 0.0).then_inc(S("m_zero"), 1)
            g.memset(m_xt[:, :, 0:PAD], 0.0).then_inc(S("m_zero"), 1)

            def pairs(b):
                for p in range(NS // 2):
                    n = 2 * p
                    g.wait_ge(S("m_c"), NS * b + n + 2)
                    g.wait_ge(S("m_nsum"), (NS // 2) * b + p)
                    g.tensor_tensor(m_q, m_b[n % 4], m_b[(n + 1) % 4], ALU.add).then_inc(S("m_q"), 1)

            pairs(0)
            with g.Fori(1, BATCH) as b:
                pairs(b)
            scatter(1)
            gather(1)

        @block.scalar
        def _(a):
            a.dma_start(wqkv[:, :, 0:D], T["Wq"].rearrange("(k p) n -> p k n", p=P)).then_inc(S("ld_a"), 16)
            a.dma_start(wqkv[:, :, D:2 * D], T["Wk"].rearrange("(k p) n -> p k n", p=P)).then_inc(S("ld_a"), 16)
            a.dma_start(wqkv[:, :, 2 * D:3 * D], T["Wv"].rearrange("(k p) n -> p k n", p=P)).then_inc(S("ld_a"), 16)
            a.dma_start(wo, T["Wo"].rearrange("(k p) n -> p k n", p=P)).then_inc(S("ld_a"), 16)
            a.dma_start(bkv, T["bkv"].partition_broadcast(P)).then_inc(S("ld_a"), 16)
            a.dma_start(bo, T["bo"].partition_broadcast(P)).then_inc(S("ld_a"), 16)
            a.dma_start(bq, T["bq"]).then_inc(S("ld_a"), 16)
            a.dma_start(wr[:, :, :], T["Wr"].rearrange("(k p) e -> p k e", p=P)).then_inc(S("ld_r"), 16)
            a.dma_start(br[:, :], T["br"].partition_broadcast(P)).then_inc(S("ld_r"), 16)
            a.dma_start(b1t[:, :, :], T["b1"]).then_inc(S("ld_r"), 16)
            for dst, name in ((zw, "zw"), (dtw, "dtw"), (bcw, "bcw"), (outw, "outw")):
                a.dma_start(dst[:, :, :], T[name].rearrange("(k p) n -> p k n", p=P)).then_inc(S("ld_m"), 16)
            a.dma_start(a_neg[:, :, :], T["A_log"]).then_inc(S("ld_m"), 16)
            a.dma_start(mvec[:, :, :], T["mvec"]).then_inc(S("ld_m"), 16)

            def xt_copy(b):
                a.wait_ge(S("a_tr"), b + 1)
                a.wait_ge(S("a_kvp"), CPB * b)
                for k in range(KD):
                    last = a.activation(a_xt[:, k, :], ps[k][:, :], ACT.Copy)
                last.then_inc(S("a_xt"), 1)

            def attention(b, more):
                a.wait_ge(S("a_q"), b + 1)
                a.wait_ge(S("a_qf"), b)
                for k in range(KD):
                    last = a.activation(a_eq[:, k, :], ps[2 + k][:, :], ACT.Exp, bias=bq[:, k:k + 1])
                last.then_inc(S("a_eq"), 1)
                a.wait_ge(S("a_kb"), CPB * b + CPB)
                a.wait_ge(S("a_kf"), b)
                a.activation(a_ek, a_k, ACT.Exp).then_inc(S("a_ek"), 1)
                if more:
                    xt_copy(b + 1)

            a.wait_ge(S("ld_a"), 16 * 7)
            xt_copy(0)
            attention(0, True)
            with a.Fori(1, BATCH - 1) as b:
                attention(b, True)
            attention(BATCH - 1, False)

            def feed(r):
                for b in range(BATCH):
                    a.wait_ge(S(f"f{r}_tr"), b + 1)
                    if b >= 2:
                        a.wait_ge(S(f"f{r}_lgmm"), b - 1)
                    for k in range(KD):
                        last = a.activation(f_xt[b % 2][:, k, :], ps[2 * (b % 2) + k][:, :], ACT.Copy)
                    last.then_inc(S(f"f{r}_xt"), 1)
                a.wait_ge(S(f"f{r}_lg"), 1)
                a.activation(r_ex, r_lg, ACT.Exp).then_inc(S(f"f{r}_ex"), 1)
                if r == 0:
                    for k in range(TAPS):
                        for d in range(KD):
                            n = KD * k + d
                            a.wait_ge(S("tap_mm"), n + 1)
                            a.activation(tapw[:, k, d, :], ps[n % 2][:, :], ACT.Copy).then_inc(S("tapw"), 1)
                    a.wait_ge(S("ld_m"), 16 * 6)
                    a.activation(a_neg[:, :, :], a_neg[:, :, :], ACT.Exp).then_inc(S("m_aexp"), 1)
                    a.wait_ge(S("m_aexp"), 1)
                    a.activation(a_neg[:, :, :], a_neg[:, :, :], ACT.Copy, scale=-1.0).then_inc(S("m_aexp"), 1)
                    a.activation(mvec[:, 1, :], mvec[:, 1, :], ACT.Copy, scale=0.5).then_inc(S("m_aexp"), 1)

                def xt(par, n):
                    a.wait_ge(S(f"f{r}_tr{par}"), n + 1)
                    a.wait_ge(S(f"f{r}_h{par}"), n)
                    a.activation(t_xt[par], ps[par][:, 0:KD * P].rearrange("p (k t) -> p k t", k=KD), ACT.Copy)\
                        .then_inc(S(f"f{r}_xt{par}"), 1)

                def relu(e, par, n):
                    a.wait_ge(S(f"f{r}_ht{par}"), n + 1)
                    a.wait_ge(S(f"f{r}_ymm{par}"), n)
                    for k in range(KH):
                        last = a.activation(t_ht[par][:, k, :], ps[4 + par][:, k * P:(k + 1) * P], ACT.Relu,
                                            bias=b1t[:, row(e), k:k + 1].rearrange("p a b -> p (a b)"))
                    last.then_inc(S(f"f{r}_relu{par}"), 1)

                def expert(j):
                    return a.value_load(tile_e[0:1, ds(j, 1)] if not isinstance(j, int) else tile_e[0:1, j:j + 1],
                                        min_val=0, max_val=E - 1)

                H = TILES // 2
                a.wait_ge(S(f"f{r}_pos"), 1)
                xt(0, 0)
                xt(1, 0)

                def turn(i, more):
                    relu(expert(2 * i), 0, i)
                    xt(0, i + 1)
                    relu(expert(2 * i + 1), 1, i)
                    if more:
                        xt(1, i + 1)

                turn(0, True)
                with a.Fori(1, H - 1) as i:
                    turn(i, True)
                turn(H - 1, False)
                relu(expert(TILES - 1), 0, H)

            feed(0)

            def m_xtcopy(n):
                a.wait_ge(S("m_tr"), n + 1)
                a.wait_ge(S("m_zmm"), KI * n)
                for k in range(KD):
                    last = a.activation(m_xt[:, k, PAD:], ps[k][:, :], ACT.Copy)
                last.then_inc(S("m_xt"), 1)

            def m_uevac(n, par, o):
                a.wait_ge(S("m_umm"), KI * n + o + 1)
                if not (isinstance(n, int) and n < 2):
                    a.wait_ge(S("m_y"), n - 1)
                a.activation(m_u[par][:, o, :], ps[o % 2][:, :], ACT.Identity, bias=mvec[:, 0, o:o + 1])\
                    .then_inc(S("m_u"), 1)

            def m_thevac(n, par, o):
                a.wait_ge(S("m_dmm"), KI * n + o + 1)
                a.activation(m_dt[par][:, o, :], ps[o % 2][:, :], ACT.Tanh, bias=mvec[:, 1, o:o + 1], scale=0.5)\
                    .then_inc(S("m_th"), 1)

            def m_bchi(n, par):
                a.wait_ge(S("m_bcmm"), n + 1)
                a.activation(m_bc[par][0:2 * NS, :], ps[0][0:2 * NS, :], ACT.Copy).then_inc(S("m_bchi"), 1)

            def m_zevac(n, par, o):
                a.wait_ge(S("m_zmm"), KI * n + o + 1)
                a.activation(m_sz[par][:, o, :], ps[(o + 1) % 2][:, :], ACT.Tanh, scale=0.5).then_inc(S("m_zth"), 1)

            def m_pre(n, par, slot, half):
                if slot == 0 and half == 0:
                    m_xtcopy(n)
                if slot == 0 and half == 1:
                    m_uevac(n, par, 0)
                if slot == 1 and half == 1:
                    m_uevac(n, par, 1)
                if slot == 3 and half == 1:
                    m_uevac(n, par, 2)
                if slot == 4 and half == 1:
                    m_uevac(n, par, 3)
                if slot in (5, 6):
                    m_thevac(n, par, 2 * (slot - 5) + half)
                if slot == 7 and half == 1:
                    m_bchi(n, par)
                    for o in range(KI):
                        m_zevac(n, par, o)

            def m_scan(b, par, more):
                for st in range(NS):
                    n = NS * b + st
                    if st == 0:
                        a.wait_ge(S("m_w"), b + 1)
                    if not (isinstance(b, int) and n < 2):
                        a.wait_ge(S("m_scan"), n - 1)
                    for k in range(KI):
                        last = a.activation(m_a[st % 2][:, k, 1:], m_dt[par][:, k, 1:], ACT.Exp,
                                            scale=a_neg[:, k, st:st + 1])
                    last.then_inc(S("m_exp"), 1)
                    a.wait_ge(S("m_db"), n + 1)
                    a.activation(m_b[st % 4], m_b[st % 4], ACT.Copy, bias=1e-6).then_inc(S("m_eps"), 1)
                    if more:
                        m_pre(b + 1, 1 - par, st // 2, st % 2)

            a.wait_ge(S("m_zero"), 3)
            a.wait_ge(S("f0_xupd"), BATCH)
            a.wait_ge(S("m_aexp"), 3)
            for slot in range(8):
                for half in range(2):
                    m_pre(0, 0, slot, half)
            m_scan(0, 0, True)
            with a.Fori(0, (BATCH - 2) // 2) as i:
                m_scan(2 * i + 1, 1, True)
                m_scan(2 * i + 2, 0, True)
            m_scan(BATCH - 1, 1, False)
            feed(1)

        @block.vector
        def _(v):
            chain = S("v_chain")
            count = [0]

            def link(ins):
                count[0] += 1
                ins.then_inc(chain, 1)
                v.wait_ge(chain, count[0])

            def row_stats(c):
                return v.bn_stats(out=stats[:, row(c), :].rearrange("p a s -> p (a s)"),
                                  in_=x[:, row(c), :].rearrange("p a d -> p (a d)"))

            def layer_norm_scales(r):
                me, m2e, mo, m2o = stats[:, :, 1], stats[:, :, 2], stats[:, :, 4], stats[:, :, 5]
                d, q, var, t = [w[:, :] for w in nw]
                v.tensor_tensor(d, me, mo, ALU.subtract)
                v.tensor_tensor(q, me, mo, ALU.add)
                link(v.tensor_tensor(t, m2e, m2o, ALU.add))
                v.tensor_scalar(mean[:, :], q, 0.5, None, ALU.mult)
                link(v.tensor_scalar(var, t, 1.0 / D, LN_EPS, ALU.mult, ALU.add))
                link(v.tensor_tensor(q, d, d, ALU.mult))
                link(v.scalar_tensor_tensor(out=d, in0=q, scalar=0.25, in1=var, op0=ALU.mult, op1=ALU.add))
                y = rstd[:, :]
                link(v.tensor_scalar(y.bitcast(I32), d.bitcast(I32), -0.5, 1597463007.0, ALU.mult, ALU.add))
                for _ in range(4):
                    link(v.tensor_tensor(q, y, y, ALU.mult))
                    link(v.scalar_tensor_tensor(out=t, in0=q, scalar=-0.5, in1=d, op0=ALU.mult, op1=ALU.mult))
                    link(v.scalar_tensor_tensor(out=y, in0=t, scalar=1.5, in1=y, op0=ALU.add, op1=ALU.mult))

            def ln_apply(out, c):
                return v.tensor_scalar(out, x[:, row(c), :].rearrange("p a d -> p (a d)"), mean[:, row(c)],
                                       rstd[:, row(c)], ALU.subtract, ALU.mult)

            v.wait_ge(S("ld_cst"), 16)
            v.wait_ge(S("ld_x"), 16 * BATCH)
            for c in range(NCH):
                last = row_stats(c)
            link(last)
            layer_norm_scales("a")

            def a_norm(b):
                v.wait_ge(S("a_tr"), b)
                for c in range(CPB):
                    last = ln_apply(a_xn[:, c, :], CPB * b + c)
                last.then_inc(S("a_xn"), 1)

            def a_project(b, more):
                v.wait_ge(S("a_eq"), b + 1)
                for k in range(KD):
                    last = v.tensor_scalar(a_rq[:, k, :], ps[2 + k][:, :], bq[:, k:k + 1], 0.0, ALU.add, ALU.max)
                last.then_inc(S("a_rq"), 1)
                if more:
                    a_norm(b + 1)
                if not (isinstance(b, int) and b == 0):
                    v.wait_ge(S("a_kvmm"), b)
                for c in range(CPB):
                    v.wait_ge(S("a_kvp"), CPB * b + c + 1)
                    v.tensor_tensor(a_v[:, c, :, 0:P], ps[4 + c % 2][:, D:2 * D].rearrange("p (k n) -> p k n", k=KD),
                                    bkv[:, D:2 * D].rearrange("p (k n) -> p k n", k=KD), ALU.add)
                    v.tensor_tensor(a_k[:, c, :], ps[4 + c % 2][:, 0:D], bkv[:, 0:D], ALU.add).then_inc(S("a_kb"), 1)
                v.wait_ge(S("a_ek"), b + 1)
                v.tensor_scalar(a_ek, a_ek, 1.0, None, ALU.min).then_inc(S("a_ekmin"), 1)
                v.wait_ge(S("a_ekmin"), b + 1)
                v.scalar_tensor_tensor(out=a_k, in0=a_k, scalar=0.0, in1=a_ek, op0=ALU.max, op1=ALU.add)\
                    .then_inc(S("a_kf"), 1)

            def a_normalise(b):
                v.wait_ge(S("a_on"), b + 1)
                for k in range(KD):
                    last = v.tensor_scalar(a_nr[:, k, :], ps[4 + k][:, :], NORM_EPS, None, ALU.max)
                last.then_inc(S("a_nmax"), 1)
                v.wait_ge(S("a_nmax"), b + 1)
                v.reciprocal(a_nr, a_nr).then_inc(S("a_nrec"), 1)
                v.wait_ge(S("a_nrec"), b + 1)
                for k in range(KD):
                    last = v.tensor_tensor(a_o[:, k, :], ps[2 + k][:, :], a_nr[:, k, :], ALU.mult)
                last.then_inc(S("a_o"), 1)

            def a_qfeature(b):
                v.wait_ge(S("a_eq"), b + 1)
                v.wait_ge(S("a_on"), b)
                v.scalar_tensor_tensor(out=a_qf, in0=a_eq, scalar=1.0, in1=a_rq, op0=ALU.min, op1=ALU.add)\
                    .then_inc(S("a_qf"), 1)

            def a_mask(b):
                v.wait_ge(S("a_kvmm"), b + 1)
                for k in range(KD):
                    g = ps[0][:, k * (P + 1):(k + 1) * (P + 1)]
                    v.tensor_tensor(a_kv[:, k, :], g[:, 0:P], blk, ALU.mult)
                    last = v.tensor_scalar(a_z[:, k, :], blk, g[:, P:P + 1], None, ALU.mult)
                last.then_inc(S("a_mask"), 1)

            def a_update(b):
                v.wait_ge(S("a_ymm"), b + 1)
                for h in range(2):
                    last = v.tensor_tensor(a_y[:, 2 * h:2 * h + 2, :],
                                           ps[6 + h][:, :].rearrange("p (c d) -> p c d", c=2),
                                           bo.unsqueeze(1).to_broadcast([P, 2, D]), ALU.add)
                last.then_inc(S("a_yb"), 1)
                v.wait_ge(S("a_yb"), b + 1)
                xv = x[:, ds(CPB * b, CPB) if not isinstance(b, int) else slice(CPB * b, CPB * b + CPB), :]
                v.tensor_tensor(xv, xv, a_y, ALU.add).then_inc(S("a_xadd"), 1)
                v.wait_ge(S("a_xadd"), b + 1)
                for c in range(CPB):
                    last = row_stats(CPB * b + c)
                last.then_inc(S("a_xupd"), 1)

            def attention(b, before, more):
                a_project(b, more)
                if before:
                    a_normalise(b - 1)
                a_qfeature(b)
                a_mask(b)
                if before:
                    a_update(b - 1)

            v.wait_ge(S("ld_a"), 16 * 7)
            v.wait_ge(S("a_vone"), 1)
            v.wait_ge(S("xs_zeroed"), 16)
            a_norm(0)
            attention(0, False, True)
            with v.Fori(1, BATCH - 1) as b:
                attention(b, True, True)
            attention(BATCH - 1, True, False)
            a_normalise(BATCH - 1)
            a_update(BATCH - 1)

            def feed(r, updated, n_updated):
                v.wait_ge(S(updated), n_updated)
                layer_norm_scales(f"f{r}")
                for c in range(NCH):
                    last = ln_apply(f_xn[:, c, :], c)
                    if c % CPB == CPB - 1:
                        last.then_inc(S(f"f{r}_xn"), 1)
                ce = "p (c e) -> p c e"
                lg, eq, ex, oh, pm, cmp_ = [q.rearrange(ce, e=E) for q in (r_lg, r_eq, r_ex, r_oh, r_pm, r_cmp)]
                ec = "p (e c) -> p e c"
                tot, cum = r_tot.rearrange(ec, e=E), r_cum.rearrange(ec, e=E)
                v.wait_ge(S("ld_r"), 16 * 3)
                v.wait_ge(S(f"f{r}_lgmm"), BATCH)
                v_log = ps[7][:, 0:NCH * E].rearrange(ce, e=E)
                link(v.tensor_tensor(lg, v_log, br[:, :].unsqueeze(1).to_broadcast([P, NCH, E]), ALU.add))
                link(v.tensor_reduce(r_mx, lg, AX.X, ALU.max))
                top = r_mx.unsqueeze(2).to_broadcast([P, NCH, E])
                link(v.tensor_tensor(eq, lg, top, ALU.is_equal))
                v.tensor_tensor(lg, lg, top, ALU.subtract).then_inc(S(f"f{r}_lg"), 1)
                link(v.tensor_tensor(eq, eq, cst[:, C_DESC:C_DESC + E].unsqueeze(1).to_broadcast([P, NCH, E]), ALU.mult))
                link(v.tensor_reduce(r_m2, eq, AX.X, ALU.max))
                v.tensor_tensor(oh, eq, r_m2.unsqueeze(2).to_broadcast([P, NCH, E]), ALU.is_equal)\
                    .then_inc(S(f"f{r}_oh"), 1)
                v.wait_ge(S(f"f{r}_ex"), 1)
                link(v.tensor_reduce(r_se, ex, AX.X, ALU.add))
                link(v.reciprocal(pmax[:, :], r_se))
                v.wait_ge(S(f"f{r}_rank"), 1)
                link(v.tensor_copy(tot, ps[6][:, 0:NCH * E].rearrange("p (c e) -> p e c", e=E)))
                link(v.tensor_tensor_scan(out=r_cum, data0=cst[:, C_RST:C_RST + E * NCH], data1=r_tot, initial=0.0,
                                          op0=ALU.mult, op1=ALU.add))
                link(v.tensor_tensor(r_cmp.rearrange(ec, e=E), cum[:, :, NCH - 1:NCH].to_broadcast([P, E, NCH]),
                                     cst[:, C_THR:C_THR + NCH].unsqueeze(1).to_broadcast([P, E, NCH]), ALU.is_gt))
                link(v.tensor_reduce(r_tl, r_cmp.rearrange(ec, e=E), AX.X, ALU.add))
                link(v.tensor_tensor_scan(out=r_te, data0=ones[:, 0:E], data1=r_tl, initial=0.0,
                                          op0=ALU.mult, op1=ALU.add))
                v.tensor_tensor(r_ba, r_te, r_tl, ALU.subtract)
                link(v.tensor_tensor(cum, cum, tot, ALU.subtract))
                link(v.tensor_scalar(r_ba, r_ba, float(P), -1.0, ALU.mult, ALU.add))
                link(v.tensor_tensor(cum, cum, r_ba.unsqueeze(2).to_broadcast([P, E, NCH]), ALU.add))
                link(v.tensor_tensor(pm, ps[5][:, 0:NCH * E].rearrange(ce, e=E), r_cum.rearrange("p (e c) -> p c e", e=E),
                                     ALU.add))
                link(v.tensor_tensor(pm, pm, oh, ALU.mult))
                link(v.tensor_reduce(r_pf, pm, AX.X, ALU.add))
                v.tensor_copy(pos[:, :], r_pf)
                c2 = r_cmp2.rearrange("p (j e) -> p j e", e=E)
                link(v.tensor_tensor(c2, cst[:, C_IOTA:C_IOTA + 40].unsqueeze(2).to_broadcast([P, 40, E]),
                                     r_te.unsqueeze(1).to_broadcast([P, 40, E]), ALU.is_ge))
                link(v.tensor_reduce(r_te40, c2, AX.X, ALU.add))
                v.tensor_scalar(tile_e[:, :], r_te40, float(E - 1), None, ALU.min).then_inc(S(f"f{r}_pos"), 1)

                def hid(par, n):
                    v.wait_ge(S(f"f{r}_h{par}"), n + 1)
                    v.wait_ge(S(f"f{r}_ht{par}"), n)
                    v.tensor_copy(t_h[par], ps[2 + par][:, :]).then_inc(S(f"f{r}_hc{par}"), 1)

                def res(j, par, n):
                    e = v.value_load(tile_e[0:1, ds(j, 1)] if not isinstance(j, int) else tile_e[0:1, j:j + 1],
                                     min_val=0, max_val=E - 1)
                    v.wait_ge(S(f"f{r}_ymm{par}"), n + 1)
                    v.wait_ge(S(f"f{r}_st{par}"), 16 * n)
                    v.tensor_tensor(t_y[par], ps[6 + par][:, 0:D], b2[:, row(e), :].rearrange("p a d -> p (a d)"), ALU.add)\
                        .then_inc(S(f"f{r}_y{par}"), 1)

                H = TILES // 2
                v.wait_ge(S(f"ld_ffn{r}"), LD_FFN)
                v.wait_ge(S(f"f{r}_pos"), 1)
                hid(0, 0)

                def turn(i):
                    hid(1, i)
                    res(2 * i, 0, i)
                    hid(0, i + 1)
                    res(2 * i + 1, 1, i)

                turn(0)
                with v.Fori(1, H) as i:
                    turn(i)
                res(TILES - 1, 0, H)
                for b in range(BATCH):
                    v.wait_ge(S(f"f{r}_g{b}"), 16 * CPB)
                    for c in range(CPB * b, CPB * b + CPB):
                        last = v.scalar_tensor_tensor(out=x[:, c, :], in0=f_gather[:, c, :], scalar=pmax[:, c:c + 1],
                                                      in1=x[:, c, :], op0=ALU.mult, op1=ALU.add)
                    if r == 0:
                        link(last)
                        for c in range(CPB * b, CPB * b + CPB):
                            last = row_stats(c)
                    last.then_inc(S(f"f{r}_xupd"), 1)

            feed(0, "a_xupd", BATCH)

            v.wait_ge(S("f0_xupd"), BATCH)
            v.wait_ge(S("m_zero"), 3)
            v.tensor_copy(stack[:, :], cst[0:4 * NS, C_STK:C_STK + 2 * NS]).then_inc(S("m_stack"), 1)
            layer_norm_scales("m")

            def m_norm(n):
                v.wait_ge(S("m_tr"), n)
                for c in range(CPB):
                    last = ln_apply(m_xn[:, c, :], CPB * n + c)
                last.then_inc(S("m_xn"), 1)

            def m_dtw(n, par):
                v.wait_ge(S("m_th"), KI * n + KI)
                v.tensor_scalar(m_dt[par], m_dt[par], 1.0, 0.5, ALU.add, ALU.mult).then_inc(S("m_dt0"), 1)
                v.wait_ge(S("m_dt0"), n + 1)
                v.tensor_scalar(m_dt[par], m_dt[par], 1e-4, 1.0, ALU.max, ALU.min).then_inc(S("m_dt1"), 1)
                v.wait_ge(S("m_dt1"), n + 1)
                v.tensor_tensor(m_w, m_dt[par], m_u[par], ALU.mult).then_inc(S("m_w"), 1)

            def m_bclo(n, par):
                v.wait_ge(S("m_bchi"), n + 1)
                v.tensor_tensor(m_bc[par][2 * NS:4 * NS, :], ps[0][0:2 * NS, :], m_bc[par][0:2 * NS, :].bitcast(F32),
                                ALU.subtract).then_inc(S("m_bclo"), 1)

            def m_gate(n, par, o):
                v.wait_ge(S("m_zth"), KI * n + o + 1)
                v.scalar_tensor_tensor(out=m_sz[par][:, o, :], in0=m_sz[par][:, o, :], scalar=1.0,
                                       in1=ps[(o + 1) % 2][:, :], op0=ALU.add, op1=ALU.mult).then_inc(S("m_sz"), 1)

            def m_final(b, par):
                v.wait_ge(S("m_nsum"), (NS // 2) * (b + 1))
                v.wait_ge(S("m_sz"), KI * (b + 1))
                for k in range(KI):
                    last = v.scalar_tensor_tensor(out=m_y[:, k, :], in0=m_u[par][:, k, :], scalar=mvec[:, 2, k:k + 1],
                                                  in1=ps[4 + k][:, :], op0=ALU.mult, op1=ALU.add)
                last.then_inc(S("m_y0"), 1)
                v.wait_ge(S("m_y0"), b + 1)
                v.scalar_tensor_tensor(out=m_y, in0=m_y, scalar=0.5, in1=m_sz[par], op0=ALU.mult, op1=ALU.mult)\
                    .then_inc(S("m_y"), 1)

            def m_update(b):
                for h in range(2):
                    v.wait_ge(S("m_omm"), 2 * b + h + 1)
                    c = CPB * b + 2 * h
                    xv = x[:, ds(c, 2) if not isinstance(c, int) else slice(c, c + 2), :]
                    v.tensor_tensor(xv, ps[h][:, :].rearrange("p (c d) -> p c d", c=2), xv, ALU.add)\
                        .then_inc(S("m_xupd"), 1)
                v.wait_ge(S("m_xupd"), 2 * b + 2)
                for c in range(CPB):
                    last = row_stats(CPB * b + c)
                last.then_inc(S("m_stat"), 1)

            def m_db(b, par, st):
                n = NS * b + st
                v.wait_ge(S("m_bb"), n + 1)
                if st >= 4:
                    v.wait_ge(S("m_q"), (NS // 2) * b + (st - 4) // 2 + 1)
                elif not (isinstance(b, int) and b == 0):
                    v.wait_ge(S("m_q"), (NS // 2) * b - 2 + st // 2 + 1)
                v.tensor_tensor(m_b[st % 4], m_w, ps[2][:, :].unsqueeze(1).to_broadcast([P, KI, SEQ]), ALU.mult)\
                    .then_inc(S("m_db"), 1)

            def m_scan(b, par, before, more):
                if more:
                    m_norm(b + 1)
                m_db(b, par, 0)
                for st in range(NS):
                    n = NS * b + st
                    v.wait_ge(S("m_exp"), n + 1)
                    v.tensor_scalar(m_a[st % 2][:, :, 1:], m_a[st % 2][:, :, 1:], 0.006737946999085467,
                                    148.4131591025766, ALU.max, ALU.min).then_inc(S("m_clip"), 1)
                    if st + 1 < NS:
                        m_db(b, par, st + 1)
                    v.wait_ge(S("m_clip"), n + 1)
                    v.wait_ge(S("m_eps"), n + 1)
                    bt = m_b[st % 4].rearrange("p k t -> p (k t)")
                    v.tensor_tensor_scan(out=bt, data0=m_a[st % 2].rearrange("p k t -> p (k t)"), data1=bt,
                                         initial=0.0, op0=ALU.mult, op1=ALU.add).then_inc(S("m_scan"), 1)
                    v.wait_ge(S("m_scan"), n + 1)
                    v.wait_ge(S("m_cb"), n + 1)
                    v.tensor_tensor(m_b[st % 4], m_b[st % 4], ps[3][:, :].unsqueeze(1).to_broadcast([P, KI, SEQ]),
                                    ALU.mult).then_inc(S("m_c"), 1)
                    if before and st == 1:
                        m_final(b - 1, 1 - par)
                    if before and st == 5:
                        m_update(b - 1)
                    if more and st == 15:
                        m_dtw(b + 1, 1 - par)
                    if more and st == 15:
                        m_bclo(b + 1, 1 - par)
                        for o in range(KI):
                            m_gate(b + 1, 1 - par, o)

            m_norm(0)
            m_dtw(0, 0)
            m_bclo(0, 0)
            for o in range(KI):
                m_gate(0, 0, o)
            m_scan(0, 0, False, True)
            with v.Fori(0, (BATCH - 2) // 2) as i:
                m_scan(2 * i + 1, 1, True, True)
                m_scan(2 * i + 2, 0, True, True)
            m_scan(BATCH - 1, 1, True, False)
            m_final(BATCH - 1, 1)
            m_update(BATCH - 1)
            feed(1, "m_stat", BATCH)

        @block.tensor
        def _(t):
            def turned(bank, src, k, n):
                return t.transpose(bank, src[:, k * P:(k + 1) * P], ident)

            def a_turn(b):
                t.wait_ge(S("a_xn"), b + 1)
                t.wait_ge(S("a_xt"), b)
                t.wait_ge(S("a_mask"), b)
                for k in range(KD):
                    for c in range(CPB):
                        last = turned(ps[k][:, c * P:(c + 1) * P], a_xn[:, c, :], k, c)
                last.then_inc(S("a_tr"), 1)

            def a_project(b):
                t.wait_ge(S("a_xt"), b + 1)
                if not (isinstance(b, int) and b == 0):
                    t.wait_ge(S("a_qf"), b)
                for m in range(KD):
                    for k in range(KD):
                        last = t.matmul(ps[2 + m][:, :], wqkv[:, k, m * P:(m + 1) * P], a_xt[:, k, :],
                                        start=(k == 0), stop=(k == KD - 1))
                last.then_inc(S("a_q"), 1)
                for c in range(CPB):
                    t.wait_ge(S("a_kb"), CPB * b + max(c - 1, 0))
                    for k in range(KD):
                        last = t.matmul(ps[4 + c % 2][:, :], a_xt[:, k, c * P:(c + 1) * P], wqkv[:, k, D:3 * D],
                                        start=(k == 0), stop=(k == KD - 1))
                    last.then_inc(S("a_kvp"), 1)

            def a_attend(b):
                t.wait_ge(S("a_qf"), b + 1)
                t.wait_ge(S("a_mask"), b + 1)
                for k in range(KD):
                    t.matmul(ps[2 + k][:, :], a_kv[:, k, :], a_qf[:, k, :], start=True, stop=True)
                    last = t.matmul(ps[4 + k][:, :], a_z[:, k, :], a_qf[:, k, :], start=True, stop=True)
                last.then_inc(S("a_on"), 1)

            def a_kvmm(b):
                t.wait_ge(S("a_kf"), b + 1)
                for k in range(KD):
                    for c in range(CPB):
                        last = t.matmul(ps[0][:, k * (P + 1):(k + 1) * (P + 1)], a_k[:, c, k * P:(k + 1) * P],
                                        a_v[:, c, k, :], start=(c == 0), stop=(c == CPB - 1))
                last.then_inc(S("a_kvmm"), 1)

            def a_out(b):
                t.wait_ge(S("a_o"), b + 1)
                for c in range(CPB):
                    for k in range(KD):
                        last = t.matmul(ps[6 + c // 2][:, (c % 2) * D:(c % 2) * D + D], a_o[:, k, c * P:(c + 1) * P],
                                        wo[:, k, :], start=(k == 0), stop=(k == KD - 1))
                last.then_inc(S("a_ymm"), 1)

            def attention(b, before, more):
                a_project(b)
                if before:
                    t.wait_ge(S("a_rq"), b + 1)
                    t.wait_ge(S("a_eq"), b + 1)
                    t.wait_ge(S("a_kb"), CPB * b + CPB)
                    a_attend(b - 1)
                a_kvmm(b)
                if before:
                    a_out(b - 1)
                if more:
                    a_turn(b + 1)

            t.wait_ge(S("ld_cst"), 16)
            t.wait_ge(S("ld_a"), 16 * 7)
            t.wait_ge(S("a_vone"), 1)
            a_turn(0)
            attention(0, False, True)
            with t.Fori(1, BATCH - 1) as b:
                attention(b, True, True)
            attention(BATCH - 1, True, False)
            a_attend(BATCH - 1)
            a_out(BATCH - 1)

            def feed(r):
                t.wait_ge(S("ld_r"), 16 * 3)
                if r == 0:
                    t.wait_ge(S("a_xupd"), BATCH)
                else:
                    t.wait_ge(S("m_stat"), BATCH)
                for b in range(BATCH):
                    t.wait_ge(S(f"f{r}_xn"), b + 1)
                    if b >= 2:
                        t.wait_ge(S(f"f{r}_xt"), b - 1)
                    for k in range(KD):
                        for c in range(CPB):
                            last = turned(ps[2 * (b % 2) + k][:, c * P:(c + 1) * P], f_xn[:, CPB * b + c, :], k, c)
                    last.then_inc(S(f"f{r}_tr"), 1)
                    if b:
                        logits(r, b - 1)
                logits(r, BATCH - 1)
                t.wait_ge(S(f"f{r}_oh"), 1)
                t.matmul(ps[5][:, 0:NCH * E], tri, r_oh, start=True, stop=True)
                t.matmul(ps[6][:, 0:NCH * E], ones, r_oh, start=True, stop=True).then_inc(S(f"f{r}_rank"), 1)
                if r == 0:
                    t.wait_ge(S("ld_ipw"), 16)
                    for k in range(TAPS):
                        t.wait_ge(S(f"ld_cw{k}"), 16)
                        for d in range(KD):
                            n = KD * k + d
                            if n >= 2:
                                t.wait_ge(S("tapw"), n - 1)
                            for c in range(KI):
                                last = t.matmul(ps[n % 2][:, :], ipw[:, c, d * P:(d + 1) * P], cw[:, c, :],
                                                start=(c == 0), stop=(c == KI - 1))
                            last.then_inc(S("tap_mm"), 1)
                    t.wait_ge(S("tapw"), TAPS * KD)

                def tr(par, n):
                    t.wait_ge(S(f"f{r}_x{par}"), 16 * (n + 1))
                    t.wait_ge(S(f"f{r}_xt{par}"), n)
                    for k in range(KD):
                        last = turned(ps[par][:, k * P:(k + 1) * P], t_x[par], k, 0)
                    last.then_inc(S(f"f{r}_tr{par}"), 1)

                def expert(j):
                    return t.value_load(tile_e[0:1, ds(j, 1)] if not isinstance(j, int) else tile_e[0:1, j:j + 1],
                                        min_val=0, max_val=E - 1)

                def first(j, par, n):
                    e = expert(j)
                    t.wait_ge(S(f"f{r}_xt{par}"), n + 1)
                    t.wait_ge(S(f"f{r}_hc{par}"), n)
                    for k in range(KD):
                        last = t.matmul(ps[2 + par][:, :], t_xt[par][:, k, :],
                                        w1[:, row(e), k, :].rearrange("p a h -> p (a h)"),
                                        start=(k == 0), stop=(k == KD - 1))
                    last.then_inc(S(f"f{r}_h{par}"), 1)

                def turn_hidden(par, n):
                    t.wait_ge(S(f"f{r}_hc{par}"), n + 1)
                    t.wait_ge(S(f"f{r}_relu{par}"), n)
                    for k in range(KH):
                        last = turned(ps[4 + par][:, k * P:(k + 1) * P], t_h[par], k, 0)
                    last.then_inc(S(f"f{r}_ht{par}"), 1)

                def second(j, par, n):
                    e = expert(j)
                    t.wait_ge(S(f"f{r}_relu{par}"), n + 1)
                    t.wait_ge(S(f"f{r}_y{par}"), n)
                    for k in range(KH):
                        last = t.matmul(ps[6 + par][:, 0:D], t_ht[par][:, k, :],
                                        w2[:, row(e), k, :].rearrange("p a h -> p (a h)"),
                                        start=(k == 0), stop=(k == KH - 1))
                    last.then_inc(S(f"f{r}_ymm{par}"), 1)

                H = TILES // 2
                t.wait_ge(S(f"ld_ffn{r}"), LD_FFN)
                t.wait_ge(S(f"f{r}_pos"), 1)
                tr(0, 0)
                tr(1, 0)
                first(0, 0, 0)

                def turn(i, more):
                    turn_hidden(0, i)
                    first(2 * i + 1, 1, i)
                    tr(0, i + 1)
                    second(2 * i, 0, i)
                    turn_hidden(1, i)
                    first(2 * i + 2, 0, i + 1)
                    if more:
                        tr(1, i + 1)
                    second(2 * i + 1, 1, i)

                turn(0, True)
                with t.Fori(1, H - 1) as i:
                    turn(i, True)
                turn(H - 1, False)
                turn_hidden(0, H)
                second(TILES - 1, 0, H)

            def logits(r, b):
                t.wait_ge(S(f"f{r}_xt"), b + 1)
                for c in range(CPB):
                    j = (CPB * b + c) * E
                    for k in range(KD):
                        last = t.matmul(ps[7][:, j:j + E], f_xt[b % 2][:, k, c * P:(c + 1) * P], wr[:, k, :],
                                        start=(k == 0), stop=(k == KD - 1))
                last.then_inc(S(f"f{r}_lgmm"), 1)

            feed(0)

            def m_turn(n):
                t.wait_ge(S("m_xn"), n + 1)
                t.wait_ge(S("m_sz"), KI * n)
                for k in range(KD):
                    for c in range(CPB):
                        last = turned(ps[k][:, c * P:(c + 1) * P], m_xn[:, c, :], k, c)
                last.then_inc(S("m_tr"), 1)

            def m_conv(n, o):
                t.wait_ge(S("m_xt"), n + 1)
                if o == 2:
                    t.wait_ge(S("m_u"), KI * n + 1)
                    if not (isinstance(n, int) and n < 2):
                        t.wait_ge(S("m_xupd"), 2 * (n - 1) - 1)
                if o == 3:
                    t.wait_ge(S("m_u"), KI * n + 2)
                    if not (isinstance(n, int) and n < 2):
                        t.wait_ge(S("m_xupd"), 2 * (n - 1))
                for k in range(TAPS):
                    for d in range(KD):
                        last = t.matmul(ps[o % 2][:, :], tapw[:, k, d, o * P:(o + 1) * P], m_xt[:, d, k:k + SEQ],
                                        start=(k == 0 and d == 0), stop=(k == TAPS - 1 and d == KD - 1))
                last.then_inc(S("m_umm"), 1)

            def m_dtmm(n, o):
                t.wait_ge(S("m_u"), KI * n + KI)
                if o >= 2:
                    t.wait_ge(S("m_th"), KI * n + o - 1)
                for k in range(KI):
                    last = t.matmul(ps[o % 2][:, :], dtw[:, k, o * P:(o + 1) * P], m_u[m_par[0]][:, k, :],
                                    start=(k == 0), stop=(k == KI - 1))
                last.then_inc(S("m_dmm"), 1)

            def m_bcmm(n):
                t.wait_ge(S("m_th"), KI * n + 3)
                for k in range(KI):
                    last = t.matmul(ps[0][0:2 * NS, :], bcw[:, k, :], m_u[m_par[0]][:, k, :],
                                    start=(k == 0), stop=(k == KI - 1))
                last.then_inc(S("m_bcmm"), 1)

            def m_zmm(n, o):
                if o == 0:
                    t.wait_ge(S("m_th"), KI * n + KI)
                if o == 1:
                    t.wait_ge(S("m_bclo"), n + 1)
                if o >= 2:
                    t.wait_ge(S("m_sz"), KI * n + o - 1)
                for k in range(KD):
                    last = t.matmul(ps[(o + 1) % 2][:, :], zw[:, k, o * P:(o + 1) * P], m_xt[:, k, PAD:],
                                    start=(k == 0), stop=(k == KD - 1))
                last.then_inc(S("m_zmm"), 1)

            def m_out(b, n):
                t.wait_ge(S("m_y"), b + 1)
                if n is not None:
                    t.wait_ge(S("m_u"), KI * n + 2)
                else:
                    t.wait_ge(S("m_sz"), KI * BATCH)
                    if b:
                        t.wait_ge(S("m_xupd"), 2 * b)
                for c in range(CPB):
                    for k in range(KI):
                        last = t.matmul(ps[c // 2][:, (c % 2) * D:(c % 2) * D + D], m_y[:, k, c * P:(c + 1) * P],
                                        outw[:, k, :], start=(k == 0), stop=(k == KI - 1))
                    if c % 2:
                        last.then_inc(S("m_omm"), 1)

            m_par = [0]

            def m_pre(n, par, slot, half):
                m_par[0] = par
                if slot == 0 and half == 0:
                    m_turn(n)
                if slot == 0 and half == 1:
                    m_conv(n, 0)
                if slot == 1 and half == 1:
                    m_conv(n, 1)
                if slot == 3 and half == 1:
                    m_conv(n, 2)
                if slot == 4 and half == 1:
                    m_conv(n, 3)
                if slot in (5, 6):
                    m_dtmm(n, 2 * (slot - 5) + half)
                if slot == 7 and half == 1:
                    m_bcmm(n)
                    for o in range(KI):
                        m_zmm(n, o)

            def spread(b, par, st):
                n = NS * b + st
                t.wait_ge(S("m_db"), n)
                t.matmul(ps[2][:, :], stack[:, st:st + 1].to_broadcast([4 * NS, P]), m_bc[par][:, :],
                         start=True, stop=True).then_inc(S("m_bb"), 1)
                t.wait_ge(S("m_c"), n)
                t.matmul(ps[3][:, :], stack[:, NS + st:NS + st + 1].to_broadcast([4 * NS, P]), m_bc[par][:, :],
                         start=True, stop=True).then_inc(S("m_cb"), 1)

            def m_nsum(b, p):
                t.wait_ge(S("m_q"), (NS // 2) * b + p + 1)
                if p == 0:
                    t.wait_ge(S("m_y0"), b)
                for k in range(KI):
                    last = t.matmul(ps[4 + k][:, :], ident, m_q[:, k, :], start=(p == 0), stop=(p == NS // 2 - 1))
                last.then_inc(S("m_nsum"), 1)

            def m_scan(b, par, before, more):
                t.wait_ge(S("m_bclo"), b + 1)
                for slot in range(NS // 2):
                    for half in range(2):
                        spread(b, par, 2 * slot + half)
                        if before and slot == 0 and half == 0:
                            m_nsum(b - 1, NS // 2 - 1)
                        if before and slot == 2 and half == 1:
                            m_out(b - 1, b + 1 if more else None)
                        if more:
                            m_pre(b + 1, 1 - par, slot, half)
                    if slot:
                        m_nsum(b, slot - 1)

            t.wait_ge(S("m_stack"), 1)
            for slot in range(8):
                for half in range(2):
                    m_pre(0, 0, slot, half)
            m_scan(0, 0, False, True)
            with t.Fori(0, (BATCH - 2) // 2) as i:
                m_scan(2 * i + 1, 1, True, True)
                m_scan(2 * i + 2, 0, True, True)
            m_scan(BATCH - 1, 1, True, False)
            m_nsum(BATCH - 1, NS // 2 - 1)
            m_out(BATCH - 1, None)
            feed(1)


def kernel(**inputs):
    import numpy as np
    import concourse.bacc as bacc
    from concourse import mybir as mb
    from concourse.bass_utils import run_bass_kernel_spmd as run

    def a(name):
        return np.asarray(inputs[name])

    def cols(v):
        return v.reshape(-1, P).T

    cst = np.zeros((P, C_ALL), np.float32)
    i = np.arange(P)
    cst[:, C_ID:C_ID + P] = i[:, None] == i
    cst[:, C_TRI:C_TRI + P] = i[:, None] <= i
    cst[:, C_ONE:C_ONE + P] = 1
    cst[:, C_BLK:C_BLK + P] = i[:, None] // HEAD == i // HEAD
    cst[:, C_RST:C_RST + E * NCH] = np.arange(E * NCH) % NCH != 0
    cst[:, C_THR:C_THR + NCH] = np.arange(NCH) * P
    cst[:, C_DESC:C_DESC + E] = E - np.arange(E)
    cst[:, C_IOTA:C_IOTA + 40] = np.arange(40)
    cst[:, C_STK:C_STK + 32] = i[:, None] % 32 == np.arange(32)
    B = "L0_attn_b_"
    arrays = {
        "cst": cst,
        "x": a("L0_attn_a_inputs_q"),
        "Wq": a("L0_attn_a_Wq"), "Wk": a("L0_attn_a_Wk"), "Wv": a("L0_attn_a_Wv"), "Wo": a("L0_attn_a_Wo"),
        "bq": cols(a("L0_attn_a_bq")),
        "bkv": np.concatenate([a("L0_attn_a_bk"), a("L0_attn_a_bv")]),
        "bo": a("L0_attn_a_bo"),
        "Wr": a("L0_ffn_Wr"), "br": a("L0_ffn_br"), "W1": a("L0_ffn_W1"), "W2": a("L0_ffn_W2"),
        "b1": a("L0_ffn_b1").reshape(E, KH, P).transpose(2, 0, 1),
        "b2": a("L0_ffn_b2"),
        "ip_x": a(B + "in_proj_w")[0:DI],
        "zw": a(B + "in_proj_w")[DI:2 * DI].T,
        "conv": a(B + "conv_w").transpose(2, 1, 0),
        "dtw": a(B + "dt_w").T,
        "bcw": np.concatenate([a(B + "B_w"), a(B + "C_w")]).T,
        "outw": a(B + "out_w").T,
        "A_log": a(B + "A_log").reshape(KI, P, NS).transpose(1, 0, 2),
        "mvec": np.stack([cols(a(B + "conv_b")), cols(a(B + "dt_b")), cols(a(B + "D"))], 1),
    }
    nc = bacc.Bacc("TRN2", target_bir_lowering=False, num_devices=1)
    T, feed = {}, {}
    for name, v in arrays.items():
        v = np.ascontiguousarray(v)
        feed[f"in_{name}"] = v
        T[name] = nc.dram_tensor(f"in_{name}", v.shape, mb.dt.from_np(v.dtype), kind="ExternalInput").ap()
    T["out"] = nc.dram_tensor("out_x", (BATCH, SEQ, D), mb.dt.float32, kind="ExternalOutput").ap()
    build(nc, T)
    r = run(nc, [feed], core_ids=[0])
    return r.results[0]["out_x"]
```

```python
from contextlib import ExitStack

import concourse.bass as bass
from concourse import mybir

P = 128
BATCH, SEQ, D = 8, 512, 256
TOK = BATCH * SEQ
NCH = TOK // P
CPB = SEQ // P
KD = D // P
HEAD = 16
HPT = P // HEAD
E, HID = 8, 512
KH = HID // P
DI, NS, TAPS = 512, 16, 4
KI = DI // P
TILES = NCH + E - 1
PAD = TAPS - 1
LN_EPS, NORM_EPS = 1e-5, 1e-6

F32 = mybir.dt.float32
F32R = mybir.dt.float32r
I32 = mybir.dt.int32
U32 = mybir.dt.uint32
ALU = mybir.AluOpType
ACT = mybir.ActivationFunctionType
AX = mybir.AxisListType
ds = bass.DynSlice

CONV_AT = (2, 3, 4, 5, 11, 12, 13, 15)
OUT_AT = (7, 8)
DT_AT = (17, 19, 21, 23)
BC_AT = 24
Z_AT = (25, 27, 28, 29)
U_AT = (2, 3, 7, 8)
TH_AT = (9, 10, 11, 12)
ZTH_AT = (13, 14, 15, 15)

POOL_C = (1, 3, 5, 7, 9, 11, 13, 15)
NPC, NVC = len(POOL_C), NS - len(POOL_C)


def pool_c(st):
    return sum(s < st for s in POOL_C)


AT_BANKS = ((6, 0, 3), (7, 3, 3), (1, 6, 2))

C_ID, C_TRI, C_ONE, C_BLK = 0, P, 2 * P, 3 * P
C_RST = 4 * P
C_THR = C_RST + E * NCH
C_DESC = C_THR + NCH
C_IOTA = C_DESC + E
C_STK = C_IOTA + 40
C_ALL = C_STK + 32


def build(nc, T):
    with ExitStack() as ctx:
        sems = {}

        def S(name):
            if name not in sems:
                sems[name] = ctx.enter_context(nc.semaphore(name))
            return sems[name]

        def sb(name, shape, dt=F32):
            return ctx.enter_context(nc.sbuf_tensor(name, shape, dt))

        x = sb("x", [P, NCH, D])
        cst = sb("cst", [P, C_ALL])
        stats = sb("stats", [P, NCH, 6])
        mean, rstd = sb("mean", [P, NCH]), sb("rstd", [P, NCH])
        nw = [sb(f"nw{i}", [P, NCH]) for i in range(4)]
        ident = cst[:, C_ID:C_ID + P]
        tri, ones = cst[:, C_TRI:C_TRI + P], cst[:, C_ONE:C_ONE + P]
        blk = cst[:, C_BLK:C_BLK + P]
        heads = cst[:, C_BLK:C_BLK + P].rearrange("p (h m) -> p h m", h=HPT)[:, :, 0]
        tapw = sb("tapw", [P, TAPS, KD, DI])
        zw = sb("zw", [P, KD, DI])
        dtw = sb("dtw", [P, KI, DI])
        bcw = sb("bcw", [P, KI, 2 * NS])
        outw = sb("outw", [P, KI, D])
        a_neg = sb("a_neg", [P, KI, NS])
        mvec = sb("mvec", [P, 3, KI])
        far = sb("far", [P, KI * NS])
        far_sum = sb("far_sum", [P, 1])
        far_flag = sb("far_flag", [P, 1], I32)
        stack = sb("stack", [2 * 2 * NS, 2 * NS], F32R)
        wr = sb("wr", [P, KD, E])
        br = sb("br", [P, E])
        b1t = sb("b1t", [P, E, KH])
        pmax = sb("pmax", [P, NCH])
        pos = sb("pos", [P, NCH], U32)
        tile_e = sb("tile_e", [P, 40], I32)
        AR = 34000
        arena = sb("arena", [P, AR])

        class Space:

            def __init__(self, at):
                self.at = at

            def take(self, n):
                v = arena[:, self.at:self.at + n]
                self.at += n
                assert self.at <= AR, self.at
                return v

        fs = Space(0)
        w1 = fs.take(E * KD * HID).rearrange("p (e k h) -> p e k h", e=E, k=KD)
        w2 = fs.take(E * KH * D).rearrange("p (e k d) -> p e k d", e=E, k=KH)
        b2 = fs.take(E * D).rearrange("p (e d) -> p e d", e=E)
        FEED = fs.at

        s = Space(FEED)
        wqkv = s.take(KD * 3 * D).rearrange("p (k n) -> p k n", k=KD)
        wo = s.take(KD * D).rearrange("p (k n) -> p k n", k=KD)
        bkv = s.take(2 * D)
        bo = s.take(D)
        bq = s.take(KD)
        a_xn = s.take(CPB * D).rearrange("p (c d) -> p c d", c=CPB)
        a_xt = s.take(KD * SEQ).rearrange("p (k t) -> p k t", k=KD)
        a_eq = s.take(KD * SEQ).rearrange("p (k t) -> p k t", k=KD)
        a_rq = s.take(KD * SEQ).rearrange("p (k t) -> p k t", k=KD)
        a_qf = s.take(KD * SEQ).rearrange("p (k t) -> p k t", k=KD)
        a_k = s.take(CPB * D).rearrange("p (c d) -> p c d", c=CPB)
        a_ek = s.take(CPB * D).rearrange("p (c d) -> p c d", c=CPB)
        a_v = s.take(CPB * KD * (P + 1)).rearrange("p (c k n) -> p c k n", c=CPB, k=KD)
        a_kv = s.take(KD * (P + HPT)).rearrange("p (k n) -> p k n", k=KD)
        a_nr = s.take(CPB * KD * HPT)
        a_o = s.take(CPB * D).rearrange("p (c d) -> p c d", c=CPB)
        a_ot = s.take(KD * SEQ).rearrange("p (k t) -> p k t", k=KD)
        zeros = s.take(D)

        s = Space(FEED)
        f_xn = s.take(NCH * D).rearrange("p (c d) -> p c d", c=NCH)
        f_gather = f_xn
        tail = s.at
        f_xt = [s.take(KD * SEQ).rearrange("p (k t) -> p k t", k=KD) for _ in range(2)]
        r_lg, r_eq, r_ex, r_oh, r_pm, r_tot, r_cum, r_cmp = [s.take(NCH * E) for _ in range(8)]
        r_mx, r_se, r_m2, r_pf = [s.take(NCH) for _ in range(4)]
        r_tl, r_te, r_ba = [s.take(E) for _ in range(3)]
        assert s.at <= AR - KI * (DI + D)
        s = Space(tail)
        r_cmp2, r_te40 = s.take(40 * E), s.take(40)
        s = Space(tail)
        t_x = [s.take(D) for _ in range(2)]
        t_xt = [s.take(KD * P).rearrange("p (k t) -> p k t", k=KD) for _ in range(2)]
        t_h = [s.take(HID) for _ in range(2)]
        t_ht = [s.take(HID).rearrange("p (k t) -> p k t", k=KH) for _ in range(2)]
        t_y = [s.take(D) for _ in range(2)]
        s = Space(AR - KI * (DI + D))
        cw = s.take(KI * DI).rearrange("p (k n) -> p k n", k=KI)
        ipw = s.take(KI * D).rearrange("p (k n) -> p k n", k=KI)

        s = Space(0)
        m_u, m_dt, m_sz = [[s.take(KI * SEQ).rearrange("p (k t) -> p k t", k=KI) for _ in range(2)]
                           for _ in range(3)]
        m_w = s.take(KI * SEQ).rearrange("p (k t) -> p k t", k=KI)
        m_xn = s.take(CPB * D).rearrange("p (c d) -> p c d", c=CPB)
        m_xt = s.take(KD * (SEQ + PAD)).rearrange("p (k t) -> p k t", k=KD)
        m_a = [s.take(KI * SEQ).rearrange("p (k t) -> p k t", k=KI) for _ in range(2)]
        m_b = [s.take(KI * SEQ).rearrange("p (k t) -> p k t", k=KI) for _ in range(4)]
        m_q = s.take(KI * SEQ).rearrange("p (k t) -> p k t", k=KI)
        m_y = s.take(KI * SEQ).rearrange("p (k t) -> p k t", k=KI)
        m_c = s.take(SEQ)
        m_bc = [sb(f"m_bc{i}", [4 * NS, SEQ], F32R) for i in range(2)]

        ps = [ctx.enter_context(nc.psum_tensor(f"ps{i}", [P, 512], F32)) for i in range(8)]

        xs = nc.dram_tensor("sorted_rows", (TILES * P, D), F32, kind="Internal").ap()
        ys = [nc.dram_tensor(f"sorted_results{r}", (TILES * P, D), F32, kind="Internal").ap() for r in range(2)]

        block = ctx.enter_context(nc.Block())

        def row(c):
            return ds(c, 1) if not isinstance(c, int) else slice(c, c + 1)

        def load_ffn(eng, r):
            for e in range(E):
                eng.dma_start(w1[:, e], T["W1"][e].rearrange("(k p) h -> p k h", p=P)).then_inc(S(f"ld_ffn{r}"), 16)
                eng.dma_start(w2[:, e], T["W2"][e].rearrange("(k p) d -> p k d", p=P)).then_inc(S(f"ld_ffn{r}"), 16)
            eng.dma_start(b2, T["b2"].partition_broadcast(P)).then_inc(S(f"ld_ffn{r}"), 16)

        LD_FFN = 16 * (2 * E + 1)

        @block.sync
        def _(sp):
            xin = T["x"].rearrange("b (c p) d -> p b c d", p=P)
            for b in range(BATCH):
                if b == 1:
                    sp.dma_start(cst[:, :], T["cst"]).then_inc(S("ld_cst"), 16)
                sp.dma_start(x[:, b * CPB:(b + 1) * CPB, :], xin[:, b]).then_inc(S(f"ld_x{min(b, 1)}"), 16)
            sp.wait_ge(S("ld_x1"), 16 * (BATCH - 1))
            load_ffn(sp, 0)
            sp.wait_ge(S("a_xupd"), BATCH)
            sp.wait_ge(S("xs_zeroed"), 16)
            sp.dma_start(ipw, T["ip_x"].rearrange("(k p) d -> p k d", p=P)).then_inc(S("ld_ipw"), 16)
            for k in range(TAPS):
                if k:
                    sp.wait_ge(S("tap_mm"), KD * k)
                sp.dma_start(cw, T["conv"][k].rearrange("(k p) d -> p k d", p=P)).then_inc(S(f"ld_cw{k}"), 16)

            def tiles_loop(r):
                def at(j):
                    return xs[j * P:(j + 1) * P] if isinstance(j, int) else xs[ds(j * P, P)]

                def load(j, par):
                    sp.dma_start(t_x[par], at(j)).then_inc(S(f"f{r}_x{par}"), 16)

                H = TILES // 2
                sp.wait_ge(S(f"f{r}_scat"), 16 * NCH)
                load(0, 0)
                load(1, 1)

                def turn(i, more):
                    sp.wait_ge(S(f"f{r}_tr0"), i + 1)
                    load(2 * i + 2, 0)
                    if more:
                        sp.wait_ge(S(f"f{r}_tr1"), i + 1)
                        load(2 * i + 3, 1)

                turn(0, True)
                with sp.Fori(1, H - 1) as i:
                    turn(i, True)
                turn(H - 1, False)

            tiles_loop(0)
            sp.wait_ge(S("m_xupd"), 2 * BATCH)
            load_ffn(sp, 1)
            tiles_loop(1)
            out = T["out"].rearrange("b (c p) d -> p b c d", p=P)
            for b in range(BATCH):
                sp.wait_ge(S("f1_xupd"), b + 1)
                sp.dma_start(out[:, b], x[:, b * CPB:(b + 1) * CPB, :]).then_inc(S("out_done"), 16)
            sp.wait_ge(S("out_done"), 16 * BATCH)

        @block.gpsimd
        def _(g):
            g.memset(a_v[:, :, :, P:P + 1], 1.0).then_inc(S("a_vone"), 1)
            g.memset(zeros, 0.0).then_inc(S("zero"), 1)
            g.wait_ge(S("zero"), 1)
            g.wait_ge(S("ld_x1"), 16 * (BATCH - 1))
            g.dma_start(xs.rearrange("(n p) d -> p n d", p=P), zeros.unsqueeze(1).to_broadcast([P, TILES, D]))\
                .then_inc(S("xs_zeroed"), 16)

            def a_bias(b):
                g.wait_ge(S("a_xn"), b + 1)
                xv = x[:, ds(CPB * b, CPB) if not isinstance(b, int) else slice(CPB * b, CPB * b + CPB), :]
                g.tensor_tensor(xv, xv, bo.unsqueeze(1).to_broadcast([P, CPB, D]), ALU.add).then_inc(S("a_bias"), 1)

            g.wait_ge(S("ld_a"), 16 * 7)
            a_bias(0)
            with g.Fori(1, BATCH) as b:
                a_bias(b)

            def scatter(r):
                g.wait_ge(S(f"f{r}_pos"), 1)
                if r == 0:
                    g.wait_ge(S("xs_zeroed"), 16)
                for c in range(NCH):
                    g.indirect_dma_start(out=xs, out_offset=bass.IndirectOffsetOnAxis(ap=pos[:, c:c + 1], axis=0),
                                         in_=f_xn[:, c, :], in_offset=None).then_inc(S(f"f{r}_scat"), 16)

            def store_tiles(r):
                def store(j, par, n):
                    g.wait_ge(S(f"f{r}_y{par}"), n)
                    g.dma_start(ys[r][j * P:(j + 1) * P] if isinstance(j, int) else ys[r][ds(j * P, P)],
                                t_y[par]).then_inc(S(f"f{r}_st{par}"), 16)

                H = TILES // 2
                store(0, 0, 1)
                store(1, 1, 1)
                with g.Fori(1, H) as i:
                    store(2 * i, 0, i + 1)
                    store(2 * i + 1, 1, i + 1)
                store(TILES - 1, 0, H + 1)

            def gather(r):
                g.wait_ge(S(f"f{r}_st0"), 16 * (TILES - TILES // 2))
                g.wait_ge(S(f"f{r}_st1"), 16 * (TILES // 2))
                for c in range(NCH):
                    g.indirect_dma_start(out=f_gather[:, c, :], out_offset=None, in_=ys[r],
                                         in_offset=bass.IndirectOffsetOnAxis(ap=pos[:, c:c + 1], axis=0))\
                        .then_inc(S(f"f_g{c // CPB}"), 16)

            scatter(0)
            store_tiles(0)
            gather(0)
            g.wait_ge(S("f0_xupd"), BATCH)
            for a in m_a:
                g.memset(a[:, :, 0:1], 0.0).then_inc(S("m_zero"), 1)
            g.memset(m_xt[:, :, 0:PAD], 0.0).then_inc(S("m_zero"), 1)

            def pairs(b):
                for p in range(NS // 2):
                    n = 2 * p
                    for st in (n, n + 1):
                        if st in POOL_C:
                            g.wait_ge(S("m_scan"), NS * b + st + 1)
                            g.wait_ge(S("m_cs"), NPC * b + pool_c(st) + 1)
                            g.tensor_tensor(m_b[st % 4], m_b[st % 4], m_c.unsqueeze(1).to_broadcast([P, KI, SEQ]),
                                            ALU.mult).then_inc(S("m_cp"), 1)
                    g.wait_ge(S("m_c"), NVC * b + n + 2 - pool_c(n + 2))
                    g.wait_ge(S("m_cp"), NPC * b + pool_c(n + 2))
                    g.wait_ge(S("m_nsum"), (NS // 2) * b + p)
                    g.tensor_tensor(m_q, m_b[n % 4], m_b[(n + 1) % 4], ALU.add).then_inc(S("m_q"), 1)

            pairs(0)
            with g.Fori(1, BATCH) as b:
                pairs(b)
            scatter(1)
            store_tiles(1)
            gather(1)

        @block.scalar
        def _(a):
            a.dma_start(wqkv[:, :, 0:D], T["Wq"].rearrange("(k p) n -> p k n", p=P)).then_inc(S("ld_a"), 16)
            a.dma_start(wqkv[:, :, D:2 * D], T["Wk"].rearrange("(k p) n -> p k n", p=P)).then_inc(S("ld_a"), 16)
            a.dma_start(wqkv[:, :, 2 * D:3 * D], T["Wv"].rearrange("(k p) n -> p k n", p=P)).then_inc(S("ld_a"), 16)
            a.dma_start(wo, T["Wo"].rearrange("(k p) n -> p k n", p=P)).then_inc(S("ld_a"), 16)
            a.dma_start(bkv, T["bkv"].partition_broadcast(P)).then_inc(S("ld_a"), 16)
            a.dma_start(bo, T["bo"].partition_broadcast(P)).then_inc(S("ld_a"), 16)
            a.dma_start(bq, T["bq"]).then_inc(S("ld_a"), 16)
            a.dma_start(wr[:, :, :], T["Wr"].rearrange("(k p) e -> p k e", p=P)).then_inc(S("ld_r"), 16)
            a.dma_start(br[:, :], T["br"].partition_broadcast(P)).then_inc(S("ld_r"), 16)
            a.dma_start(b1t[:, :, :], T["b1"]).then_inc(S("ld_r"), 16)
            a.wait_ge(S("ld_x1"), 16 * (BATCH - 1))
            for dst, name in ((zw, "zw"), (dtw, "dtw"), (bcw, "bcw"), (outw, "outw")):
                a.dma_start(dst[:, :, :], T[name].rearrange("(k p) n -> p k n", p=P)).then_inc(S("ld_m"), 16)
            a.dma_start(a_neg[:, :, :], T["A_log"]).then_inc(S("ld_m"), 16)
            a.dma_start(mvec[:, :, :], T["mvec"]).then_inc(S("ld_m"), 16)

            def xt_copy(b):
                a.wait_ge(S("a_tr"), b + 1)
                if not (isinstance(b, int) and b == 0):
                    a.wait_ge(S("a_kvp"), CPB * b)
                for k in range(KD):
                    last = a.activation(a_xt[:, k, :], ps[k][:, :], ACT.Copy)
                last.then_inc(S("a_xt"), 1)

            def attention(b, before, more):
                a.wait_ge(S("a_q"), b + 1)
                if not (isinstance(b, int) and b == 0):
                    a.wait_ge(S("a_qf"), b)
                for k in range(KD):
                    a.activation(a_eq[:, k, :], ps[2 + k][:, :], ACT.Exp, bias=bq[:, k:k + 1])
                    last = a.activation(a_rq[:, k, :], ps[2 + k][:, :], ACT.Relu, bias=bq[:, k:k + 1])
                last.then_inc(S("a_eq"), 1)
                if before:
                    o_copy(b - 1)
                a.wait_ge(S("a_kb"), CPB * b + CPB)
                if not (isinstance(b, int) and b == 0):
                    a.wait_ge(S("a_kf"), b)
                a.activation(a_ek, a_k, ACT.Exp).then_inc(S("a_ek"), 1)
                if more:
                    xt_copy(b + 1)

            def o_copy(b):
                a.wait_ge(S("a_otr"), b + 1)
                if not (isinstance(b, int) and b == 0):
                    a.wait_ge(S("a_ymm"), b)
                for k in range(KD):
                    last = a.activation(a_ot[:, k, :], ps[2 + k][:, :], ACT.Copy)
                last.then_inc(S("a_ot"), 1)

            a.wait_ge(S("ld_a"), 16 * 7)
            xt_copy(0)
            attention(0, False, True)
            with a.Fori(1, BATCH - 1) as b:
                attention(b, True, True)
            attention(BATCH - 1, True, False)
            o_copy(BATCH - 1)

            def feed(r):
                for b in range(BATCH):
                    a.wait_ge(S(f"f{r}_tr"), b + 1)
                    if b >= 2:
                        a.wait_ge(S(f"f{r}_lgmm"), b - 1)
                    for k in range(KD):
                        last = a.activation(f_xt[b % 2][:, k, :], ps[2 * (b % 2) + k][:, :], ACT.Copy)
                    last.then_inc(S(f"f{r}_xt"), 1)
                a.wait_ge(S(f"f{r}_lg"), 1)
                a.activation(r_ex, r_lg, ACT.Exp).then_inc(S(f"f{r}_ex"), 1)
                if r == 0:
                    for k in range(TAPS):
                        for d in range(KD):
                            n = KD * k + d
                            a.wait_ge(S("tap_mm"), n + 1)
                            a.activation(tapw[:, k, d, :], ps[n % 2][:, :], ACT.Copy).then_inc(S("tapw"), 1)
                    a.wait_ge(S("ld_m"), 16 * 6)
                    a.activation(a_neg[:, :, :], a_neg[:, :, :], ACT.Exp).then_inc(S("m_aexp"), 1)
                    a.wait_ge(S("m_aexp"), 1)
                    a.activation(a_neg[:, :, :], a_neg[:, :, :], ACT.Copy, scale=-1.0).then_inc(S("m_aexp"), 1)
                    a.activation(mvec[:, 1, :], mvec[:, 1, :], ACT.Copy, scale=0.5).then_inc(S("m_aexp"), 1)

                def xt(par, n):
                    a.wait_ge(S(f"f{r}_tr{par}"), n + 1)
                    a.wait_ge(S(f"f{r}_h{par}"), n)
                    a.activation(t_xt[par], ps[par][:, 0:KD * P].rearrange("p (k t) -> p k t", k=KD), ACT.Copy)\
                        .then_inc(S(f"f{r}_xt{par}"), 1)

                def relu(e, par, n):
                    a.wait_ge(S(f"f{r}_ht{par}"), n + 1)
                    a.wait_ge(S(f"f{r}_ymm{par}"), n)
                    for k in range(KH):
                        last = a.activation(t_ht[par][:, k, :], ps[4 + par][:, k * P:(k + 1) * P], ACT.Relu,
                                            bias=b1t[:, row(e), k:k + 1].rearrange("p a b -> p (a b)"))
                    last.then_inc(S(f"f{r}_relu{par}"), 1)

                def expert(j):
                    return a.value_load(tile_e[0:1, ds(j, 1)] if not isinstance(j, int) else tile_e[0:1, j:j + 1],
                                        min_val=0, max_val=E - 1)

                H = TILES // 2
                a.wait_ge(S(f"f{r}_pos"), 1)
                xt(0, 0)
                xt(1, 0)

                def turn(i, more):
                    relu(expert(2 * i), 0, i)
                    xt(0, i + 1)
                    relu(expert(2 * i + 1), 1, i)
                    if more:
                        xt(1, i + 1)

                turn(0, True)
                with a.Fori(1, H - 1) as i:
                    turn(i, True)
                turn(H - 1, False)
                relu(expert(TILES - 1), 0, H)

            feed(0)

            def m_xtcopy(n):
                a.wait_ge(S("m_tr"), n + 1)
                a.wait_ge(S("m_zmm"), KI * n)
                for k in range(KD):
                    last = a.activation(m_xt[:, k, PAD:], ps[k][:, :], ACT.Copy)
                last.then_inc(S("m_xt"), 1)

            def m_uevac(n, par, o):
                a.wait_ge(S("m_umm"), KI * n + o + 1)
                if not (isinstance(n, int) and n < 2):
                    a.wait_ge(S("m_y"), n - 1)
                a.activation(m_u[par][:, o, :], ps[o % 2][:, :], ACT.Identity, bias=mvec[:, 0, o:o + 1])\
                    .then_inc(S("m_u"), 1)

            def m_thevac(n, par, o):
                a.wait_ge(S("m_dmm"), KI * n + o + 1)
                a.activation(m_dt[par][:, o, :], ps[o % 2][:, :], ACT.Tanh, bias=mvec[:, 1, o:o + 1], scale=0.5)\
                    .then_inc(S("m_th"), 1)

            def m_bchi(n, par):
                a.wait_ge(S("m_bcmm"), n + 1)
                a.activation(m_bc[par][0:2 * NS, :], ps[0][0:2 * NS, :], ACT.Copy).then_inc(S("m_bchi"), 1)

            def m_zevac(n, par, o):
                a.wait_ge(S("m_zmm"), KI * n + o + 1)
                a.activation(m_sz[par][:, o, :], ps[(o + 1) % 2][:, :], ACT.Tanh, scale=0.5).then_inc(S("m_zth"), 1)

            def m_pre(n, par, st):
                if st == 0:
                    m_xtcopy(n)
                if st in U_AT:
                    m_uevac(n, par, U_AT.index(st))
                if st in TH_AT:
                    m_thevac(n, par, TH_AT.index(st))
                if st == 13:
                    m_bchi(n, par)
                if st in ZTH_AT:
                    for o in range(KI):
                        if ZTH_AT[o] == st:
                            m_zevac(n, par, o)

            def m_scan(b, par, more):
                for st in range(NS):
                    n = NS * b + st
                    if st == 0:
                        a.wait_ge(S("m_w"), b + 1)
                    if not (isinstance(b, int) and n < 2):
                        a.wait_ge(S("m_scan"), n - 1)
                    for k in range(KI):
                        last = a.activation(m_a[st % 2][:, k, 1:], m_dt[par][:, k, 1:], ACT.Exp,
                                            scale=a_neg[:, k, st:st + 1])
                    last.then_inc(S("m_exp"), 1)
                    a.wait_ge(S("m_db"), n + 1)
                    a.activation(m_b[st % 4], m_b[st % 4], ACT.Copy, bias=1e-6).then_inc(S("m_eps"), 1)
                    if st in POOL_C:
                        a.wait_ge(S("m_cb"), n + 1)
                        a.wait_ge(S("m_cp"), NPC * b + pool_c(st))
                        a.activation(m_c, ps[3][:, :], ACT.Copy).then_inc(S("m_cs"), 1)
                    if more:
                        m_pre(b + 1, 1 - par, st)

            a.wait_ge(S("m_zero"), 3)
            a.wait_ge(S("f0_xupd"), BATCH)
            a.wait_ge(S("m_aexp"), 3)
            for st in range(NS):
                m_pre(0, 0, st)
            m_scan(0, 0, True)
            with a.Fori(0, (BATCH - 2) // 2) as i:
                m_scan(2 * i + 1, 1, True)
                m_scan(2 * i + 2, 0, True)
            m_scan(BATCH - 1, 1, False)
            feed(1)

        @block.vector
        def _(v):
            chain = S("v_chain")
            count = [0]

            def link(ins):
                count[0] += 1
                ins.then_inc(chain, 1)
                v.wait_ge(chain, count[0])

            def row_stats(c):
                return v.bn_stats(out=stats[:, row(c), :].rearrange("p a s -> p (a s)"),
                                  in_=x[:, row(c), :].rearrange("p a d -> p (a d)"))

            def layer_norm_scales(lo=0, hi=NCH):
                me, m2e, mo, m2o = [stats[:, lo:hi, i] for i in (1, 2, 4, 5)]
                d, q, var, t = [w[:, lo:hi] for w in nw]
                v.tensor_tensor(d, me, mo, ALU.subtract)
                v.tensor_tensor(q, me, mo, ALU.add)
                link(v.tensor_tensor(t, m2e, m2o, ALU.add))
                v.tensor_scalar(mean[:, lo:hi], q, 0.5, None, ALU.mult)
                link(v.tensor_scalar(var, t, 1.0 / D, LN_EPS, ALU.mult, ALU.add))
                link(v.tensor_tensor(q, d, d, ALU.mult))
                link(v.scalar_tensor_tensor(out=d, in0=q, scalar=0.25, in1=var, op0=ALU.mult, op1=ALU.add))
                y = rstd[:, lo:hi]
                link(v.tensor_scalar(y.bitcast(I32), d.bitcast(I32), -0.5, 1597463007.0, ALU.mult, ALU.add))
                for _ in range(4):
                    link(v.tensor_tensor(q, y, y, ALU.mult))
                    link(v.scalar_tensor_tensor(out=t, in0=q, scalar=-0.5, in1=d, op0=ALU.mult, op1=ALU.mult))
                    link(v.scalar_tensor_tensor(out=y, in0=t, scalar=1.5, in1=y, op0=ALU.add, op1=ALU.mult))

            def ln_apply(out, c):
                return v.tensor_scalar(out, x[:, row(c), :].rearrange("p a d -> p (a d)"), mean[:, row(c)],
                                       rstd[:, row(c)], ALU.subtract, ALU.mult)

            def first_stats(lo, hi):
                for c in range(lo, hi):
                    last = row_stats(c)
                link(last)
                layer_norm_scales(lo, hi)

            def a_norm(b):
                if not (isinstance(b, int) and b == 0):
                    v.wait_ge(S("a_tr"), b)
                for c in range(CPB):
                    last = ln_apply(a_xn[:, c, :], CPB * b + c)
                last.then_inc(S("a_xn"), 1)

            def a_kvbias(b):
                if not (isinstance(b, int) and b == 0):
                    v.wait_ge(S("a_kvmm"), b)
                for c in range(CPB):
                    v.wait_ge(S("a_kvp"), CPB * b + c + 1)
                    v.tensor_tensor(a_v[:, c, :, 0:P], ps[4 + c % 2][:, D:2 * D].rearrange("p (k n) -> p k n", k=KD),
                                    bkv[:, D:2 * D].rearrange("p (k n) -> p k n", k=KD), ALU.add)
                    v.tensor_tensor(a_k[:, c, :], ps[4 + c % 2][:, 0:D], bkv[:, 0:D], ALU.add).then_inc(S("a_kb"), 1)

            def a_kfeature(b):
                v.wait_ge(S("a_ek"), b + 1)
                v.tensor_scalar(a_ek, a_ek, 1.0, None, ALU.min).then_inc(S("a_ekmin"), 1)
                v.wait_ge(S("a_ekmin"), b + 1)
                v.scalar_tensor_tensor(out=a_k, in0=a_k, scalar=0.0, in1=a_ek, op0=ALU.max, op1=ALU.add)\
                    .then_inc(S("a_kf"), 1)

            def a_normalise(b):
                v.wait_ge(S("a_at"), b + 1)
                if not (isinstance(b, int) and b == 0):
                    v.wait_ge(S("a_otr"), b)
                for bank, u0, n in AT_BANKS:
                    g = ps[bank][:, 0:n * (P + HPT)].rearrange("p (u n) -> p u n", u=n)
                    last = v.tensor_scalar(a_nr[:, u0 * HPT:(u0 + n) * HPT].rearrange("p (u h) -> p u h", u=n),
                                           g[:, :, P:P + HPT], NORM_EPS, None, ALU.max)
                last.then_inc(S("a_nmax"), 1)
                v.wait_ge(S("a_nmax"), b + 1)
                v.reciprocal(a_nr, a_nr).then_inc(S("a_nrec"), 1)
                v.wait_ge(S("a_nrec"), b + 1)
                o = a_o.rearrange("p c (k h m) -> p (c k) h m", k=KD, h=HPT)
                for bank, u0, n in AT_BANKS:
                    g = ps[bank][:, 0:n * (P + HPT)].rearrange("p (u n) -> p u n", u=n)
                    last = v.tensor_tensor(o[:, u0:u0 + n], g[:, :, 0:P].rearrange("p u (h m) -> p u h m", h=HPT),
                                           a_nr[:, u0 * HPT:(u0 + n) * HPT].rearrange("p (u h) -> p u h", u=n)
                                           .unsqueeze(3).to_broadcast([P, n, HPT, HEAD]), ALU.mult)
                last.then_inc(S("a_o"), 1)

            def a_qfeature(b):
                v.wait_ge(S("a_eq"), b + 1)
                if not (isinstance(b, int) and b == 0):
                    v.wait_ge(S("a_at"), b)
                v.scalar_tensor_tensor(out=a_qf, in0=a_eq, scalar=1.0, in1=a_rq, op0=ALU.min, op1=ALU.add)\
                    .then_inc(S("a_qf"), 1)

            def a_mask(b):
                v.wait_ge(S("a_kvmm"), b + 1)
                for k in range(KD):
                    g = ps[4][:, k * (P + 1):(k + 1) * (P + 1)]
                    v.tensor_tensor(a_kv[:, k, 0:P], g[:, 0:P], blk, ALU.mult)
                    last = v.tensor_scalar(a_kv[:, k, P:P + HPT], heads, g[:, P:P + 1], None, ALU.mult)
                last.then_inc(S("a_mask"), 1)

            def a_update(b):
                v.wait_ge(S("a_ymm"), b + 1)
                v.wait_ge(S("a_bias"), b + 1)
                for h in range(2):
                    c = CPB * b + 2 * h
                    xv = x[:, ds(c, 2) if not isinstance(b, int) else slice(c, c + 2), :]
                    last = v.tensor_tensor(xv, ps[6 + h][:, :].rearrange("p (c d) -> p c d", c=2), xv, ALU.add)
                last.then_inc(S("a_xadd"), 1)
                v.wait_ge(S("a_xadd"), b + 1)
                for c in range(CPB):
                    last = row_stats(CPB * b + c)
                last.then_inc(S("a_xupd"), 1)

            def attention(b, before, more):
                if more:
                    a_norm(b + 1)
                if before:
                    a_normalise(b - 1)
                a_kvbias(b)
                a_qfeature(b)
                a_kfeature(b)
                if before:
                    a_update(b - 1)
                a_mask(b)

            v.wait_ge(S("ld_x0"), 16)
            first_stats(0, CPB)
            a_norm(0)
            v.wait_ge(S("ld_x1"), 16 * (BATCH - 1))
            first_stats(CPB, NCH)
            v.wait_ge(S("ld_a"), 16 * 7)
            v.wait_ge(S("ld_cst"), 16)
            v.wait_ge(S("a_vone"), 1)
            attention(0, False, True)
            with v.Fori(1, BATCH - 1) as b:
                attention(b, True, True)
            attention(BATCH - 1, True, False)
            a_normalise(BATCH - 1)
            a_update(BATCH - 1)
            v.wait_ge(S("xs_zeroed"), 16)

            def feed(r, updated, n_updated):
                v.wait_ge(S(updated), n_updated)
                layer_norm_scales()
                for c in range(NCH):
                    last = ln_apply(f_xn[:, c, :], c)
                    if c % CPB == CPB - 1:
                        last.then_inc(S(f"f{r}_xn"), 1)
                ce = "p (c e) -> p c e"
                lg, eq, ex, oh, pm, cmp_ = [q.rearrange(ce, e=E) for q in (r_lg, r_eq, r_ex, r_oh, r_pm, r_cmp)]
                ec = "p (e c) -> p e c"
                tot, cum = r_tot.rearrange(ec, e=E), r_cum.rearrange(ec, e=E)
                v.wait_ge(S("ld_r"), 16 * 3)
                v.wait_ge(S(f"f{r}_lgmm"), BATCH)
                v_log = ps[7][:, 0:NCH * E].rearrange(ce, e=E)
                link(v.tensor_tensor(lg, v_log, br[:, :].unsqueeze(1).to_broadcast([P, NCH, E]), ALU.add))
                link(v.tensor_reduce(r_mx, lg, AX.X, ALU.max))
                top = r_mx.unsqueeze(2).to_broadcast([P, NCH, E])
                link(v.tensor_tensor(eq, lg, top, ALU.is_equal))
                v.tensor_tensor(lg, lg, top, ALU.subtract).then_inc(S(f"f{r}_lg"), 1)
                link(v.tensor_tensor(eq, eq, cst[:, C_DESC:C_DESC + E].unsqueeze(1).to_broadcast([P, NCH, E]), ALU.mult))
                link(v.tensor_reduce(r_m2, eq, AX.X, ALU.max))
                v.tensor_tensor(oh, eq, r_m2.unsqueeze(2).to_broadcast([P, NCH, E]), ALU.is_equal)\
                    .then_inc(S(f"f{r}_oh"), 1)
                v.wait_ge(S(f"f{r}_ex"), 1)
                link(v.tensor_reduce(r_se, ex, AX.X, ALU.add))
                link(v.reciprocal(pmax[:, :], r_se))
                v.wait_ge(S(f"f{r}_rank"), 1)
                link(v.tensor_copy(tot, ps[6][:, 0:NCH * E].rearrange("p (c e) -> p e c", e=E)))
                link(v.tensor_tensor_scan(out=r_cum, data0=cst[:, C_RST:C_RST + E * NCH], data1=r_tot, initial=0.0,
                                          op0=ALU.mult, op1=ALU.add))
                link(v.tensor_tensor(r_cmp.rearrange(ec, e=E), cum[:, :, NCH - 1:NCH].to_broadcast([P, E, NCH]),
                                     cst[:, C_THR:C_THR + NCH].unsqueeze(1).to_broadcast([P, E, NCH]), ALU.is_gt))
                link(v.tensor_reduce(r_tl, r_cmp.rearrange(ec, e=E), AX.X, ALU.add))
                link(v.tensor_tensor_scan(out=r_te, data0=ones[:, 0:E], data1=r_tl, initial=0.0,
                                          op0=ALU.mult, op1=ALU.add))
                v.tensor_tensor(r_ba, r_te, r_tl, ALU.subtract)
                link(v.tensor_tensor(cum, cum, tot, ALU.subtract))
                link(v.tensor_scalar(r_ba, r_ba, float(P), -1.0, ALU.mult, ALU.add))
                link(v.tensor_tensor(cum, cum, r_ba.unsqueeze(2).to_broadcast([P, E, NCH]), ALU.add))
                link(v.tensor_tensor(pm, ps[5][:, 0:NCH * E].rearrange(ce, e=E), r_cum.rearrange("p (e c) -> p c e", e=E),
                                     ALU.add))
                link(v.tensor_tensor(pm, pm, oh, ALU.mult))
                link(v.tensor_reduce(r_pf, pm, AX.X, ALU.add))
                v.tensor_copy(pos[:, :], r_pf)
                c2 = r_cmp2.rearrange("p (j e) -> p j e", e=E)
                link(v.tensor_tensor(c2, cst[:, C_IOTA:C_IOTA + 40].unsqueeze(2).to_broadcast([P, 40, E]),
                                     r_te.unsqueeze(1).to_broadcast([P, 40, E]), ALU.is_ge))
                link(v.tensor_reduce(r_te40, c2, AX.X, ALU.add))
                v.tensor_scalar(tile_e[:, :], r_te40, float(E - 1), None, ALU.min).then_inc(S(f"f{r}_pos"), 1)

                def hid(par, n):
                    v.wait_ge(S(f"f{r}_h{par}"), n + 1)
                    v.wait_ge(S(f"f{r}_ht{par}"), n)
                    v.tensor_copy(t_h[par], ps[2 + par][:, :]).then_inc(S(f"f{r}_hc{par}"), 1)

                def res(j, par, n):
                    e = v.value_load(tile_e[0:1, ds(j, 1)] if not isinstance(j, int) else tile_e[0:1, j:j + 1],
                                     min_val=0, max_val=E - 1)
                    v.wait_ge(S(f"f{r}_ymm{par}"), n + 1)
                    v.wait_ge(S(f"f{r}_st{par}"), 16 * n)
                    v.tensor_tensor(t_y[par], ps[6 + par][:, 0:D], b2[:, row(e), :].rearrange("p a d -> p (a d)"), ALU.add)\
                        .then_inc(S(f"f{r}_y{par}"), 1)

                H = TILES // 2
                v.wait_ge(S(f"ld_ffn{r}"), LD_FFN)
                v.wait_ge(S(f"f{r}_pos"), 1)
                hid(0, 0)

                def turn(i):
                    hid(1, i)
                    res(2 * i, 0, i)
                    hid(0, i + 1)
                    res(2 * i + 1, 1, i)

                turn(0)
                with v.Fori(1, H) as i:
                    turn(i)
                res(TILES - 1, 0, H)
                for b in range(BATCH):
                    v.wait_ge(S(f"f_g{b}"), 16 * CPB * (r + 1))
                    for c in range(CPB * b, CPB * b + CPB):
                        last = v.scalar_tensor_tensor(out=x[:, c, :], in0=f_gather[:, c, :], scalar=pmax[:, c:c + 1],
                                                      in1=x[:, c, :], op0=ALU.mult, op1=ALU.add)
                    if r == 0:
                        link(last)
                        for c in range(CPB * b, CPB * b + CPB):
                            last = row_stats(c)
                    last.then_inc(S(f"f{r}_xupd"), 1)

            feed(0, "a_xupd", BATCH)

            v.wait_ge(S("f0_xupd"), BATCH)
            v.wait_ge(S("m_zero"), 3)
            v.tensor_copy(stack[:, :], cst[0:4 * NS, C_STK:C_STK + 2 * NS]).then_inc(S("m_stack"), 1)
            layer_norm_scales()
            v.wait_ge(S("m_aexp"), 3)
            link(v.tensor_scalar(far[:, :], a_neg[:, :, :].rearrange("p k s -> p (k s)"), -5.0, None, ALU.is_lt))
            v.tensor_reduce(far_sum[:, :], far[:, :], AX.X, ALU.add).then_inc(S("m_far"), 1)
            v.wait_ge(S("m_farsum"), 1)
            link(v.tensor_copy(far_flag[:, :], ps[7][:, 0:1]))

            def m_norm(n):
                v.wait_ge(S("m_tr"), n)
                for c in range(CPB):
                    last = ln_apply(m_xn[:, c, :], CPB * n + c)
                last.then_inc(S("m_xn"), 1)

            def m_dtw(n, par):
                v.wait_ge(S("m_th"), KI * n + KI)
                v.tensor_scalar(m_dt[par], m_dt[par], 1.0, 0.5, ALU.add, ALU.mult).then_inc(S("m_dt0"), 1)
                v.wait_ge(S("m_dt0"), n + 1)
                v.tensor_scalar(m_dt[par], m_dt[par], 1e-4, 1.0, ALU.max, ALU.min).then_inc(S("m_dt1"), 1)
                v.wait_ge(S("m_dt1"), n + 1)
                v.tensor_tensor(m_w, m_dt[par], m_u[par], ALU.mult).then_inc(S("m_w"), 1)

            def m_bclo(n, par):
                v.wait_ge(S("m_bchi"), n + 1)
                v.tensor_tensor(m_bc[par][2 * NS:4 * NS, :], ps[0][0:2 * NS, :], m_bc[par][0:2 * NS, :].bitcast(F32),
                                ALU.subtract).then_inc(S("m_bclo"), 1)

            def m_gate(n, par, o):
                v.wait_ge(S("m_zth"), KI * n + o + 1)
                v.scalar_tensor_tensor(out=m_sz[par][:, o, :], in0=m_sz[par][:, o, :], scalar=1.0,
                                       in1=ps[(o + 1) % 2][:, :], op0=ALU.add, op1=ALU.mult).then_inc(S("m_sz"), 1)

            def m_final(b, par):
                v.wait_ge(S("m_nsum"), (NS // 2) * (b + 1))
                v.wait_ge(S("m_sz"), KI * (b + 1))
                for k in range(KI):
                    last = v.scalar_tensor_tensor(out=m_y[:, k, :], in0=m_u[par][:, k, :], scalar=mvec[:, 2, k:k + 1],
                                                  in1=ps[4 + k][:, :], op0=ALU.mult, op1=ALU.add)
                last.then_inc(S("m_y0"), 1)
                v.wait_ge(S("m_y0"), b + 1)
                v.scalar_tensor_tensor(out=m_y, in0=m_y, scalar=0.5, in1=m_sz[par], op0=ALU.mult, op1=ALU.mult)\
                    .then_inc(S("m_y"), 1)

            def m_update(b, h):
                v.wait_ge(S("m_omm"), 2 * b + h + 1)
                c = CPB * b + 2 * h
                xv = x[:, ds(c, 2) if not isinstance(c, int) else slice(c, c + 2), :]
                v.tensor_tensor(xv, ps[h][:, :].rearrange("p (c d) -> p c d", c=2), xv, ALU.add)\
                    .then_inc(S("m_xupd"), 1)
                if h == 0:
                    return
                v.wait_ge(S("m_xupd"), 2 * b + 2)
                for c in range(CPB):
                    last = row_stats(CPB * b + c)
                last.then_inc(S("m_stat"), 1)

            def m_db(b, par, st):
                n = NS * b + st
                v.wait_ge(S("m_bb"), n + 1)
                if st >= 4:
                    v.wait_ge(S("m_q"), (NS // 2) * b + (st - 4) // 2 + 1)
                elif not (isinstance(b, int) and b == 0):
                    v.wait_ge(S("m_q"), (NS // 2) * b - 2 + st // 2 + 1)
                v.tensor_tensor(m_b[st % 4], m_w, ps[2][:, :].unsqueeze(1).to_broadcast([P, KI, SEQ]), ALU.mult)\
                    .then_inc(S("m_db"), 1)

            def m_scan(b, par, before, more, clip):
                if more:
                    m_norm(b + 1)
                v.wait_ge(S("m_w"), b + 1)
                m_db(b, par, 0)
                for st in range(NS):
                    n = NS * b + st
                    v.wait_ge(S("m_exp"), n + 1)
                    if clip:
                        v.tensor_scalar(m_a[st % 2][:, :, 1:], m_a[st % 2][:, :, 1:], 0.006737946999085467,
                                        148.4131591025766, ALU.max, ALU.min).then_inc(S("m_clip"), 1)
                    if st + 1 < NS:
                        m_db(b, par, st + 1)
                    if clip:
                        v.wait_ge(S("m_clip"), n + 1)
                    v.wait_ge(S("m_eps"), n + 1)
                    bt = m_b[st % 4].rearrange("p k t -> p (k t)")
                    v.tensor_tensor_scan(out=bt, data0=m_a[st % 2].rearrange("p k t -> p (k t)"), data1=bt,
                                         initial=0.0, op0=ALU.mult, op1=ALU.add).then_inc(S("m_scan"), 1)
                    if st not in POOL_C:
                        v.wait_ge(S("m_scan"), n + 1)
                        v.wait_ge(S("m_cb"), n + 1)
                        v.tensor_tensor(m_b[st % 4], m_b[st % 4], ps[3][:, :].unsqueeze(1).to_broadcast([P, KI, SEQ]),
                                        ALU.mult).then_inc(S("m_c"), 1)
                    if before and st == 1:
                        m_final(b - 1, 1 - par)
                    if before and st in (4, 5):
                        m_update(b - 1, st - 4)
                    if more and st == 13:
                        m_bclo(b + 1, 1 - par)
                        m_gate(b + 1, 1 - par, 0)
                    if more and st == 14:
                        m_gate(b + 1, 1 - par, 1)
                        m_dtw(b + 1, 1 - par)
                    if more and st == 15:
                        m_gate(b + 1, 1 - par, 2)
                        m_gate(b + 1, 1 - par, 3)

            def m_all(clip):
                m_scan(0, 0, False, True, clip)
                with v.Fori(0, (BATCH - 2) // 2) as i:
                    m_scan(2 * i + 1, 1, True, True, clip)
                    m_scan(2 * i + 2, 0, True, True, clip)
                m_scan(BATCH - 1, 1, True, False, clip)

            m_norm(0)
            m_bclo(0, 0)
            m_gate(0, 0, 0)
            m_gate(0, 0, 1)
            m_dtw(0, 0)
            m_gate(0, 0, 2)
            m_gate(0, 0, 3)
            binds = v.value_load(far_flag[0:1, 0:1], min_val=0, max_val=P * KI * NS)
            with v.If(binds > 0):
                m_all(True)
            with v.Else():
                m_all(False)
            m_final(BATCH - 1, 1)
            m_update(BATCH - 1, 0)
            m_update(BATCH - 1, 1)
            feed(1, "m_stat", BATCH)

        @block.tensor
        def _(t):
            def turned(bank, src, k, n):
                return t.transpose(bank, src[:, k * P:(k + 1) * P], ident)

            def a_turn(b):
                t.wait_ge(S("a_xn"), b + 1)
                if not (isinstance(b, int) and b == 0):
                    t.wait_ge(S("a_xt"), b)
                for k in range(KD):
                    for c in range(CPB):
                        last = turned(ps[k][:, c * P:(c + 1) * P], a_xn[:, c, :], k, c)
                last.then_inc(S("a_tr"), 1)

            def a_query(b):
                t.wait_ge(S("a_xt"), b + 1)
                for m in range(KD):
                    for k in range(KD):
                        last = t.matmul(ps[2 + m][:, :], wqkv[:, k, m * P:(m + 1) * P], a_xt[:, k, :],
                                        start=(k == 0), stop=(k == KD - 1))
                last.then_inc(S("a_q"), 1)

            def a_keyvalue(b):
                for c in range(CPB):
                    if c >= 2:
                        t.wait_ge(S("a_kb"), CPB * b + c - 1)
                    for k in range(KD):
                        last = t.matmul(ps[4 + c % 2][:, :], a_xt[:, k, c * P:(c + 1) * P], wqkv[:, k, D:3 * D],
                                        start=(k == 0), stop=(k == KD - 1))
                    last.then_inc(S("a_kvp"), 1)

            def a_attend(b):
                t.wait_ge(S("a_qf"), b + 1)
                t.wait_ge(S("a_mask"), b + 1)
                if not (isinstance(b, int) and b == 0):
                    t.wait_ge(S("a_xadd"), b)
                for bank, u0, n in AT_BANKS:
                    for u in range(u0, u0 + n):
                        c, k = u // KD, u % KD
                        at = (u - u0) * (P + HPT)
                        last = t.matmul(ps[bank][:, at:at + P + HPT], a_qf[:, k, c * P:(c + 1) * P], a_kv[:, k, :],
                                        start=True, stop=True)
                last.then_inc(S("a_at"), 1)

            def a_kvmm(b):
                t.wait_ge(S("a_kf"), b + 1)
                for k in range(KD):
                    for c in range(CPB):
                        last = t.matmul(ps[4][:, k * (P + 1):(k + 1) * (P + 1)], a_k[:, c, k * P:(k + 1) * P],
                                        a_v[:, c, k, :], start=(c == 0), stop=(c == CPB - 1))
                last.then_inc(S("a_kvmm"), 1)

            def a_oturn(b, newest_q):
                t.wait_ge(S("a_o"), b + 1)
                t.wait_ge(S("a_eq"), newest_q + 1)
                for k in range(KD):
                    for c in range(CPB):
                        last = turned(ps[2 + k][:, c * P:(c + 1) * P], a_o[:, c, :], k, c)
                last.then_inc(S("a_otr"), 1)

            def a_out(b):
                t.wait_ge(S("a_ot"), b + 1)
                for c in range(CPB):
                    for k in range(KD):
                        last = t.matmul(ps[6 + c // 2][:, (c % 2) * D:(c % 2) * D + D], a_ot[:, k, c * P:(c + 1) * P],
                                        wo[:, k, :], start=(k == 0), stop=(k == KD - 1))
                last.then_inc(S("a_ymm"), 1)

            def attention(b, before, more):
                a_query(b)
                if before:
                    a_attend(b - 1)
                a_keyvalue(b)
                if before:
                    a_oturn(b - 1, b)
                    a_out(b - 1)
                if more:
                    a_turn(b + 1)
                a_kvmm(b)

            t.wait_ge(S("ld_cst"), 16)
            a_turn(0)
            t.wait_ge(S("ld_a"), 16 * 7)
            t.wait_ge(S("a_vone"), 1)
            attention(0, False, True)
            with t.Fori(1, BATCH - 1) as b:
                attention(b, True, True)
            attention(BATCH - 1, True, False)
            a_attend(BATCH - 1)
            a_oturn(BATCH - 1, BATCH - 1)
            a_out(BATCH - 1)

            def feed(r):
                t.wait_ge(S("ld_r"), 16 * 3)
                if r == 0:
                    t.wait_ge(S("a_xupd"), BATCH)
                else:
                    t.wait_ge(S("m_stat"), BATCH)
                for b in range(BATCH):
                    t.wait_ge(S(f"f{r}_xn"), b + 1)
                    if b >= 2:
                        t.wait_ge(S(f"f{r}_xt"), b - 1)
                    for k in range(KD):
                        for c in range(CPB):
                            last = turned(ps[2 * (b % 2) + k][:, c * P:(c + 1) * P], f_xn[:, CPB * b + c, :], k, c)
                    last.then_inc(S(f"f{r}_tr"), 1)
                    if b:
                        logits(r, b - 1)
                logits(r, BATCH - 1)
                t.wait_ge(S(f"f{r}_oh"), 1)
                t.matmul(ps[5][:, 0:NCH * E], tri, r_oh, start=True, stop=True)
                t.matmul(ps[6][:, 0:NCH * E], ones, r_oh, start=True, stop=True).then_inc(S(f"f{r}_rank"), 1)
                if r == 0:
                    t.wait_ge(S("ld_ipw"), 16)
                    for k in range(TAPS):
                        t.wait_ge(S(f"ld_cw{k}"), 16)
                        for d in range(KD):
                            n = KD * k + d
                            if n >= 2:
                                t.wait_ge(S("tapw"), n - 1)
                            for c in range(KI):
                                last = t.matmul(ps[n % 2][:, :], ipw[:, c, d * P:(d + 1) * P], cw[:, c, :],
                                                start=(c == 0), stop=(c == KI - 1))
                            last.then_inc(S("tap_mm"), 1)
                    t.wait_ge(S("tapw"), TAPS * KD)

                def tr(par, n):
                    t.wait_ge(S(f"f{r}_x{par}"), 16 * (n + 1))
                    t.wait_ge(S(f"f{r}_xt{par}"), n)
                    for k in range(KD):
                        last = turned(ps[par][:, k * P:(k + 1) * P], t_x[par], k, 0)
                    last.then_inc(S(f"f{r}_tr{par}"), 1)

                def expert(j):
                    return t.value_load(tile_e[0:1, ds(j, 1)] if not isinstance(j, int) else tile_e[0:1, j:j + 1],
                                        min_val=0, max_val=E - 1)

                def first(j, par, n):
                    e = expert(j)
                    t.wait_ge(S(f"f{r}_xt{par}"), n + 1)
                    t.wait_ge(S(f"f{r}_hc{par}"), n)
                    for k in range(KD):
                        last = t.matmul(ps[2 + par][:, :], t_xt[par][:, k, :],
                                        w1[:, row(e), k, :].rearrange("p a h -> p (a h)"),
                                        start=(k == 0), stop=(k == KD - 1))
                    last.then_inc(S(f"f{r}_h{par}"), 1)

                def turn_hidden(par, n):
                    t.wait_ge(S(f"f{r}_hc{par}"), n + 1)
                    t.wait_ge(S(f"f{r}_relu{par}"), n)
                    for k in range(KH):
                        last = turned(ps[4 + par][:, k * P:(k + 1) * P], t_h[par], k, 0)
                    last.then_inc(S(f"f{r}_ht{par}"), 1)

                def second(j, par, n):
                    e = expert(j)
                    t.wait_ge(S(f"f{r}_relu{par}"), n + 1)
                    t.wait_ge(S(f"f{r}_y{par}"), n)
                    for k in range(KH):
                        last = t.matmul(ps[6 + par][:, 0:D], t_ht[par][:, k, :],
                                        w2[:, row(e), k, :].rearrange("p a h -> p (a h)"),
                                        start=(k == 0), stop=(k == KH - 1))
                    last.then_inc(S(f"f{r}_ymm{par}"), 1)

                H = TILES // 2
                t.wait_ge(S(f"ld_ffn{r}"), LD_FFN)
                t.wait_ge(S(f"f{r}_pos"), 1)
                tr(0, 0)
                tr(1, 0)
                first(0, 0, 0)

                def turn(i, more):
                    turn_hidden(0, i)
                    first(2 * i + 1, 1, i)
                    tr(0, i + 1)
                    second(2 * i, 0, i)
                    turn_hidden(1, i)
                    first(2 * i + 2, 0, i + 1)
                    if more:
                        tr(1, i + 1)
                    second(2 * i + 1, 1, i)

                turn(0, True)
                with t.Fori(1, H - 1) as i:
                    turn(i, True)
                turn(H - 1, False)
                turn_hidden(0, H)
                second(TILES - 1, 0, H)

            def logits(r, b):
                t.wait_ge(S(f"f{r}_xt"), b + 1)
                for c in range(CPB):
                    j = (CPB * b + c) * E
                    for k in range(KD):
                        last = t.matmul(ps[7][:, j:j + E], f_xt[b % 2][:, k, c * P:(c + 1) * P], wr[:, k, :],
                                        start=(k == 0), stop=(k == KD - 1))
                last.then_inc(S(f"f{r}_lgmm"), 1)

            feed(0)

            def m_turn(n):
                t.wait_ge(S("m_xn"), n + 1)
                t.wait_ge(S("m_sz"), KI * n)
                for k in range(KD):
                    for c in range(CPB):
                        last = turned(ps[k][:, c * P:(c + 1) * P], m_xn[:, c, :], k, c)
                last.then_inc(S("m_tr"), 1)

            def m_conv(n, o, h):
                if h == 0:
                    t.wait_ge(S("m_xt"), n + 1)
                    if o >= 2:
                        t.wait_ge(S("m_u"), KI * n + o - 1)
                        if not (isinstance(n, int) and n < 2):
                            t.wait_ge(S("m_xupd"), 2 * (n - 1) + o - 3)
                for k in range(2 * h, 2 * h + 2):
                    for d in range(KD):
                        last = t.matmul(ps[o % 2][:, :], tapw[:, k, d, o * P:(o + 1) * P], m_xt[:, d, k:k + SEQ],
                                        start=(k == 0 and d == 0), stop=(k == TAPS - 1 and d == KD - 1))
                if h:
                    last.then_inc(S("m_umm"), 1)

            def m_dtmm(n, o):
                t.wait_ge(S("m_u"), KI * n + KI)
                if o >= 2:
                    t.wait_ge(S("m_th"), KI * n + o - 1)
                for k in range(KI):
                    last = t.matmul(ps[o % 2][:, :], dtw[:, k, o * P:(o + 1) * P], m_u[m_par[0]][:, k, :],
                                    start=(k == 0), stop=(k == KI - 1))
                last.then_inc(S("m_dmm"), 1)

            def m_bcmm(n):
                t.wait_ge(S("m_th"), KI * n + 3)
                for k in range(KI):
                    last = t.matmul(ps[0][0:2 * NS, :], bcw[:, k, :], m_u[m_par[0]][:, k, :],
                                    start=(k == 0), stop=(k == KI - 1))
                last.then_inc(S("m_bcmm"), 1)

            def m_zmm(n, o):
                if o == 0:
                    t.wait_ge(S("m_th"), KI * n + KI)
                if o == 1:
                    t.wait_ge(S("m_bclo"), n + 1)
                if o >= 2:
                    t.wait_ge(S("m_sz"), KI * n + o - 1)
                for k in range(KD):
                    last = t.matmul(ps[(o + 1) % 2][:, :], zw[:, k, o * P:(o + 1) * P], m_xt[:, k, PAD:],
                                    start=(k == 0), stop=(k == KD - 1))
                last.then_inc(S("m_zmm"), 1)

            def m_out(b, h, more):
                t.wait_ge(S("m_y"), b + 1)
                if more:
                    t.wait_ge(S("m_u"), KI * (b + 2) + h + 1)
                elif b < BATCH - 1:
                    t.wait_ge(S("m_sz"), KI * BATCH)
                else:
                    t.wait_ge(S("m_xupd"), 2 * b)
                for c in (2 * h, 2 * h + 1):
                    for k in range(KI):
                        last = t.matmul(ps[h][:, (c % 2) * D:(c % 2) * D + D], m_y[:, k, c * P:(c + 1) * P],
                                        outw[:, k, :], start=(k == 0), stop=(k == KI - 1))
                last.then_inc(S("m_omm"), 1)

            def m_pre(n, q):
                if q == 0:
                    m_turn(n)
                if q in CONV_AT:
                    i = CONV_AT.index(q)
                    m_conv(n, i // 2, i % 2)
                if q in DT_AT:
                    m_dtmm(n, DT_AT.index(q))
                if q == BC_AT:
                    m_bcmm(n)
                if q in Z_AT:
                    m_zmm(n, Z_AT.index(q))

            m_par = [0]

            def spread_b(b, par, st):
                t.wait_ge(S("m_db"), NS * b + st)
                t.matmul(ps[2][:, :], stack[:, st:st + 1].to_broadcast([4 * NS, P]), m_bc[par][:, :],
                         start=True, stop=True).then_inc(S("m_bb"), 1)

            def spread_c(b, par, st):
                t.wait_ge(S("m_c"), NVC * b + st - pool_c(st))
                t.wait_ge(S("m_cs"), NPC * b + pool_c(st))
                t.matmul(ps[3][:, :], stack[:, NS + st:NS + st + 1].to_broadcast([4 * NS, P]), m_bc[par][:, :],
                         start=True, stop=True).then_inc(S("m_cb"), 1)

            def m_nsum(b, p):
                t.wait_ge(S("m_q"), (NS // 2) * b + p + 1)
                if p == 0:
                    t.wait_ge(S("m_y0"), b)
                for k in range(KI):
                    last = t.matmul(ps[4 + k][:, :], ident, m_q[:, k, :], start=(p == 0), stop=(p == NS // 2 - 1))
                last.then_inc(S("m_nsum"), 1)

            def m_scan(b, par, before, more):
                t.wait_ge(S("m_bclo"), b + 1)
                spread_b(b, par, 0)
                spread_c(b, par, 0)
                spread_b(b, par, 1)
                m_par[0] = 1 - par
                for q in range(2 * NS):
                    st = q // 2
                    if q % 2 == 1 and st < NS - 2:
                        spread_b(b, par, st + 2)
                    if q % 2 == 0 and st:
                        spread_c(b, par, st)
                    if before and q == 1:
                        m_nsum(b - 1, NS // 2 - 1)
                    if before and q in OUT_AT:
                        m_out(b - 1, OUT_AT.index(q), more)
                    if more:
                        m_pre(b + 1, q)
                    if q % 4 == 2 and q >= 6:
                        m_nsum(b, (q - 6) // 4)

            t.wait_ge(S("m_far"), 1)
            t.matmul(ps[7][:, 0:1], ones, far_sum[:, :], start=True, stop=True).then_inc(S("m_farsum"), 1)
            t.wait_ge(S("m_stack"), 1)
            for q in range(2 * NS):
                m_pre(0, q)
            m_scan(0, 0, False, True)
            with t.Fori(0, (BATCH - 2) // 2) as i:
                m_scan(2 * i + 1, 1, True, True)
                m_scan(2 * i + 2, 0, True, True)
            m_scan(BATCH - 1, 1, True, False)
            m_nsum(BATCH - 1, NS // 2 - 1)
            m_out(BATCH - 1, 0, False)
            m_out(BATCH - 1, 1, False)
            feed(1)


def kernel(**inputs):
    import numpy as np
    import concourse.bacc as bacc
    from concourse import mybir as mb
    from concourse.bass_utils import run_bass_kernel_spmd as run

    def a(name):
        return np.asarray(inputs[name])

    def cols(v):
        return v.reshape(-1, P).T

    cst = np.zeros((P, C_ALL), np.float32)
    i = np.arange(P)
    cst[:, C_ID:C_ID + P] = i[:, None] == i
    cst[:, C_TRI:C_TRI + P] = i[:, None] <= i
    cst[:, C_ONE:C_ONE + P] = 1
    cst[:, C_BLK:C_BLK + P] = i[:, None] // HEAD == i // HEAD
    cst[:, C_RST:C_RST + E * NCH] = np.arange(E * NCH) % NCH != 0
    cst[:, C_THR:C_THR + NCH] = np.arange(NCH) * P
    cst[:, C_DESC:C_DESC + E] = E - np.arange(E)
    cst[:, C_IOTA:C_IOTA + 40] = np.arange(40)
    cst[:, C_STK:C_STK + 32] = i[:, None] % 32 == np.arange(32)
    B = "L0_attn_b_"
    arrays = {
        "cst": cst,
        "x": a("L0_attn_a_inputs_q"),
        "Wq": a("L0_attn_a_Wq"), "Wk": a("L0_attn_a_Wk"), "Wv": a("L0_attn_a_Wv"), "Wo": a("L0_attn_a_Wo"),
        "bq": cols(a("L0_attn_a_bq")),
        "bkv": np.concatenate([a("L0_attn_a_bk"), a("L0_attn_a_bv")]),
        "bo": a("L0_attn_a_bo"),
        "Wr": a("L0_ffn_Wr"), "br": a("L0_ffn_br"), "W1": a("L0_ffn_W1"), "W2": a("L0_ffn_W2"),
        "b1": a("L0_ffn_b1").reshape(E, KH, P).transpose(2, 0, 1),
        "b2": a("L0_ffn_b2"),
        "ip_x": a(B + "in_proj_w")[0:DI],
        "zw": a(B + "in_proj_w")[DI:2 * DI].T,
        "conv": a(B + "conv_w").transpose(2, 1, 0),
        "dtw": a(B + "dt_w").T,
        "bcw": np.concatenate([a(B + "B_w"), a(B + "C_w")]).T,
        "outw": a(B + "out_w").T,
        "A_log": a(B + "A_log").reshape(KI, P, NS).transpose(1, 0, 2),
        "mvec": np.stack([cols(a(B + "conv_b")), cols(a(B + "dt_b")), cols(a(B + "D"))], 1),
    }
    nc = bacc.Bacc("TRN2", target_bir_lowering=False, num_devices=1)
    T, feed = {}, {}
    for name, v in arrays.items():
        v = np.ascontiguousarray(v)
        feed[f"in_{name}"] = v
        T[name] = nc.dram_tensor(f"in_{name}", v.shape, mb.dt.from_np(v.dtype), kind="ExternalInput").ap()
    T["out"] = nc.dram_tensor("out_x", (BATCH, SEQ, D), mb.dt.float32, kind="ExternalOutput").ap()
    build(nc, T)
    r = run(nc, [feed], core_ids=[0])
    return r.results[0]["out_x"]
```

```python
from contextlib import ExitStack

import concourse.bass as bass
from concourse import mybir

P = 128
BATCH, SEQ, D = 8, 512, 256
TOK = BATCH * SEQ
NCH = TOK // P
CPB = SEQ // P
KD = D // P
HEAD = 16
HPT = P // HEAD
E, HID = 8, 512
KH = HID // P
DI, NS, TAPS = 512, 16, 4
KI = DI // P
TILES = NCH + E - 1
TURNS = TILES // 2
XB = 8
XT = XB // 2
PAD = TAPS - 1
LN_EPS, NORM_EPS = 1e-5, 1e-6

F32 = mybir.dt.float32
F32R = mybir.dt.float32r
I32 = mybir.dt.int32
U32 = mybir.dt.uint32
ALU = mybir.AluOpType
ACT = mybir.ActivationFunctionType
AX = mybir.AxisListType
ds = bass.DynSlice

TURN_AT = 1
CONV_AT = (3, 4, 6, 7, 11, 12, 15, 16)
OUT_AT = (8, 10)
DT_AT = (19, 22, 23, 24)
BC_AT = 26
Z_AT = (14, 18, 27, 30)
XT_AT = 1
U_AT = (3, 4, 7, 9)
TH_AT = (10, 11, 12, 13)
BCHI_AT = 14
ZTH_AT = (8, 10, 15)
GATE_AT = (8, 10, 15)
Z_BANK = (1, 1, 1, 0)
U_BANK = (0, 1, 0, 0)

POOL_C = (0, 2, 4, 6, 8, 10, 12, 14)
NPC, NVC = len(POOL_C), NS - len(POOL_C)


def pool_c(st):
    return sum(s < st for s in POOL_C)


AT_BANKS = ((6, 0, 3), (7, 3, 3), (1, 6, 2))

C_ID, C_TRI, C_ONE, C_BLK = 0, P, 2 * P, 3 * P
C_RST = 4 * P
C_THR = C_RST + E * NCH
C_DESC = C_THR + NCH
C_IOTA = C_DESC + E
C_STK = C_IOTA + 40
C_TOK = C_STK + 32
C_ALL = C_TOK + NCH

X_MEAN, X_RSTD, X_PMAX, X_TOK = D, D + 1, D + 2, D + 3
XW = D + 4


def build(nc, T):
    with ExitStack() as ctx:
        sems = {}

        def S(name):
            if name not in sems:
                sems[name] = ctx.enter_context(nc.semaphore(name))
            return sems[name]

        def sb(name, shape, dt=F32):
            return ctx.enter_context(nc.sbuf_tensor(name, shape, dt))

        x_all = sb("x", [P, NCH, XW])
        x = x_all[:, :, 0:D]
        mean, rstd, pmax = [x_all[:, :, i] for i in (X_MEAN, X_RSTD, X_PMAX)]
        cst = sb("cst", [P, C_ALL])
        stats = sb("stats", [P, NCH, 6])
        nw = [sb(f"nw{i}", [P, NCH]) for i in range(4)]
        ident = cst[:, C_ID:C_ID + P]
        tri, ones = cst[:, C_TRI:C_TRI + P], cst[:, C_ONE:C_ONE + P]
        blk = cst[:, C_BLK:C_BLK + P]
        heads = cst[:, C_BLK:C_BLK + P].rearrange("p (h m) -> p h m", h=HPT)[:, :, 0]
        tapw = sb("tapw", [P, TAPS, KD, DI])
        zw = sb("zw", [P, KD, DI])
        dtw = sb("dtw", [P, KI, DI])
        bcw = sb("bcw", [P, KI, 2 * NS])
        outw = sb("outw", [P, KI, D])
        a_neg = sb("a_neg", [P, KI, NS])
        mvec = sb("mvec", [P, 3, KI])
        far = sb("far", [P, KI * NS])
        far_sum = sb("far_sum", [P, 1])
        far_flag = sb("far_flag", [P, 1], I32)
        stack = sb("stack", [2 * 2 * NS, 2 * NS], F32R)
        wr = sb("wr", [P, KD, E])
        br = sb("br", [P, E])
        b1t = sb("b1t", [P, E, KH])
        pos = sb("pos", [P, NCH], U32)
        tile_e = sb("tile_e", [P, 40], I32)
        AR = 33900
        arena = sb("arena", [P, AR])

        class Space:

            def __init__(self, at):
                self.at = at

            def take(self, n):
                v = arena[:, self.at:self.at + n]
                self.at += n
                assert self.at <= AR, self.at
                return v

        fs = Space(0)
        w1 = fs.take(E * KD * HID).rearrange("p (e k h) -> p e k h", e=E, k=KD)
        w2 = fs.take(E * KH * D).rearrange("p (e k d) -> p e k d", e=E, k=KH)
        b2 = fs.take(E * D).rearrange("p (e d) -> p e d", e=E)
        FEED = fs.at

        s = Space(FEED)
        wqkv = s.take(KD * 3 * D).rearrange("p (k n) -> p k n", k=KD)
        wo = s.take(KD * D).rearrange("p (k n) -> p k n", k=KD)
        bkv = s.take(2 * D)
        bo = s.take(D)
        bq = s.take(KD)
        a_xn = s.take(CPB * D).rearrange("p (c d) -> p c d", c=CPB)
        a_xt = s.take(KD * SEQ).rearrange("p (k t) -> p k t", k=KD)
        a_eq = s.take(KD * SEQ).rearrange("p (k t) -> p k t", k=KD)
        a_rq = s.take(KD * SEQ).rearrange("p (k t) -> p k t", k=KD)
        a_qf = s.take(KD * SEQ).rearrange("p (k t) -> p k t", k=KD)
        a_k = s.take(CPB * D).rearrange("p (c d) -> p c d", c=CPB)
        a_ek = s.take(CPB * D).rearrange("p (c d) -> p c d", c=CPB)
        a_v = s.take(CPB * KD * (P + 1)).rearrange("p (c k n) -> p c k n", c=CPB, k=KD)
        a_kv = s.take(KD * (P + HPT)).rearrange("p (k n) -> p k n", k=KD)
        a_nr = s.take(CPB * KD * HPT)
        a_o = s.take(CPB * D).rearrange("p (c d) -> p c d", c=CPB)
        a_ot = s.take(KD * SEQ).rearrange("p (k t) -> p k t", k=KD)
        pad = s.take(XW)

        s = Space(FEED)
        f_xn = [s.take(CPB * D).rearrange("p (c d) -> p c d", c=CPB) for _ in range(2)]
        tail = s.at
        f_xt = [s.take(KD * SEQ).rearrange("p (k t) -> p k t", k=KD) for _ in range(2)]
        r_lg, r_eq, r_ex, r_oh, r_pm, r_tot, r_cum, r_cmp = [s.take(NCH * E) for _ in range(8)]
        r_mx, r_se, r_m2, r_pf = [s.take(NCH) for _ in range(4)]
        r_tl, r_te, r_ba = [s.take(E) for _ in range(3)]
        assert s.at <= AR - KI * (DI + D)
        s = Space(tail)
        r_cmp2, r_te40 = s.take(40 * E), s.take(40)
        s = Space(tail)
        t_x = [s.take(XW) for _ in range(XB)]
        t_n = [s.take(D) for _ in range(2)]
        t_xt = [s.take(KD * P).rearrange("p (k t) -> p k t", k=KD) for _ in range(2)]
        t_h = [s.take(HID) for _ in range(2)]
        t_ht = [s.take(HID).rearrange("p (k t) -> p k t", k=KH) for _ in range(2)]
        t_y = [s.take(D) for _ in range(2)]
        s = Space(AR - KI * (DI + D))
        cw = s.take(KI * DI).rearrange("p (k n) -> p k n", k=KI)
        ipw = s.take(KI * D).rearrange("p (k n) -> p k n", k=KI)

        s = Space(0)
        m_u, m_dt, m_sz = [[s.take(KI * SEQ).rearrange("p (k t) -> p k t", k=KI) for _ in range(2)]
                           for _ in range(3)]
        m_w = s.take(KI * SEQ).rearrange("p (k t) -> p k t", k=KI)
        m_xn = s.take(CPB * D).rearrange("p (c d) -> p c d", c=CPB)
        m_xt = s.take(KD * (SEQ + PAD)).rearrange("p (k t) -> p k t", k=KD)
        m_a = [s.take(KI * SEQ).rearrange("p (k t) -> p k t", k=KI) for _ in range(2)]
        m_b = [s.take(KI * SEQ).rearrange("p (k t) -> p k t", k=KI) for _ in range(4)]
        m_q = s.take(KI * SEQ).rearrange("p (k t) -> p k t", k=KI)
        m_y = s.take(KI * SEQ).rearrange("p (k t) -> p k t", k=KI)
        m_c = [s.take(SEQ) for _ in range(2)]
        m_bc = [sb(f"m_bc{i}", [4 * NS, SEQ], F32R) for i in range(2)]

        ps = [ctx.enter_context(nc.psum_tensor(f"ps{i}", [P, 512], F32)) for i in range(8)]

        xs = [nc.dram_tensor(f"sorted_rows{r}", (TILES * P, XW), F32, kind="Internal").ap() for r in range(2)]
        x_mid = nc.dram_tensor("residual", (TOK, D), F32, kind="Internal").ap()

        block = ctx.enter_context(nc.Block())

        def row(c):
            return ds(c, 1) if not isinstance(c, int) else slice(c, c + 1)

        def load_ffn(eng, r):
            for e in range(E):
                eng.dma_start(w1[:, e], T["W1"][e].rearrange("(k p) h -> p k h", p=P)).then_inc(S(f"ld_ffn{r}"), 16)
                eng.dma_start(w2[:, e], T["W2"][e].rearrange("(k p) d -> p k d", p=P)).then_inc(S(f"ld_ffn{r}"), 16)
            eng.dma_start(b2, T["b2"].partition_broadcast(P)).then_inc(S(f"ld_ffn{r}"), 16)

        LD_FFN = 16 * (2 * E + 1)

        @block.sync
        def _(sp):
            xin = T["x"].rearrange("b (c p) d -> p b c d", p=P)
            for b in range(BATCH):
                if b == 1:
                    sp.dma_start(cst[:, :], T["cst"]).then_inc(S("ld_cst"), 16)
                sp.dma_start(x[:, b * CPB:(b + 1) * CPB, :], xin[:, b]).then_inc(S(f"ld_x{min(b, 1)}"), 16)
            sp.wait_ge(S("ld_x1"), 16 * (BATCH - 1))
            load_ffn(sp, 0)
            sp.wait_ge(S("a_xupd"), BATCH)
            sp.wait_ge(S("xs_padded"), 32)
            sp.dma_start(ipw, T["ip_x"].rearrange("(k p) d -> p k d", p=P)).then_inc(S("ld_ipw"), 16)
            for k in range(TAPS):
                if k:
                    sp.wait_ge(S("tap_mm"), KD * k)
                sp.dma_start(cw, T["conv"][k].rearrange("(k p) d -> p k d", p=P)).then_inc(S(f"ld_cw{k}"), 16)

            def tiles_loop(r):
                def at(j):
                    return xs[r][j * P:(j + 1) * P] if isinstance(j, int) else xs[r][ds(j * P, P)]

                def load(k, kmod, par):
                    if not (isinstance(k, int) and k < XT):
                        sp.wait_ge(S(f"f{r}_st{par}"), 16 * (k - XT + 1))
                    sp.dma_start(t_x[2 * kmod + par], at(2 * k + par)).then_inc(S(f"f_x{2 * kmod + par}"), 16)

                sp.wait_ge(S(f"f{r}_scat"), 16 * NCH)
                for k in range(XT):
                    load(k, k, 0)
                    load(k, k, 1)
                whole = TURNS // XT
                with sp.Fori(1, whole) as i:
                    for m in range(XT):
                        load(XT * i + m, m, 0)
                        load(XT * i + m, m, 1)
                for k in range(XT * whole, TURNS + 1):
                    load(k, k % XT, 0)
                    if k < TURNS:
                        load(k, k % XT, 1)

            tiles_loop(0)
            sp.wait_ge(S("f0_st0"), 16 * (TURNS + 1))
            sp.wait_ge(S("f0_st1"), 16 * TURNS)
            for b in range(BATCH):
                sp.dma_start(x[:, b * CPB:(b + 1) * CPB, :],
                             x_mid[b * SEQ:(b + 1) * SEQ].rearrange("(c p) d -> p c d", p=P))\
                    .then_inc(S(f"ld_mid{min(b, 1)}"), 16)
            sp.wait_ge(S("m_xupd"), 2 * BATCH)
            load_ffn(sp, 1)
            tiles_loop(1)
            sp.wait_ge(S("f1_st0"), 16 * (TURNS + 1))
            sp.wait_ge(S("f1_st1"), 16 * TURNS)

        @block.gpsimd
        def _(g):
            g.memset(a_v[:, :, :, P:P + 1], 1.0).then_inc(S("a_vone"), 1)
            g.memset(pad, 0.0).then_inc(S("zero"), 1)
            g.wait_ge(S("zero"), 1)
            g.wait_ge(S("ld_cst"), 16)
            g.tensor_copy(x_all[:, :, X_TOK:X_TOK + 1].bitcast(U32), cst[:, C_TOK:C_TOK + NCH].unsqueeze(2))\
                .then_inc(S("tok"), 1)
            g.tensor_scalar(pad[:, X_TOK:X_TOK + 1].bitcast(U32), pad[:, X_TOK:X_TOK + 1], float(TOK), None, ALU.add)\
                .then_inc(S("tok"), 1)
            g.wait_ge(S("tok"), 2)
            g.wait_ge(S("ld_x1"), 16 * (BATCH - 1))
            for r in range(2):
                g.dma_start(xs[r].rearrange("(n p) d -> p n d", p=P), pad.unsqueeze(1).to_broadcast([P, TILES, XW]))\
                    .then_inc(S("xs_padded"), 16)

            def a_bias(b):
                g.wait_ge(S("a_xn"), b + 1)
                xv = x[:, ds(CPB * b, CPB) if not isinstance(b, int) else slice(CPB * b, CPB * b + CPB), :]
                g.tensor_tensor(xv, xv, bo.unsqueeze(1).to_broadcast([P, CPB, D]), ALU.add).then_inc(S("a_bias"), 1)

            g.wait_ge(S("ld_a"), 16 * 7)
            a_bias(0)
            with g.Fori(1, BATCH) as b:
                a_bias(b)

            def scatter(r):
                g.wait_ge(S(f"f{r}_pos"), 1)
                g.wait_ge(S("xs_padded"), 32)
                for c in range(NCH):
                    g.indirect_dma_start(out=xs[r], out_offset=bass.IndirectOffsetOnAxis(ap=pos[:, c:c + 1], axis=0),
                                         in_=x_all[:, c, :], in_offset=None).then_inc(S(f"f{r}_scat"), 16)

            def send_tiles(r):
                for j in range(TILES):
                    k, par = j // 2, j % 2
                    g.wait_ge(S(f"f{r}_y{par}"), k + 1)
                    place = bass.IndirectOffsetOnAxis(ap=t_x[j % XB][:, X_TOK:X_TOK + 1].bitcast(U32), axis=0)
                    g.indirect_dma_start(out=x_mid if r == 0 else T["out"].rearrange("b s d -> (b s) d"),
                                         out_offset=place, in_=t_y[par], in_offset=None, bounds_check=TOK - 1,
                                         oob_is_err=False).then_inc(S(f"f{r}_st{par}"), 16)

            scatter(0)
            send_tiles(0)
            g.wait_ge(S("m_stat0"), 1)
            for a in m_a:
                g.memset(a[:, :, 0:1], 0.0).then_inc(S("m_zero"), 1)
            g.memset(m_xt[:, :, 0:PAD], 0.0).then_inc(S("m_zero"), 1)

            def pairs(b):
                for p in range(NS // 2):
                    n = 2 * p
                    for st in (n, n + 1):
                        if st in POOL_C:
                            g.wait_ge(S("m_scan"), NS * b + st + 1)
                            g.wait_ge(S("m_cs"), NPC * b + pool_c(st) + 1)
                            g.tensor_tensor(m_b[st % 4], m_b[st % 4], m_c[pool_c(st) % 2].unsqueeze(1).to_broadcast([P, KI, SEQ]),
                                            ALU.mult).then_inc(S("m_cp"), 1)
                    g.wait_ge(S("m_c"), NVC * b + n + 2 - pool_c(n + 2))
                    g.wait_ge(S("m_cp"), NPC * b + pool_c(n + 2))
                    g.wait_ge(S("m_nsum"), (NS // 2) * b + p)
                    g.tensor_tensor(m_q, m_b[n % 4], m_b[(n + 1) % 4], ALU.add).then_inc(S("m_q"), 1)

            pairs(0)
            with g.Fori(1, BATCH) as b:
                pairs(b)
            scatter(1)
            send_tiles(1)

        @block.scalar
        def _(a):
            a.dma_start(wqkv[:, :, 0:D], T["Wq"].rearrange("(k p) n -> p k n", p=P)).then_inc(S("ld_a"), 16)
            a.dma_start(wqkv[:, :, D:2 * D], T["Wk"].rearrange("(k p) n -> p k n", p=P)).then_inc(S("ld_a"), 16)
            a.dma_start(wqkv[:, :, 2 * D:3 * D], T["Wv"].rearrange("(k p) n -> p k n", p=P)).then_inc(S("ld_a"), 16)
            a.dma_start(wo, T["Wo"].rearrange("(k p) n -> p k n", p=P)).then_inc(S("ld_a"), 16)
            a.dma_start(bkv, T["bkv"].partition_broadcast(P)).then_inc(S("ld_a"), 16)
            a.dma_start(bo, T["bo"].partition_broadcast(P)).then_inc(S("ld_a"), 16)
            a.dma_start(bq, T["bq"]).then_inc(S("ld_a"), 16)
            a.dma_start(wr[:, :, :], T["Wr"].rearrange("(k p) e -> p k e", p=P)).then_inc(S("ld_r"), 16)
            a.dma_start(br[:, :], T["br"].partition_broadcast(P)).then_inc(S("ld_r"), 16)
            a.dma_start(b1t[:, :, :], T["b1"]).then_inc(S("ld_r"), 16)
            a.wait_ge(S("ld_x1"), 16 * (BATCH - 1))
            for dst, name in ((zw, "zw"), (dtw, "dtw"), (bcw, "bcw"), (outw, "outw")):
                a.dma_start(dst[:, :, :], T[name].rearrange("(k p) n -> p k n", p=P)).then_inc(S("ld_m"), 16)
            a.dma_start(a_neg[:, :, :], T["A_log"]).then_inc(S("ld_m"), 16)
            a.dma_start(mvec[:, :, :], T["mvec"]).then_inc(S("ld_m"), 16)

            def xt_copy(b):
                a.wait_ge(S("a_tr"), b + 1)
                if not (isinstance(b, int) and b == 0):
                    a.wait_ge(S("a_kvp"), CPB * b)
                for k in range(KD):
                    last = a.activation(a_xt[:, k, :], ps[k][:, :], ACT.Copy)
                last.then_inc(S("a_xt"), 1)

            def attention(b, before, more):
                a.wait_ge(S("a_q"), b + 1)
                if not (isinstance(b, int) and b == 0):
                    a.wait_ge(S("a_qf"), b)
                for k in range(KD):
                    a.activation(a_eq[:, k, :], ps[2 + k][:, :], ACT.Exp, bias=bq[:, k:k + 1])
                    last = a.activation(a_rq[:, k, :], ps[2 + k][:, :], ACT.Relu, bias=bq[:, k:k + 1])
                last.then_inc(S("a_eq"), 1)
                if before:
                    o_copy(b - 1)
                a.wait_ge(S("a_kb"), CPB * b + CPB)
                if not (isinstance(b, int) and b == 0):
                    a.wait_ge(S("a_kf"), b)
                a.activation(a_ek, a_k, ACT.Exp).then_inc(S("a_ek"), 1)
                if more:
                    xt_copy(b + 1)

            def o_copy(b):
                a.wait_ge(S("a_otr"), b + 1)
                if not (isinstance(b, int) and b == 0):
                    a.wait_ge(S("a_ymm"), b)
                for k in range(KD):
                    last = a.activation(a_ot[:, k, :], ps[2 + k][:, :], ACT.Copy)
                last.then_inc(S("a_ot"), 1)

            a.wait_ge(S("ld_a"), 16 * 7)
            xt_copy(0)
            attention(0, False, True)
            with a.Fori(1, BATCH - 1) as b:
                attention(b, True, True)
            attention(BATCH - 1, True, False)
            o_copy(BATCH - 1)

            def feed(r):
                for b in range(BATCH):
                    a.wait_ge(S(f"f{r}_tr"), b + 1)
                    if b >= 2:
                        a.wait_ge(S(f"f{r}_lgmm"), b - 1)
                    for k in range(KD):
                        last = a.activation(f_xt[b % 2][:, k, :], ps[2 * (b % 2) + k][:, :], ACT.Copy)
                    last.then_inc(S(f"f{r}_xt"), 1)
                a.wait_ge(S(f"f{r}_lg"), 1)
                a.activation(r_ex, r_lg, ACT.Exp).then_inc(S(f"f{r}_ex"), 1)
                if r == 0:
                    for k in range(TAPS):
                        for d in range(KD):
                            n = KD * k + d
                            a.wait_ge(S("tap_mm"), n + 1)
                            a.activation(tapw[:, k, d, :], ps[n % 2][:, :], ACT.Copy).then_inc(S("tapw"), 1)
                    a.wait_ge(S("ld_m"), 16 * 6)
                    a.activation(a_neg[:, :, :], a_neg[:, :, :], ACT.Exp).then_inc(S("m_aexp"), 1)
                    a.wait_ge(S("m_aexp"), 1)
                    a.activation(a_neg[:, :, :], a_neg[:, :, :], ACT.Copy, scale=-1.0).then_inc(S("m_aexp"), 1)
                    a.activation(mvec[:, 1, :], mvec[:, 1, :], ACT.Copy, scale=0.5).then_inc(S("m_aexp"), 1)

                def xt(par, n):
                    a.wait_ge(S(f"f{r}_tr{par}"), n + 1)
                    a.wait_ge(S(f"f{r}_h{par}"), n)
                    a.activation(t_xt[par], ps[par][:, 0:KD * P].rearrange("p (k t) -> p k t", k=KD), ACT.Copy)\
                        .then_inc(S(f"f{r}_xt{par}"), 1)

                def relu(e, par, n):
                    a.wait_ge(S(f"f{r}_ht{par}"), n + 1)
                    a.wait_ge(S(f"f{r}_ymm{par}"), n)
                    for k in range(KH):
                        last = a.activation(t_ht[par][:, k, :], ps[4 + par][:, k * P:(k + 1) * P], ACT.Relu,
                                            bias=b1t[:, row(e), k:k + 1].rearrange("p a b -> p (a b)"))
                    last.then_inc(S(f"f{r}_relu{par}"), 1)

                def expert(j):
                    return a.value_load(tile_e[0:1, ds(j, 1)] if not isinstance(j, int) else tile_e[0:1, j:j + 1],
                                        min_val=0, max_val=E - 1)

                H = TILES // 2
                a.wait_ge(S(f"f{r}_pos"), 1)
                xt(0, 0)
                xt(1, 0)

                def turn(i, more):
                    relu(expert(2 * i), 0, i)
                    xt(0, i + 1)
                    relu(expert(2 * i + 1), 1, i)
                    if more:
                        xt(1, i + 1)

                turn(0, True)
                with a.Fori(1, H - 1) as i:
                    turn(i, True)
                turn(H - 1, False)
                relu(expert(TILES - 1), 0, H)

            feed(0)

            def m_xtcopy(n):
                a.wait_ge(S("m_tr"), n + 1)
                a.wait_ge(S("m_zmm"), KI * n)
                for k in range(KD):
                    last = a.activation(m_xt[:, k, PAD:], ps[k][:, :], ACT.Copy)
                last.then_inc(S("m_xt"), 1)

            def m_uevac(n, par, o):
                a.wait_ge(S("m_umm"), KI * n + o + 1)
                if not (isinstance(n, int) and n < 2):
                    a.wait_ge(S("m_y"), n - 1)
                a.activation(m_u[par][:, o, :], ps[U_BANK[o]][:, :], ACT.Identity, bias=mvec[:, 0, o:o + 1])\
                    .then_inc(S("m_u"), 1)

            def m_thevac(n, par, o):
                a.wait_ge(S("m_dmm"), KI * n + o + 1)
                a.activation(m_dt[par][:, o, :], ps[o % 2][:, :], ACT.Tanh, bias=mvec[:, 1, o:o + 1], scale=0.5)\
                    .then_inc(S("m_th"), 1)

            def m_bchi(n, par):
                a.wait_ge(S("m_bcmm"), n + 1)
                a.activation(m_bc[par][0:2 * NS, :], ps[0][0:2 * NS, :], ACT.Copy).then_inc(S("m_bchi"), 1)

            def m_zevac(n, par, o):
                a.wait_ge(S("m_zmm"), KI * n + o + 1)
                a.activation(m_sz[par][:, o, :], ps[Z_BANK[o]][:, :], ACT.Tanh, scale=0.5).then_inc(S("m_zth"), 1)

            def m_sigmoid(n, par):
                a.wait_ge(S("m_th"), KI * n + KI)
                a.activation(m_dt[par], m_dt[par], ACT.Copy, bias=0.5, scale=0.5).then_inc(S("m_dt0"), 1)

            def m_pre(n, par, st):
                if st == XT_AT:
                    m_xtcopy(n)
                if st in U_AT:
                    m_uevac(n, par, U_AT.index(st))
                if st in TH_AT:
                    m_thevac(n, par, TH_AT.index(st))
                    if st == TH_AT[-1]:
                        m_sigmoid(n, par)
                if st == BCHI_AT:
                    m_bchi(n, par)
                if st in ZTH_AT:
                    m_zevac(n, par, ZTH_AT.index(st))

            def m_scan(b, par, more):
                def decays(st):
                    n = NS * b + st
                    if not (isinstance(b, int) and n < 2):
                        a.wait_ge(S("m_scan"), n - 1)
                    for k in range(KI):
                        last = a.activation(m_a[st % 2][:, k, 1:], m_dt[par][:, k, 1:], ACT.Exp,
                                            scale=a_neg[:, k, st:st + 1])
                    last.then_inc(S("m_exp"), 1)

                a.wait_ge(S("m_dt1"), b + 1)
                for st in range(NS):
                    n = NS * b + st
                    if st % 2 == 0:
                        decays(st)
                        decays(st + 1)
                    a.wait_ge(S("m_db"), n + 1)
                    a.activation(m_b[st % 4], m_b[st % 4], ACT.Copy, bias=1e-6).then_inc(S("m_eps"), 1)
                    if st in POOL_C:
                        a.wait_ge(S("m_cb"), n + 1)
                        i = pool_c(st)
                        if not (isinstance(b, int) and NPC * b + i < 2):
                            a.wait_ge(S("m_cp"), NPC * b + i - 1)
                        a.activation(m_c[i % 2], ps[3][:, :], ACT.Copy).then_inc(S("m_cs"), 1)
                    if st == 0:
                        m_zevac(b, par, KI - 1)
                    if more:
                        m_pre(b + 1, 1 - par, st)

            a.wait_ge(S("m_zero"), 3)
            a.wait_ge(S("m_stat0"), 1)
            a.wait_ge(S("m_aexp"), 3)
            for st in range(NS):
                m_pre(0, 0, st)
            m_scan(0, 0, True)
            with a.Fori(0, (BATCH - 2) // 2) as i:
                m_scan(2 * i + 1, 1, True)
                m_scan(2 * i + 2, 0, True)
            m_scan(BATCH - 1, 1, False)
            feed(1)

        @block.vector
        def _(v):
            chain = S("v_chain")
            count = [0]

            def link(ins):
                count[0] += 1
                ins.then_inc(chain, 1)
                v.wait_ge(chain, count[0])

            def row_stats(c):
                return v.bn_stats(out=stats[:, row(c), :].rearrange("p a s -> p (a s)"),
                                  in_=x[:, row(c), :].rearrange("p a d -> p (a d)"))

            def layer_norm_scales(lo=0, hi=NCH):
                me, m2e, mo, m2o = [stats[:, lo:hi, i] for i in (1, 2, 4, 5)]
                d, q, var, t = [w[:, lo:hi] for w in nw]
                v.tensor_tensor(d, me, mo, ALU.subtract)
                v.tensor_tensor(q, me, mo, ALU.add)
                link(v.tensor_tensor(t, m2e, m2o, ALU.add))
                v.tensor_scalar(mean[:, lo:hi], q, 0.5, None, ALU.mult)
                link(v.tensor_scalar(var, t, 1.0 / D, LN_EPS, ALU.mult, ALU.add))
                link(v.tensor_tensor(q, d, d, ALU.mult))
                link(v.scalar_tensor_tensor(out=d, in0=q, scalar=0.25, in1=var, op0=ALU.mult, op1=ALU.add))
                y = rstd[:, lo:hi]
                link(v.tensor_scalar(y.bitcast(I32), d.bitcast(I32), -0.5, 1597463007.0, ALU.mult, ALU.add))
                for _ in range(4):
                    link(v.tensor_tensor(q, y, y, ALU.mult))
                    link(v.scalar_tensor_tensor(out=t, in0=q, scalar=-0.5, in1=d, op0=ALU.mult, op1=ALU.mult))
                    link(v.scalar_tensor_tensor(out=y, in0=t, scalar=1.5, in1=y, op0=ALU.add, op1=ALU.mult))

            def ln_apply(out, c):
                return v.tensor_scalar(out, x[:, row(c), :].rearrange("p a d -> p (a d)"), mean[:, row(c)],
                                       rstd[:, row(c)], ALU.subtract, ALU.mult)

            def first_stats(lo, hi):
                for c in range(lo, hi):
                    last = row_stats(c)
                link(last)
                layer_norm_scales(lo, hi)

            def a_norm(b):
                if not (isinstance(b, int) and b == 0):
                    v.wait_ge(S("a_tr"), b)
                for c in range(CPB):
                    last = ln_apply(a_xn[:, c, :], CPB * b + c)
                last.then_inc(S("a_xn"), 1)

            def a_kvbias(b):
                if not (isinstance(b, int) and b == 0):
                    v.wait_ge(S("a_kvmm"), b)
                for c in range(CPB):
                    v.wait_ge(S("a_kvp"), CPB * b + c + 1)
                    v.tensor_tensor(a_v[:, c, :, 0:P], ps[4 + c % 2][:, D:2 * D].rearrange("p (k n) -> p k n", k=KD),
                                    bkv[:, D:2 * D].rearrange("p (k n) -> p k n", k=KD), ALU.add)
                    v.tensor_tensor(a_k[:, c, :], ps[4 + c % 2][:, 0:D], bkv[:, 0:D], ALU.add).then_inc(S("a_kb"), 1)

            def a_kfeature(b):
                v.wait_ge(S("a_ek"), b + 1)
                v.tensor_scalar(a_ek, a_ek, 1.0, None, ALU.min).then_inc(S("a_ekmin"), 1)
                v.wait_ge(S("a_ekmin"), b + 1)
                v.scalar_tensor_tensor(out=a_k, in0=a_k, scalar=0.0, in1=a_ek, op0=ALU.max, op1=ALU.add)\
                    .then_inc(S("a_kf"), 1)

            def a_normalise(b):
                v.wait_ge(S("a_at"), b + 1)
                if not (isinstance(b, int) and b == 0):
                    v.wait_ge(S("a_otr"), b)
                for bank, u0, n in AT_BANKS:
                    g = ps[bank][:, 0:n * (P + HPT)].rearrange("p (u n) -> p u n", u=n)
                    last = v.tensor_scalar(a_nr[:, u0 * HPT:(u0 + n) * HPT].rearrange("p (u h) -> p u h", u=n),
                                           g[:, :, P:P + HPT], NORM_EPS, None, ALU.max)
                last.then_inc(S("a_nmax"), 1)
                v.wait_ge(S("a_nmax"), b + 1)
                v.reciprocal(a_nr, a_nr).then_inc(S("a_nrec"), 1)
                v.wait_ge(S("a_nrec"), b + 1)
                o = a_o.rearrange("p c (k h m) -> p (c k) h m", k=KD, h=HPT)
                for bank, u0, n in AT_BANKS:
                    g = ps[bank][:, 0:n * (P + HPT)].rearrange("p (u n) -> p u n", u=n)
                    last = v.tensor_tensor(o[:, u0:u0 + n], g[:, :, 0:P].rearrange("p u (h m) -> p u h m", h=HPT),
                                           a_nr[:, u0 * HPT:(u0 + n) * HPT].rearrange("p (u h) -> p u h", u=n)
                                           .unsqueeze(3).to_broadcast([P, n, HPT, HEAD]), ALU.mult)
                last.then_inc(S("a_o"), 1)

            def a_qfeature(b):
                v.wait_ge(S("a_eq"), b + 1)
                if not (isinstance(b, int) and b == 0):
                    v.wait_ge(S("a_at"), b)
                v.scalar_tensor_tensor(out=a_qf, in0=a_eq, scalar=1.0, in1=a_rq, op0=ALU.min, op1=ALU.add)\
                    .then_inc(S("a_qf"), 1)

            def a_mask(b):
                v.wait_ge(S("a_kvmm"), b + 1)
                for k in range(KD):
                    g = ps[4][:, k * (P + 1):(k + 1) * (P + 1)]
                    v.tensor_tensor(a_kv[:, k, 0:P], g[:, 0:P], blk, ALU.mult)
                    last = v.tensor_scalar(a_kv[:, k, P:P + HPT], heads, g[:, P:P + 1], None, ALU.mult)
                last.then_inc(S("a_mask"), 1)

            def a_update(b):
                v.wait_ge(S("a_ymm"), b + 1)
                v.wait_ge(S("a_bias"), b + 1)
                for h in range(2):
                    c = CPB * b + 2 * h
                    xv = x[:, ds(c, 2) if not isinstance(b, int) else slice(c, c + 2), :]
                    last = v.tensor_tensor(xv, ps[6 + h][:, :].rearrange("p (c d) -> p c d", c=2), xv, ALU.add)
                last.then_inc(S("a_xadd"), 1)
                v.wait_ge(S("a_xadd"), b + 1)
                for c in range(CPB):
                    last = row_stats(CPB * b + c)
                last.then_inc(S("a_xupd"), 1)

            def attention(b, before, more):
                if more:
                    a_norm(b + 1)
                if before:
                    a_normalise(b - 1)
                a_kvbias(b)
                a_qfeature(b)
                a_kfeature(b)
                if before:
                    a_update(b - 1)
                a_mask(b)

            v.wait_ge(S("ld_x0"), 16)
            first_stats(0, CPB)
            a_norm(0)
            v.wait_ge(S("ld_x1"), 16 * (BATCH - 1))
            first_stats(CPB, NCH)
            v.wait_ge(S("ld_a"), 16 * 7)
            v.wait_ge(S("ld_cst"), 16)
            v.wait_ge(S("a_vone"), 1)
            attention(0, False, True)
            with v.Fori(1, BATCH - 1) as b:
                attention(b, True, True)
            attention(BATCH - 1, True, False)
            a_normalise(BATCH - 1)
            a_update(BATCH - 1)
            v.wait_ge(S("xs_padded"), 32)

            def feed(r, updated, n_updated):
                v.wait_ge(S(updated), n_updated)
                layer_norm_scales()
                for b in range(BATCH):
                    if b >= 2:
                        v.wait_ge(S(f"f{r}_tr"), b - 1)
                    for c in range(CPB):
                        last = ln_apply(f_xn[b % 2][:, c, :], CPB * b + c)
                    last.then_inc(S(f"f{r}_xn"), 1)
                ce = "p (c e) -> p c e"
                lg, eq, ex, oh, pm, cmp_ = [q.rearrange(ce, e=E) for q in (r_lg, r_eq, r_ex, r_oh, r_pm, r_cmp)]
                ec = "p (e c) -> p e c"
                tot, cum = r_tot.rearrange(ec, e=E), r_cum.rearrange(ec, e=E)
                v.wait_ge(S("ld_r"), 16 * 3)
                v.wait_ge(S(f"f{r}_lgmm"), BATCH)
                v_log = ps[7][:, 0:NCH * E].rearrange(ce, e=E)
                link(v.tensor_tensor(lg, v_log, br[:, :].unsqueeze(1).to_broadcast([P, NCH, E]), ALU.add))
                link(v.tensor_reduce(r_mx, lg, AX.X, ALU.max))
                top = r_mx.unsqueeze(2).to_broadcast([P, NCH, E])
                link(v.tensor_tensor(eq, lg, top, ALU.is_equal))
                v.tensor_tensor(lg, lg, top, ALU.subtract).then_inc(S(f"f{r}_lg"), 1)
                link(v.tensor_tensor(eq, eq, cst[:, C_DESC:C_DESC + E].unsqueeze(1).to_broadcast([P, NCH, E]), ALU.mult))
                link(v.tensor_reduce(r_m2, eq, AX.X, ALU.max))
                v.tensor_tensor(oh, eq, r_m2.unsqueeze(2).to_broadcast([P, NCH, E]), ALU.is_equal)\
                    .then_inc(S(f"f{r}_oh"), 1)
                v.wait_ge(S(f"f{r}_ex"), 1)
                link(v.tensor_reduce(r_se, ex, AX.X, ALU.add))
                link(v.reciprocal(r_mx, r_se))
                link(v.tensor_copy(pmax, r_mx))
                v.wait_ge(S(f"f{r}_rank"), 1)
                link(v.tensor_copy(tot, ps[6][:, 0:NCH * E].rearrange("p (c e) -> p e c", e=E)))
                link(v.tensor_tensor_scan(out=r_cum, data0=cst[:, C_RST:C_RST + E * NCH], data1=r_tot, initial=0.0,
                                          op0=ALU.mult, op1=ALU.add))
                link(v.tensor_tensor(r_cmp.rearrange(ec, e=E), cum[:, :, NCH - 1:NCH].to_broadcast([P, E, NCH]),
                                     cst[:, C_THR:C_THR + NCH].unsqueeze(1).to_broadcast([P, E, NCH]), ALU.is_gt))
                link(v.tensor_reduce(r_tl, r_cmp.rearrange(ec, e=E), AX.X, ALU.add))
                link(v.tensor_tensor_scan(out=r_te, data0=ones[:, 0:E], data1=r_tl, initial=0.0,
                                          op0=ALU.mult, op1=ALU.add))
                v.tensor_tensor(r_ba, r_te, r_tl, ALU.subtract)
                link(v.tensor_tensor(cum, cum, tot, ALU.subtract))
                link(v.tensor_scalar(r_ba, r_ba, float(P), -1.0, ALU.mult, ALU.add))
                link(v.tensor_tensor(cum, cum, r_ba.unsqueeze(2).to_broadcast([P, E, NCH]), ALU.add))
                link(v.tensor_tensor(pm, ps[5][:, 0:NCH * E].rearrange(ce, e=E), r_cum.rearrange("p (e c) -> p c e", e=E),
                                     ALU.add))
                link(v.tensor_tensor(pm, pm, oh, ALU.mult))
                link(v.tensor_reduce(r_pf, pm, AX.X, ALU.add))
                v.tensor_copy(pos[:, :], r_pf)
                c2 = r_cmp2.rearrange("p (j e) -> p j e", e=E)
                link(v.tensor_tensor(c2, cst[:, C_IOTA:C_IOTA + 40].unsqueeze(2).to_broadcast([P, 40, E]),
                                     r_te.unsqueeze(1).to_broadcast([P, 40, E]), ALU.is_ge))
                link(v.tensor_reduce(r_te40, c2, AX.X, ALU.add))
                v.tensor_scalar(tile_e[:, :], r_te40, float(E - 1), None, ALU.min).then_inc(S(f"f{r}_pos"), 1)

                def hid(par, n):
                    v.wait_ge(S(f"f{r}_h{par}"), n + 1)
                    v.wait_ge(S(f"f{r}_ht{par}"), n)
                    v.tensor_copy(t_h[par], ps[2 + par][:, :]).then_inc(S(f"f{r}_hc{par}"), 1)

                def norm(k, n, kmod, par):
                    q = 2 * kmod + par
                    tx = t_x[q]
                    before = r * ((TILES - q + XB - 1) // XB)
                    v.wait_ge(S(f"f_x{q}"), 16 * (n + before + 1))
                    if not (isinstance(k, int) and k == 0):
                        v.wait_ge(S(f"f{r}_tr{par}"), k)
                    v.tensor_scalar(t_n[par], tx[:, 0:D], tx[:, X_MEAN:X_MEAN + 1], tx[:, X_RSTD:X_RSTD + 1],
                                    ALU.subtract, ALU.mult).then_inc(S(f"f{r}_n{par}"), 1)

                def bias(k, par):
                    j = 2 * k + par
                    e = v.value_load(tile_e[0:1, ds(j, 1)] if not isinstance(j, int) else tile_e[0:1, j:j + 1],
                                     min_val=0, max_val=E - 1)
                    v.wait_ge(S(f"f{r}_ymm{par}"), k + 1)
                    if not (isinstance(k, int) and k == 0):
                        v.wait_ge(S(f"f{r}_st{par}"), 16 * k)
                    v.tensor_tensor(t_y[par], ps[6 + par][:, 0:D], b2[:, row(e), :].rearrange("p a d -> p (a d)"), ALU.add)\
                        .then_inc(S(f"f{r}_yb{par}"), 1)

                def result(k, kmod, par):
                    tx = t_x[2 * kmod + par]
                    v.wait_ge(S(f"f{r}_yb{par}"), k + 1)
                    v.scalar_tensor_tensor(out=t_y[par], in0=t_y[par], scalar=tx[:, X_PMAX:X_PMAX + 1], in1=tx[:, 0:D],
                                           op0=ALU.mult, op1=ALU.add).then_inc(S(f"f{r}_y{par}"), 1)

                v.wait_ge(S(f"ld_ffn{r}"), LD_FFN)
                v.wait_ge(S(f"f{r}_pos"), 1)
                norm(0, 0, 0, 0)
                norm(0, 0, 0, 1)
                hid(0, 0)

                def turn(k, n, kmod):
                    norm(k + 1, n, (kmod + 1) % XT, 0)
                    hid(1, k)
                    bias(k, 0)
                    if not (isinstance(k, int) and k == TURNS - 1):
                        norm(k + 1, n, (kmod + 1) % XT, 1)
                    result(k, kmod, 0)
                    hid(0, k + 1)
                    bias(k, 1)
                    result(k, kmod, 1)

                for k in range(XT - 1):
                    turn(k, 0, k)
                whole = (TURNS - XT) // XT
                with v.Fori(1, whole + 1) as i:
                    for m in range(XT):
                        turn(XT * i - 1 + m, i, (XT - 1 + m) % XT)
                for k in range(XT * whole + XT - 1, TURNS):
                    turn(k, (k + 1) // XT, k % XT)
                bias(TURNS, 0)
                result(TURNS, TURNS % XT, 0)

            feed(0, "a_xupd", BATCH)

            v.wait_ge(S("ld_mid0"), 16)
            for c in range(CPB):
                last = row_stats(c)
            link(last)
            layer_norm_scales(0, CPB)
            v.tensor_copy(stack[:, :], cst[0:4 * NS, C_STK:C_STK + 2 * NS]).then_inc(S("m_stack"), 1)
            v.tensor_copy(nw[0][:, 0:1], ones[:, 0:1]).then_inc(S("m_stat0"), 1)
            def m_norm(n):
                if not (isinstance(n, int) and n == 0):
                    v.wait_ge(S("m_tr"), n)
                for c in range(CPB):
                    last = ln_apply(m_xn[:, c, :], CPB * n + c)
                last.then_inc(S("m_xn"), 1)

            m_norm(0)
            v.wait_ge(S("m_aexp"), 3)
            link(v.tensor_scalar(far[:, :], a_neg[:, :, :].rearrange("p k s -> p (k s)"), -5.0, None, ALU.is_lt))
            v.tensor_reduce(far_sum[:, :], far[:, :], AX.X, ALU.add).then_inc(S("m_far"), 1)
            v.wait_ge(S("m_farsum"), 1)
            link(v.tensor_copy(far_flag[:, :], ps[7][:, 0:1]))

            def m_dtw(n, par):
                v.wait_ge(S("m_dt0"), n + 1)
                v.tensor_scalar(m_dt[par], m_dt[par], 1e-4, 1.0, ALU.max, ALU.min).then_inc(S("m_dt1"), 1)
                v.wait_ge(S("m_dt1"), n + 1)
                v.tensor_tensor(m_w, m_dt[par], m_u[par], ALU.mult).then_inc(S("m_w"), 1)

            def m_bclo(n, par):
                v.wait_ge(S("m_bchi"), n + 1)
                v.tensor_tensor(m_bc[par][2 * NS:4 * NS, :], ps[0][0:2 * NS, :], m_bc[par][0:2 * NS, :].bitcast(F32),
                                ALU.subtract).then_inc(S("m_bclo"), 1)

            def m_gate(n, par, o):
                v.wait_ge(S("m_zth"), KI * n + o + 1)
                v.scalar_tensor_tensor(out=m_sz[par][:, o, :], in0=m_sz[par][:, o, :], scalar=1.0,
                                       in1=ps[Z_BANK[o]][:, :], op0=ALU.add, op1=ALU.mult).then_inc(S("m_sz"), 1)

            def m_final(b, par):
                v.wait_ge(S("m_nsum"), (NS // 2) * (b + 1))
                v.wait_ge(S("m_sz"), KI * (b + 1))
                for k in range(KI):
                    last = v.scalar_tensor_tensor(out=m_y[:, k, :], in0=m_u[par][:, k, :], scalar=mvec[:, 2, k:k + 1],
                                                  in1=ps[4 + k][:, :], op0=ALU.mult, op1=ALU.add)
                last.then_inc(S("m_y0"), 1)
                v.wait_ge(S("m_y0"), b + 1)
                v.scalar_tensor_tensor(out=m_y, in0=m_y, scalar=0.5, in1=m_sz[par], op0=ALU.mult, op1=ALU.mult)\
                    .then_inc(S("m_y"), 1)

            def m_update(b, h):
                v.wait_ge(S("m_omm"), 2 * b + h + 1)
                c = CPB * b + 2 * h
                xv = x[:, ds(c, 2) if not isinstance(c, int) else slice(c, c + 2), :]
                v.tensor_tensor(xv, ps[h][:, :].rearrange("p (c d) -> p c d", c=2), xv, ALU.add)\
                    .then_inc(S("m_xupd"), 1)
                if h == 0:
                    return
                v.wait_ge(S("m_xupd"), 2 * b + 2)
                for c in range(CPB):
                    last = row_stats(CPB * b + c)
                last.then_inc(S("m_stat"), 1)

            def m_db(b, par, st):
                n = NS * b + st
                v.wait_ge(S("m_bb"), n + 1)
                if st >= 4:
                    v.wait_ge(S("m_q"), (NS // 2) * b + (st - 4) // 2 + 1)
                elif not (isinstance(b, int) and b == 0):
                    v.wait_ge(S("m_q"), (NS // 2) * b - 2 + st // 2 + 1)
                v.tensor_tensor(m_b[st % 4], m_w, ps[2][:, :].unsqueeze(1).to_broadcast([P, KI, SEQ]), ALU.mult)\
                    .then_inc(S("m_db"), 1)

            def m_scan(b, par, before, more, clip):
                def scan(st):
                    n = NS * b + st
                    if clip:
                        v.wait_ge(S("m_clip"), n + 1)
                    v.wait_ge(S("m_exp"), n + 1)
                    v.wait_ge(S("m_eps"), n + 1)
                    bt = m_b[st % 4].rearrange("p k t -> p (k t)")
                    v.tensor_tensor_scan(out=bt, data0=m_a[st % 2].rearrange("p k t -> p (k t)"), data1=bt,
                                         initial=0.0, op0=ALU.mult, op1=ALU.add).then_inc(S("m_scan"), 1)

                def clipped(st):
                    v.wait_ge(S("m_exp"), NS * b + st + 1)
                    v.tensor_scalar(m_a[st % 2][:, :, 1:], m_a[st % 2][:, :, 1:], 0.006737946999085467,
                                    148.4131591025766, ALU.max, ALU.min).then_inc(S("m_clip"), 1)

                def c_product(st):
                    n = NS * b + st
                    v.wait_ge(S("m_scan"), n + 1)
                    v.wait_ge(S("m_cb"), n + 1)
                    v.tensor_tensor(m_b[st % 4], m_b[st % 4], ps[3][:, :].unsqueeze(1).to_broadcast([P, KI, SEQ]),
                                    ALU.mult).then_inc(S("m_c"), 1)

                def others(st):
                    if st == 0:
                        if more:
                            m_norm(b + 1)
                        m_gate(b, par, KI - 1)
                    if before and st == 2:
                        m_final(b - 1, 1 - par)
                    if before and st in (5, 6):
                        m_update(b - 1, st - 5)
                    if more and st == NS - 2:
                        m_dtw(b + 1, 1 - par)
                        m_bclo(b + 1, 1 - par)
                    if more and st in GATE_AT:
                        m_gate(b + 1, 1 - par, GATE_AT.index(st))

                for st in range(0, NS, 2):
                    if clip:
                        clipped(st)
                    m_db(b, par, st + 1)
                    scan(st)
                    others(st)
                    if clip:
                        clipped(st + 1)
                    scan(st + 1)
                    if st + 2 < NS:
                        m_db(b, par, st + 2)
                    elif more:
                        v.wait_ge(S("m_w"), b + 2)
                        m_db(b + 1, 1 - par, 0)
                    c_product(st + 1)
                    others(st + 1)

            def m_all(clip):
                m_scan(0, 0, False, True, clip)
                with v.Fori(0, (BATCH - 2) // 2) as i:
                    m_scan(2 * i + 1, 1, True, True, clip)
                    m_scan(2 * i + 2, 0, True, True, clip)
                m_scan(BATCH - 1, 1, True, False, clip)

            v.wait_ge(S("m_zero"), 3)
            v.wait_ge(S("ld_mid1"), 16 * (BATCH - 1))
            first_stats(CPB, NCH)
            m_gate(0, 0, 0)
            m_gate(0, 0, 1)
            m_dtw(0, 0)
            m_bclo(0, 0)
            m_gate(0, 0, 2)
            v.wait_ge(S("m_w"), 1)
            m_db(0, 0, 0)
            binds = v.value_load(far_flag[0:1, 0:1], min_val=0, max_val=P * KI * NS)
            with v.If(binds > 0):
                m_all(True)
            with v.Else():
                m_all(False)
            m_final(BATCH - 1, 1)
            m_update(BATCH - 1, 0)
            m_update(BATCH - 1, 1)
            feed(1, "m_stat", BATCH)

        @block.tensor
        def _(t):
            def turned(bank, src, k, n):
                return t.transpose(bank, src[:, k * P:(k + 1) * P], ident)

            def a_turn(b):
                t.wait_ge(S("a_xn"), b + 1)
                if not (isinstance(b, int) and b == 0):
                    t.wait_ge(S("a_xt"), b)
                for k in range(KD):
                    for c in range(CPB):
                        last = turned(ps[k][:, c * P:(c + 1) * P], a_xn[:, c, :], k, c)
                last.then_inc(S("a_tr"), 1)

            def a_query(b):
                t.wait_ge(S("a_xt"), b + 1)
                for m in range(KD):
                    for k in range(KD):
                        last = t.matmul(ps[2 + m][:, :], wqkv[:, k, m * P:(m + 1) * P], a_xt[:, k, :],
                                        start=(k == 0), stop=(k == KD - 1))
                last.then_inc(S("a_q"), 1)

            def a_keyvalue(b):
                for c in range(CPB):
                    if c >= 2:
                        t.wait_ge(S("a_kb"), CPB * b + c - 1)
                    for k in range(KD):
                        last = t.matmul(ps[4 + c % 2][:, :], a_xt[:, k, c * P:(c + 1) * P], wqkv[:, k, D:3 * D],
                                        start=(k == 0), stop=(k == KD - 1))
                    last.then_inc(S("a_kvp"), 1)

            def a_attend(b):
                t.wait_ge(S("a_qf"), b + 1)
                t.wait_ge(S("a_mask"), b + 1)
                if not (isinstance(b, int) and b == 0):
                    t.wait_ge(S("a_xadd"), b)
                for bank, u0, n in AT_BANKS:
                    for u in range(u0, u0 + n):
                        c, k = u // KD, u % KD
                        at = (u - u0) * (P + HPT)
                        last = t.matmul(ps[bank][:, at:at + P + HPT], a_qf[:, k, c * P:(c + 1) * P], a_kv[:, k, :],
                                        start=True, stop=True)
                last.then_inc(S("a_at"), 1)

            def a_kvmm(b):
                t.wait_ge(S("a_kf"), b + 1)
                for k in range(KD):
                    for c in range(CPB):
                        last = t.matmul(ps[4][:, k * (P + 1):(k + 1) * (P + 1)], a_k[:, c, k * P:(k + 1) * P],
                                        a_v[:, c, k, :], start=(c == 0), stop=(c == CPB - 1))
                last.then_inc(S("a_kvmm"), 1)

            def a_oturn(b, newest_q):
                t.wait_ge(S("a_o"), b + 1)
                t.wait_ge(S("a_eq"), newest_q + 1)
                for k in range(KD):
                    for c in range(CPB):
                        last = turned(ps[2 + k][:, c * P:(c + 1) * P], a_o[:, c, :], k, c)
                last.then_inc(S("a_otr"), 1)

            def a_out(b):
                t.wait_ge(S("a_ot"), b + 1)
                for c in range(CPB):
                    for k in range(KD):
                        last = t.matmul(ps[6 + c // 2][:, (c % 2) * D:(c % 2) * D + D], a_ot[:, k, c * P:(c + 1) * P],
                                        wo[:, k, :], start=(k == 0), stop=(k == KD - 1))
                last.then_inc(S("a_ymm"), 1)

            def attention(b, before, more):
                a_query(b)
                if before:
                    a_attend(b - 1)
                a_keyvalue(b)
                if before:
                    a_oturn(b - 1, b)
                    a_out(b - 1)
                if more:
                    a_turn(b + 1)
                a_kvmm(b)

            t.wait_ge(S("ld_cst"), 16)
            a_turn(0)
            t.wait_ge(S("ld_a"), 16 * 7)
            t.wait_ge(S("a_vone"), 1)
            attention(0, False, True)
            with t.Fori(1, BATCH - 1) as b:
                attention(b, True, True)
            attention(BATCH - 1, True, False)
            a_attend(BATCH - 1)
            a_oturn(BATCH - 1, BATCH - 1)
            a_out(BATCH - 1)

            def feed(r):
                t.wait_ge(S("ld_r"), 16 * 3)
                if r == 0:
                    t.wait_ge(S("a_xupd"), BATCH)
                else:
                    t.wait_ge(S("m_stat"), BATCH)
                for b in range(BATCH):
                    t.wait_ge(S(f"f{r}_xn"), b + 1)
                    if b >= 2:
                        t.wait_ge(S(f"f{r}_xt"), b - 1)
                    for k in range(KD):
                        for c in range(CPB):
                            last = turned(ps[2 * (b % 2) + k][:, c * P:(c + 1) * P], f_xn[b % 2][:, c, :], k, c)
                    last.then_inc(S(f"f{r}_tr"), 1)
                    if b:
                        logits(r, b - 1)
                logits(r, BATCH - 1)
                t.wait_ge(S(f"f{r}_oh"), 1)
                t.matmul(ps[5][:, 0:NCH * E], tri, r_oh, start=True, stop=True)
                t.matmul(ps[6][:, 0:NCH * E], ones, r_oh, start=True, stop=True).then_inc(S(f"f{r}_rank"), 1)
                if r == 0:
                    t.wait_ge(S("ld_ipw"), 16)
                    for k in range(TAPS):
                        t.wait_ge(S(f"ld_cw{k}"), 16)
                        for d in range(KD):
                            n = KD * k + d
                            if n >= 2:
                                t.wait_ge(S("tapw"), n - 1)
                            for c in range(KI):
                                last = t.matmul(ps[n % 2][:, :], ipw[:, c, d * P:(d + 1) * P], cw[:, c, :],
                                                start=(c == 0), stop=(c == KI - 1))
                            last.then_inc(S("tap_mm"), 1)
                    t.wait_ge(S("tapw"), TAPS * KD)

                def tr(par, n):
                    t.wait_ge(S(f"f{r}_n{par}"), n + 1)
                    if not (isinstance(n, int) and n == 0):
                        t.wait_ge(S(f"f{r}_xt{par}"), n)
                    for k in range(KD):
                        last = turned(ps[par][:, k * P:(k + 1) * P], t_n[par], k, 0)
                    last.then_inc(S(f"f{r}_tr{par}"), 1)

                def expert(j):
                    return t.value_load(tile_e[0:1, ds(j, 1)] if not isinstance(j, int) else tile_e[0:1, j:j + 1],
                                        min_val=0, max_val=E - 1)

                def first(j, par, n):
                    e = expert(j)
                    t.wait_ge(S(f"f{r}_xt{par}"), n + 1)
                    t.wait_ge(S(f"f{r}_hc{par}"), n)
                    for k in range(KD):
                        last = t.matmul(ps[2 + par][:, :], t_xt[par][:, k, :],
                                        w1[:, row(e), k, :].rearrange("p a h -> p (a h)"),
                                        start=(k == 0), stop=(k == KD - 1))
                    last.then_inc(S(f"f{r}_h{par}"), 1)

                def turn_hidden(par, n):
                    t.wait_ge(S(f"f{r}_hc{par}"), n + 1)
                    t.wait_ge(S(f"f{r}_relu{par}"), n)
                    for k in range(KH):
                        last = turned(ps[4 + par][:, k * P:(k + 1) * P], t_h[par], k, 0)
                    last.then_inc(S(f"f{r}_ht{par}"), 1)

                def second(j, par, n):
                    e = expert(j)
                    t.wait_ge(S(f"f{r}_relu{par}"), n + 1)
                    t.wait_ge(S(f"f{r}_y{par}"), n)
                    for k in range(KH):
                        last = t.matmul(ps[6 + par][:, 0:D], t_ht[par][:, k, :],
                                        w2[:, row(e), k, :].rearrange("p a h -> p (a h)"),
                                        start=(k == 0), stop=(k == KH - 1))
                    last.then_inc(S(f"f{r}_ymm{par}"), 1)

                H = TILES // 2
                t.wait_ge(S(f"ld_ffn{r}"), LD_FFN)
                t.wait_ge(S(f"f{r}_pos"), 1)
                tr(0, 0)
                tr(1, 0)
                first(0, 0, 0)

                def turn(i, more):
                    turn_hidden(0, i)
                    first(2 * i + 1, 1, i)
                    tr(0, i + 1)
                    second(2 * i, 0, i)
                    turn_hidden(1, i)
                    first(2 * i + 2, 0, i + 1)
                    if more:
                        tr(1, i + 1)
                    second(2 * i + 1, 1, i)

                turn(0, True)
                with t.Fori(1, H - 1) as i:
                    turn(i, True)
                turn(H - 1, False)
                turn_hidden(0, H)
                second(TILES - 1, 0, H)

            def logits(r, b):
                t.wait_ge(S(f"f{r}_xt"), b + 1)
                for c in range(CPB):
                    j = (CPB * b + c) * E
                    for k in range(KD):
                        last = t.matmul(ps[7][:, j:j + E], f_xt[b % 2][:, k, c * P:(c + 1) * P], wr[:, k, :],
                                        start=(k == 0), stop=(k == KD - 1))
                last.then_inc(S(f"f{r}_lgmm"), 1)

            feed(0)

            def m_turn(n):
                t.wait_ge(S("m_xn"), n + 1)
                t.wait_ge(S("m_sz"), KI * n)
                for k in range(KD):
                    for c in range(CPB):
                        last = turned(ps[k][:, c * P:(c + 1) * P], m_xn[:, c, :], k, c)
                last.then_inc(S("m_tr"), 1)

            def m_conv(n, o, h):
                if h == 0:
                    t.wait_ge(S("m_xt"), n + 1)
                    if o >= 2:
                        t.wait_ge(S("m_u"), KI * n + o)
                    if o == 2 and not (isinstance(n, int) and n < 2):
                        t.wait_ge(S("m_xupd"), 2 * (n - 2) + 1)
                for k in range(2 * h, 2 * h + 2):
                    for d in range(KD):
                        last = t.matmul(ps[U_BANK[o]][:, :], tapw[:, k, d, o * P:(o + 1) * P], m_xt[:, d, k:k + SEQ],
                                        start=(k == 0 and d == 0), stop=(k == TAPS - 1 and d == KD - 1))
                if h:
                    last.then_inc(S("m_umm"), 1)

            def m_dtmm(n, o):
                t.wait_ge(S("m_u"), KI * n + KI)
                if o == 1:
                    t.wait_ge(S("m_sz"), KI * n + 2)
                if o >= 2:
                    t.wait_ge(S("m_th"), KI * n + o - 1)
                for k in range(KI):
                    last = t.matmul(ps[o % 2][:, :], dtw[:, k, o * P:(o + 1) * P], m_u[m_par[0]][:, k, :],
                                    start=(k == 0), stop=(k == KI - 1))
                last.then_inc(S("m_dmm"), 1)

            def m_bcmm(n):
                t.wait_ge(S("m_th"), KI * n + 3)
                for k in range(KI):
                    last = t.matmul(ps[0][0:2 * NS, :], bcw[:, k, :], m_u[m_par[0]][:, k, :],
                                    start=(k == 0), stop=(k == KI - 1))
                last.then_inc(S("m_bcmm"), 1)

            def m_zmm(n, o):
                if o == 0:
                    t.wait_ge(S("m_u"), KI * n + 2)
                    if not (isinstance(n, int) and n < 2):
                        t.wait_ge(S("m_xupd"), 2 * (n - 2) + 2)
                if o == 1:
                    t.wait_ge(S("m_sz"), KI * n + 1)
                if o == 2:
                    t.wait_ge(S("m_th"), KI * n + KI)
                if o == 3:
                    t.wait_ge(S("m_bclo"), n + 1)
                for k in range(KD):
                    last = t.matmul(ps[Z_BANK[o]][:, :], zw[:, k, o * P:(o + 1) * P], m_xt[:, k, PAD:],
                                    start=(k == 0), stop=(k == KD - 1))
                last.then_inc(S("m_zmm"), 1)

            def m_out(b, h, more):
                t.wait_ge(S("m_y"), b + 1)
                if more:
                    t.wait_ge(S("m_u"), KI * (b + 2) + h + 1)
                elif b < BATCH - 1:
                    t.wait_ge(S("m_sz"), KI * BATCH)
                else:
                    t.wait_ge(S("m_xupd"), 2 * b)
                for c in (2 * h, 2 * h + 1):
                    for k in range(KI):
                        last = t.matmul(ps[h][:, (c % 2) * D:(c % 2) * D + D], m_y[:, k, c * P:(c + 1) * P],
                                        outw[:, k, :], start=(k == 0), stop=(k == KI - 1))
                last.then_inc(S("m_omm"), 1)

            def m_pre(n, q):
                if q == TURN_AT:
                    m_turn(n)
                if q in CONV_AT:
                    i = CONV_AT.index(q)
                    m_conv(n, i // 2, i % 2)
                if q in DT_AT:
                    m_dtmm(n, DT_AT.index(q))
                if q == BC_AT:
                    m_bcmm(n)
                if q in Z_AT:
                    m_zmm(n, Z_AT.index(q))

            m_par = [0]

            def spread_b(b, par, st):
                t.wait_ge(S("m_db"), NS * b + st)
                t.matmul(ps[2][:, :], stack[:, st:st + 1].to_broadcast([4 * NS, P]), m_bc[par][:, :],
                         start=True, stop=True).then_inc(S("m_bb"), 1)

            def spread_c(b, par, st):
                t.wait_ge(S("m_c"), NVC * b + st - pool_c(st))
                t.wait_ge(S("m_cs"), NPC * b + pool_c(st))
                t.matmul(ps[3][:, :], stack[:, NS + st:NS + st + 1].to_broadcast([4 * NS, P]), m_bc[par][:, :],
                         start=True, stop=True).then_inc(S("m_cb"), 1)

            def m_nsum(b, p):
                t.wait_ge(S("m_q"), (NS // 2) * b + p + 1)
                if p == 0:
                    t.wait_ge(S("m_y0"), b)
                for k in range(KI):
                    last = t.matmul(ps[4 + k][:, :], ident, m_q[:, k, :], start=(p == 0), stop=(p == NS // 2 - 1))
                last.then_inc(S("m_nsum"), 1)

            def m_scan(b, par, before, more):
                m_par[0] = 1 - par
                for q in range(2 * NS):
                    st = q // 4 * 2
                    if q % 4 == 0:
                        spread_c(b, par, st)
                    if q % 4 == 1:
                        if st + 2 < NS:
                            spread_b(b, par, st + 2)
                        spread_c(b, par, st + 1)
                        if q > 1:
                            m_nsum(b, q // 4 - 1)
                        elif before:
                            m_nsum(b - 1, NS // 2 - 1)
                    if q % 4 == 3 and st + 3 < NS:
                        spread_b(b, par, st + 3)
                    if more and q == 2 * NS - 2:
                        t.wait_ge(S("m_bclo"), b + 2)
                        spread_b(b + 1, 1 - par, 0)
                    if before and q in OUT_AT:
                        m_out(b - 1, OUT_AT.index(q), more)
                    if more:
                        m_pre(b + 1, q)
                    if more and q == 2 * NS - 1:
                        spread_b(b + 1, 1 - par, 1)

            t.wait_ge(S("m_far"), 1)
            t.matmul(ps[7][:, 0:1], ones, far_sum[:, :], start=True, stop=True).then_inc(S("m_farsum"), 1)
            t.wait_ge(S("m_stack"), 1)
            for q in range(2 * NS):
                m_pre(0, q)
            t.wait_ge(S("m_bclo"), 1)
            spread_b(0, 0, 0)
            spread_b(0, 0, 1)
            m_scan(0, 0, False, True)
            with t.Fori(0, (BATCH - 2) // 2) as i:
                m_scan(2 * i + 1, 1, True, True)
                m_scan(2 * i + 2, 0, True, True)
            m_scan(BATCH - 1, 1, True, False)
            m_nsum(BATCH - 1, NS // 2 - 1)
            m_out(BATCH - 1, 0, False)
            m_out(BATCH - 1, 1, False)
            feed(1)


def kernel(**inputs):
    import numpy as np
    import concourse.bacc as bacc
    from concourse import mybir as mb
    from concourse.bass_utils import run_bass_kernel_spmd as run

    def a(name):
        return np.asarray(inputs[name])

    def cols(v):
        return v.reshape(-1, P).T

    cst = np.zeros((P, C_ALL), np.float32)
    i = np.arange(P)
    cst[:, C_ID:C_ID + P] = i[:, None] == i
    cst[:, C_TRI:C_TRI + P] = i[:, None] <= i
    cst[:, C_ONE:C_ONE + P] = 1
    cst[:, C_BLK:C_BLK + P] = i[:, None] // HEAD == i // HEAD
    cst[:, C_RST:C_RST + E * NCH] = np.arange(E * NCH) % NCH != 0
    cst[:, C_THR:C_THR + NCH] = np.arange(NCH) * P
    cst[:, C_DESC:C_DESC + E] = E - np.arange(E)
    cst[:, C_IOTA:C_IOTA + 40] = np.arange(40)
    cst[:, C_TOK:C_TOK + NCH] = np.arange(NCH) * P + i[:, None]
    cst[:, C_STK:C_STK + 32] = i[:, None] % 32 == np.arange(32)
    B = "L0_attn_b_"
    arrays = {
        "cst": cst,
        "x": a("L0_attn_a_inputs_q"),
        "Wq": a("L0_attn_a_Wq"), "Wk": a("L0_attn_a_Wk"), "Wv": a("L0_attn_a_Wv"), "Wo": a("L0_attn_a_Wo"),
        "bq": cols(a("L0_attn_a_bq")),
        "bkv": np.concatenate([a("L0_attn_a_bk"), a("L0_attn_a_bv")]),
        "bo": a("L0_attn_a_bo"),
        "Wr": a("L0_ffn_Wr"), "br": a("L0_ffn_br"), "W1": a("L0_ffn_W1"), "W2": a("L0_ffn_W2"),
        "b1": a("L0_ffn_b1").reshape(E, KH, P).transpose(2, 0, 1),
        "b2": a("L0_ffn_b2"),
        "ip_x": a(B + "in_proj_w")[0:DI],
        "zw": a(B + "in_proj_w")[DI:2 * DI].T,
        "conv": a(B + "conv_w").transpose(2, 1, 0),
        "dtw": a(B + "dt_w").T,
        "bcw": np.concatenate([a(B + "B_w"), a(B + "C_w")]).T,
        "outw": a(B + "out_w").T,
        "A_log": a(B + "A_log").reshape(KI, P, NS).transpose(1, 0, 2),
        "mvec": np.stack([cols(a(B + "conv_b")), cols(a(B + "dt_b")), cols(a(B + "D"))], 1),
    }
    nc = bacc.Bacc("TRN2", target_bir_lowering=False, num_devices=1)
    T, feed = {}, {}
    for name, v in arrays.items():
        v = np.ascontiguousarray(v)
        feed[f"in_{name}"] = v
        T[name] = nc.dram_tensor(f"in_{name}", v.shape, mb.dt.from_np(v.dtype), kind="ExternalInput").ap()
    T["out"] = nc.dram_tensor("out_x", (BATCH, SEQ, D), mb.dt.float32, kind="ExternalOutput").ap()
    build(nc, T)
    r = run(nc, [feed], core_ids=[0])
    return r.results[0]["out_x"]
```
